# Optimizing a Trainium2 kernel written in Bass

```python
import numpy as np
import jax
import jax.numpy as jnp

def _softmax(x, axis=-1):
    return jax.nn.softmax(x, axis=axis)

def _gelu(x):
    return jax.nn.gelu(x, approximate=True)

def _silu(x):
    return jax.nn.silu(x)

def _sigmoid(x):
    return jax.nn.sigmoid(x)

def _layernorm(x, axis=-1, eps=1e-05):
    m = jnp.mean(x, axis=axis, keepdims=True)
    v = jnp.var(x, axis=axis, keepdims=True)
    return (x - m) / jnp.sqrt(v + eps)

def _scatter_add(tgt, idx, src, axis=0):
    return tgt.at[idx].add(src)

def _segment_sum(src, seg, n):
    return jax.ops.segment_sum(src, seg, n)
kernel_name = 'mk_adaln_d2_jaxref_r8_1bcbca'

def setup_inputs(seed: int=0):
    np.random.seed(seed)
    _w = jnp.asarray

    def _L0_attn_setup():
        import jax, jax.numpy as jnp
        import numpy as np
        NH, HS, K = (32, 256, 16)
        HD = HS // NH
        B, L = (4, 256)
        EPS = 1e-06

        def _ln(x, gamma, beta):
            mu = x.mean(-1, keepdims=True)
            var = x.var(-1, keepdims=True)
            return gamma * ((x - mu) / jnp.sqrt(var + EPS)) + beta

        def _ln_fused_l2_bwd(x, target, gamma, beta):
            D = x.shape[-1]
            mu = x.mean(-1, keepdims=True)
            std = jnp.sqrt(x.var(-1, keepdims=True) + EPS)
            xh = (x - mu) / std
            gxh = (gamma * xh + beta - target) * gamma
            return (D * gxh - gxh.sum(-1, keepdims=True) - xh * (gxh * xh).sum(-1, keepdims=True)) / (D * std)

        def _forward(hidden_states, q_w, k_w, v_w, o_w, W1, b1, ttt_norm_weight, ttt_norm_bias, ttt_lr_weight, ttt_lr_bias, learnable_token_idx, post_norm_weight, post_norm_bias):
            Bb, Ll, _ = hidden_states.shape
            NM = Ll // K

            def proj_heads(w):
                return (hidden_states @ w.T).reshape(Bb, Ll, NH, HD).transpose(0, 2, 1, 3)
            XQ = proj_heads(q_w).reshape(Bb, NH, NM, K, HD)
            XK = proj_heads(k_w).reshape(Bb, NH, NM, K, HD)
            XV = proj_heads(v_w).reshape(Bb, NH, NM, K, HD)
            X = hidden_states.reshape(Bb, NM, K, HS)
            ttt_lr = jnp.einsum('bnkc,hdc->bhnkd', X, ttt_lr_weight) + ttt_lr_bias.reshape(1, NH, 1, 1, 1)
            ttt_lr_eta = jax.nn.sigmoid(ttt_lr).transpose(0, 1, 2, 4, 3) / HD
            token_idx = jnp.clip(1.0 / jnp.arange(1, K + 1, dtype=jnp.float32) + learnable_token_idx, 0.0, None)
            eta = token_idx.reshape(1, 1, 1, K, 1) * ttt_lr_eta
            ln_w = ttt_norm_weight.reshape(NH, 1, HD)
            ln_b = ttt_norm_bias.reshape(NH, 1, HD)

            def step(carry, x):
                W1_s, b1_s = carry
                xq, xk, xv, eta_mb = x
                Z1 = xk @ W1_s + b1_s
                grad = _ln_fused_l2_bwd(Z1, xv - xk, ln_w, ln_b)
                Attn1 = jnp.tril(xq @ xk.swapaxes(-1, -2))
                b1_bar = b1_s - jnp.tril(eta_mb) @ grad
                Z1_bar = xq @ W1_s - eta_mb * Attn1 @ grad + b1_bar
                last_eta = eta_mb[:, :, -1, :, None]
                W1_new = W1_s - (last_eta * xk).swapaxes(-1, -2) @ grad
                b1_new = b1_s - jnp.sum(last_eta * grad, axis=-2, keepdims=True)
                out = xq + _ln(Z1_bar, ln_w, ln_b)
                return ((W1_new, b1_new), out)
            init = (jnp.tile(W1[None], (Bb, 1, 1, 1)), jnp.tile(b1[None], (Bb, 1, 1, 1)))
            xs = (XQ.transpose(2, 0, 1, 3, 4), XK.transpose(2, 0, 1, 3, 4), XV.transpose(2, 0, 1, 3, 4), eta.transpose(2, 0, 1, 3, 4))
            _, ys = jax.lax.scan(step, init, xs)
            out = ys.transpose(1, 0, 3, 2, 4).reshape(Bb, Ll, HS)
            out = _ln(out, post_norm_weight, post_norm_bias)
            return out @ o_w.T
        key = jax.random.key(seed)
        ks = jax.random.split(key, 8)
        s = 0.02
        return {'hidden_states': jax.random.normal(ks[0], (B, L, HS), jnp.float32), 'position_ids': jnp.tile(jnp.arange(L, dtype=jnp.int32)[None], (B, 1)), 'q_w': jax.random.normal(ks[1], (HS, HS), jnp.float32) * s, 'k_w': jax.random.normal(ks[2], (HS, HS), jnp.float32) * s, 'v_w': jax.random.normal(ks[3], (HS, HS), jnp.float32) * s, 'o_w': jax.random.normal(ks[4], (HS, HS), jnp.float32) * s, 'W1': jax.random.normal(ks[5], (NH, HD, HD), jnp.float32) * s, 'b1': jnp.zeros((NH, 1, HD), jnp.float32), 'ttt_norm_weight': jnp.ones((NH, HD), jnp.float32), 'ttt_norm_bias': jnp.zeros((NH, HD), jnp.float32), 'ttt_lr_weight': jax.random.normal(ks[6], (NH, 1, HS), jnp.float32) * s, 'ttt_lr_bias': jnp.zeros((NH, 1), jnp.float32), 'learnable_token_idx': jnp.zeros((K,), jnp.float32), 'post_norm_weight': jnp.ones((HS,), jnp.float32), 'post_norm_bias': jnp.zeros((HS,), jnp.float32)}
    _L0_attn_in = _L0_attn_setup()

    def _L0_ffn_setup():
        import jax, jax.numpy as jnp
        import numpy as np
        TOP_K = 8
        ROUTED_SCALING = 2.5
        key = jax.random.key(seed)
        ks = jax.random.split(key, 8)
        B, S, H, E, I = (2, 128, 256, 32, 128)
        IS = 2 * I
        w = lambda k, shape: jax.random.normal(k, shape, dtype=jnp.float32) * 0.02
        return {'hidden_states': jax.random.normal(ks[0], (B, S, H), dtype=jnp.float32), 'gate_weight': w(ks[1], (E, H)), 'w_gate': w(ks[2], (E, H, I)), 'w_up': w(ks[3], (E, H, I)), 'w_down': w(ks[4], (E, I, H)), 'ws_gate': w(ks[5], (H, IS)), 'ws_up': w(ks[6], (H, IS)), 'ws_down': w(ks[7], (IS, H))}
    _L0_ffn_in = _L0_ffn_setup()
    _L0_c = _w((lambda *s: np.random.randn(*s).astype(np.float32) * 0.05)(1, 256))
    _L0_wmod = _w((lambda *s: np.random.randn(*s).astype(np.float32) * 0.05)(256, 6 * 256) * 256 ** (-0.5))

    def _L1_attn_setup():
        import jax, jax.numpy as jnp
        import numpy as np
        B, S, HID = (1, 128, 256)
        H, DQK, DV = (16, 128, 128)
        K = 4
        SCALE = DQK ** (-0.5)

        def _dwconv_causal(x_btc, wk, bk, seq):
            y = jax.lax.conv_general_dilated(x_btc.transpose(0, 2, 1), wk, (1,), [(K - 1, K - 1)], dimension_numbers=('NCH', 'OIH', 'NCH'), feature_group_count=wk.shape[0])
            return (y[:, :, :seq] + bk[None, :, None]).transpose(0, 2, 1)

        def _kda_forward(x, Wq, Wk, Wv, Wa, ba, Wb, bb, Wg, Wo, qc_w, qc_b, kc_w, kc_b, vc_w, vc_b, ln_g, ln_b):
            Bb, Ss, _ = x.shape
            q = x @ Wq.T
            k = x @ Wk.T
            v = x @ Wv.T
            q = jax.nn.silu(_dwconv_causal(q, qc_w, qc_b, Ss))
            k = jax.nn.silu(_dwconv_causal(k, kc_w, kc_b, Ss))
            v = jax.nn.silu(_dwconv_causal(v, vc_w, vc_b, Ss))
            q = q.reshape(Bb, Ss, H, DQK)
            k = k.reshape(Bb, Ss, H, DQK) * SCALE
            v = v.reshape(Bb, Ss, H, DV)
            a = jax.nn.sigmoid(x @ Wa.T + ba).reshape(Bb, Ss, H, DV)
            beta = jax.nn.sigmoid(x @ Wb.T + bb)

            def step(St, inp):
                kt, qt, vt, at, bt = inp
                Sk = jnp.einsum('bhij,bhj->bhi', St, kt)
                err = Sk - vt
                Sn = at[..., None] * St - (bt[..., None] * err)[..., None] * kt[:, :, None, :]
                ot = jnp.einsum('bhij,bhj->bhi', Sn, qt)
                return (Sn, ot)
            tfirst = lambda u: u.transpose(1, 0, 2, 3)
            S0 = jnp.zeros((Bb, H, DV, DQK), x.dtype)
            _, outs = jax.lax.scan(step, S0, (tfirst(k), tfirst(q), tfirst(v), tfirst(a), beta.transpose(1, 0, 2)))
            out = outs.transpose(1, 0, 2, 3)
            mu = out.mean(-1, keepdims=True)
            var = out.var(-1, keepdims=True)
            o = (out - mu) * jax.lax.rsqrt(var + 1e-05) * ln_g + ln_b
            g = jax.nn.sigmoid(x @ Wg.T).reshape(Bb, Ss, H, DV)
            o = (o * g).reshape(Bb, Ss, H * DV)
            return o @ Wo.T
        key = jax.random.key(seed)
        ks = jax.random.split(key, 12)
        w = lambda i, shape, sc=0.02: jax.random.normal(ks[i], shape, jnp.float32) * sc
        return dict(x=jax.random.normal(ks[0], (B, S, HID), jnp.float32), Wq=w(1, (H * DQK, HID)), Wk=w(2, (H * DQK, HID)), Wv=w(3, (H * DV, HID)), Wa=w(4, (H * DV, HID)), ba=jnp.zeros((H * DV,), jnp.float32), Wb=w(5, (H, HID)), bb=jnp.zeros((H,), jnp.float32), Wg=w(6, (H * DV, HID)), Wo=w(7, (HID, H * DV)), qc_w=w(8, (H * DQK, 1, K), 0.2), qc_b=jnp.zeros((H * DQK,), jnp.float32), kc_w=w(9, (H * DQK, 1, K), 0.2), kc_b=jnp.zeros((H * DQK,), jnp.float32), vc_w=w(10, (H * DV, 1, K), 0.2), vc_b=jnp.zeros((H * DV,), jnp.float32), ln_g=jnp.ones((DV,), jnp.float32), ln_b=jnp.zeros((DV,), jnp.float32))
    _L1_attn_in = _L1_attn_setup()

    def _L1_ffn_setup():
        import jax, jax.numpy as jnp
        import numpy as np
        NUM_EXPERTS = 8
        TOP_K = 2
        IN_DIM = 256
        BOT_DIM = 64
        BATCH, SEQ = (4, 256)

        def _gelu(x):
            return jax.nn.gelu(x, approximate=False)
        key = jax.random.key(seed)
        ks = jax.random.split(key, 8)
        scale_d = 1.0 / np.sqrt(IN_DIM)
        scale_b = 1.0 / np.sqrt(BOT_DIM)
        return {'hidden_states': jax.random.normal(ks[0], (BATCH, SEQ, IN_DIM), jnp.float32), 'gate_w': jax.random.normal(ks[1], (NUM_EXPERTS, IN_DIM), jnp.float32) * scale_d, 'wd': jax.random.normal(ks[2], (NUM_EXPERTS, BOT_DIM, IN_DIM), jnp.float32) * scale_d, 'bd': jnp.zeros((NUM_EXPERTS, BOT_DIM), jnp.float32), 'wu': jax.random.normal(ks[3], (NUM_EXPERTS, IN_DIM, BOT_DIM), jnp.float32) * scale_b * 0.02, 'bu': jnp.zeros((NUM_EXPERTS, IN_DIM), jnp.float32), 'ws_d': jax.random.normal(ks[4], (BOT_DIM, IN_DIM), jnp.float32) * scale_d, 'bs_d': jnp.zeros((BOT_DIM,), jnp.float32), 'ws_u': jax.random.normal(ks[5], (IN_DIM, BOT_DIM), jnp.float32) * scale_b * 0.02, 'bs_u': jnp.zeros((IN_DIM,), jnp.float32)}
    _L1_ffn_in = _L1_ffn_setup()
    _L1_c = _w((lambda *s: np.random.randn(*s).astype(np.float32) * 0.05)(1, 256))
    _L1_wmod = _w((lambda *s: np.random.randn(*s).astype(np.float32) * 0.05)(256, 6 * 256) * 256 ** (-0.5))
    _d = {'L0_attn_hidden_states': _L0_attn_in['hidden_states'], 'L0_attn_position_ids': _L0_attn_in['position_ids'], 'L0_attn_q_w': _L0_attn_in['q_w'], 'L0_attn_k_w': _L0_attn_in['k_w'], 'L0_attn_v_w': _L0_attn_in['v_w'], 'L0_attn_o_w': _L0_attn_in['o_w'], 'L0_attn_W1': _L0_attn_in['W1'], 'L0_attn_b1': _L0_attn_in['b1'], 'L0_attn_ttt_norm_weight': _L0_attn_in['ttt_norm_weight'], 'L0_attn_ttt_norm_bias': _L0_attn_in['ttt_norm_bias'], 'L0_attn_ttt_lr_weight': _L0_attn_in['ttt_lr_weight'], 'L0_attn_ttt_lr_bias': _L0_attn_in['ttt_lr_bias'], 'L0_attn_learnable_token_idx': _L0_attn_in['learnable_token_idx'], 'L0_attn_post_norm_weight': _L0_attn_in['post_norm_weight'], 'L0_attn_post_norm_bias': _L0_attn_in['post_norm_bias'], 'L0_ffn_gate_weight': _L0_ffn_in['gate_weight'], 'L0_ffn_w_gate': _L0_ffn_in['w_gate'], 'L0_ffn_w_up': _L0_ffn_in['w_up'], 'L0_ffn_w_down': _L0_ffn_in['w_down'], 'L0_ffn_ws_gate': _L0_ffn_in['ws_gate'], 'L0_ffn_ws_up': _L0_ffn_in['ws_up'], 'L0_ffn_ws_down': _L0_ffn_in['ws_down'], 'L0_c': _L0_c, 'L0_wmod': _L0_wmod, 'L1_attn_Wq': _L1_attn_in['Wq'], 'L1_attn_Wk': _L1_attn_in['Wk'], 'L1_attn_Wv': _L1_attn_in['Wv'], 'L1_attn_Wa': _L1_attn_in['Wa'], 'L1_attn_ba': _L1_attn_in['ba'], 'L1_attn_Wb': _L1_attn_in['Wb'], 'L1_attn_bb': _L1_attn_in['bb'], 'L1_attn_Wg': _L1_attn_in['Wg'], 'L1_attn_Wo': _L1_attn_in['Wo'], 'L1_attn_qc_w': _L1_attn_in['qc_w'], 'L1_attn_qc_b': _L1_attn_in['qc_b'], 'L1_attn_kc_w': _L1_attn_in['kc_w'], 'L1_attn_kc_b': _L1_attn_in['kc_b'], 'L1_attn_vc_w': _L1_attn_in['vc_w'], 'L1_attn_vc_b': _L1_attn_in['vc_b'], 'L1_attn_ln_g': _L1_attn_in['ln_g'], 'L1_attn_ln_b': _L1_attn_in['ln_b'], 'L1_ffn_gate_w': _L1_ffn_in['gate_w'], 'L1_ffn_wd': _L1_ffn_in['wd'], 'L1_ffn_bd': _L1_ffn_in['bd'], 'L1_ffn_wu': _L1_ffn_in['wu'], 'L1_ffn_bu': _L1_ffn_in['bu'], 'L1_ffn_ws_d': _L1_ffn_in['ws_d'], 'L1_ffn_bs_d': _L1_ffn_in['bs_d'], 'L1_ffn_ws_u': _L1_ffn_in['ws_u'], 'L1_ffn_bs_u': _L1_ffn_in['bs_u'], 'L1_c': _L1_c, 'L1_wmod': _L1_wmod}
    _x0 = _d['L0_attn_hidden_states']
    _d['L0_attn_hidden_states'] = jax.random.normal(jax.random.fold_in(jax.random.key(seed), 1), (1, 2048, 256), dtype=_x0.dtype)
    del _x0
    return _d

def reference(L0_attn_hidden_states, L0_attn_position_ids, L0_attn_q_w, L0_attn_k_w, L0_attn_v_w, L0_attn_o_w, L0_attn_W1, L0_attn_b1, L0_attn_ttt_norm_weight, L0_attn_ttt_norm_bias, L0_attn_ttt_lr_weight, L0_attn_ttt_lr_bias, L0_attn_learnable_token_idx, L0_attn_post_norm_weight, L0_attn_post_norm_bias, L0_ffn_gate_weight, L0_ffn_w_gate, L0_ffn_w_up, L0_ffn_w_down, L0_ffn_ws_gate, L0_ffn_ws_up, L0_ffn_ws_down, L0_c, L0_wmod, L1_attn_Wq, L1_attn_Wk, L1_attn_Wv, L1_attn_Wa, L1_attn_ba, L1_attn_Wb, L1_attn_bb, L1_attn_Wg, L1_attn_Wo, L1_attn_qc_w, L1_attn_qc_b, L1_attn_kc_w, L1_attn_kc_b, L1_attn_vc_w, L1_attn_vc_b, L1_attn_ln_g, L1_attn_ln_b, L1_ffn_gate_w, L1_ffn_wd, L1_ffn_bd, L1_ffn_wu, L1_ffn_bu, L1_ffn_ws_d, L1_ffn_bs_d, L1_ffn_ws_u, L1_ffn_bs_u, L1_c, L1_wmod):

    def _L0_attn_ref(hidden_states, position_ids, q_w, k_w, v_w, o_w, W1, b1, ttt_norm_weight, ttt_norm_bias, ttt_lr_weight, ttt_lr_bias, learnable_token_idx, post_norm_weight, post_norm_bias):
        import jax, jax.numpy as jnp
        import numpy as np
        NH, HS, K = (32, 256, 16)
        HD = HS // NH
        B, L = (4, 256)
        EPS = 1e-06

        def _ln(x, gamma, beta):
            mu = x.mean(-1, keepdims=True)
            var = x.var(-1, keepdims=True)
            return gamma * ((x - mu) / jnp.sqrt(var + EPS)) + beta

        def _ln_fused_l2_bwd(x, target, gamma, beta):
            D = x.shape[-1]
            mu = x.mean(-1, keepdims=True)
            std = jnp.sqrt(x.var(-1, keepdims=True) + EPS)
            xh = (x - mu) / std
            gxh = (gamma * xh + beta - target) * gamma
            return (D * gxh - gxh.sum(-1, keepdims=True) - xh * (gxh * xh).sum(-1, keepdims=True)) / (D * std)

        def _forward(hidden_states, q_w, k_w, v_w, o_w, W1, b1, ttt_norm_weight, ttt_norm_bias, ttt_lr_weight, ttt_lr_bias, learnable_token_idx, post_norm_weight, post_norm_bias):
            Bb, Ll, _ = hidden_states.shape
            NM = Ll // K

            def proj_heads(w):
                return (hidden_states @ w.T).reshape(Bb, Ll, NH, HD).transpose(0, 2, 1, 3)
            XQ = proj_heads(q_w).reshape(Bb, NH, NM, K, HD)
            XK = proj_heads(k_w).reshape(Bb, NH, NM, K, HD)
            XV = proj_heads(v_w).reshape(Bb, NH, NM, K, HD)
            X = hidden_states.reshape(Bb, NM, K, HS)
            ttt_lr = jnp.einsum('bnkc,hdc->bhnkd', X, ttt_lr_weight) + ttt_lr_bias.reshape(1, NH, 1, 1, 1)
            ttt_lr_eta = jax.nn.sigmoid(ttt_lr).transpose(0, 1, 2, 4, 3) / HD
            token_idx = jnp.clip(1.0 / jnp.arange(1, K + 1, dtype=jnp.float32) + learnable_token_idx, 0.0, None)
            eta = token_idx.reshape(1, 1, 1, K, 1) * ttt_lr_eta
            ln_w = ttt_norm_weight.reshape(NH, 1, HD)
            ln_b = ttt_norm_bias.reshape(NH, 1, HD)

            def step(carry, x):
                W1_s, b1_s = carry
                xq, xk, xv, eta_mb = x
                Z1 = xk @ W1_s + b1_s
                grad = _ln_fused_l2_bwd(Z1, xv - xk, ln_w, ln_b)
                Attn1 = jnp.tril(xq @ xk.swapaxes(-1, -2))
                b1_bar = b1_s - jnp.tril(eta_mb) @ grad
                Z1_bar = xq @ W1_s - eta_mb * Attn1 @ grad + b1_bar
                last_eta = eta_mb[:, :, -1, :, None]
                W1_new = W1_s - (last_eta * xk).swapaxes(-1, -2) @ grad
                b1_new = b1_s - jnp.sum(last_eta * grad, axis=-2, keepdims=True)
                out = xq + _ln(Z1_bar, ln_w, ln_b)
                return ((W1_new, b1_new), out)
            init = (jnp.tile(W1[None], (Bb, 1, 1, 1)), jnp.tile(b1[None], (Bb, 1, 1, 1)))
            xs = (XQ.transpose(2, 0, 1, 3, 4), XK.transpose(2, 0, 1, 3, 4), XV.transpose(2, 0, 1, 3, 4), eta.transpose(2, 0, 1, 3, 4))
            _, ys = jax.lax.scan(step, init, xs)
            out = ys.transpose(1, 0, 3, 2, 4).reshape(Bb, Ll, HS)
            out = _ln(out, post_norm_weight, post_norm_bias)
            return out @ o_w.T
        del position_ids
        return _forward(hidden_states, q_w, k_w, v_w, o_w, W1, b1, ttt_norm_weight, ttt_norm_bias, ttt_lr_weight, ttt_lr_bias, learnable_token_idx, post_norm_weight, post_norm_bias)

    def _L0_ffn_ref(hidden_states, gate_weight, w_gate, w_up, w_down, ws_gate, ws_up, ws_down):
        import jax, jax.numpy as jnp
        import numpy as np
        TOP_K = 8
        ROUTED_SCALING = 2.5
        B, S, H = hidden_states.shape
        x = hidden_states.reshape(-1, H)
        T = x.shape[0]
        E = gate_weight.shape[0]
        scores = jax.nn.sigmoid(x @ gate_weight.T)
        topk_w, topk_i = jax.lax.top_k(scores, TOP_K)
        topk_w = topk_w / (jnp.sum(topk_w, axis=-1, keepdims=True) + 1e-20)
        topk_w = topk_w * ROUTED_SCALING
        dense_w = jnp.zeros((T, E), dtype=topk_w.dtype).at[jnp.arange(T)[:, None], topk_i].add(topk_w)
        g = jnp.einsum('th,ehi->eti', x, w_gate)
        u = jnp.einsum('th,ehi->eti', x, w_up)
        eo = jnp.einsum('eti,eih->eth', jax.nn.silu(g) * u, w_down)
        routed = jnp.einsum('eth,te->th', eo, dense_w)
        shared = jax.nn.silu(x @ ws_gate) * (x @ ws_up) @ ws_down
        return (routed + shared).reshape(B, S, H)

    def _L1_attn_ref(x, Wq, Wk, Wv, Wa, ba, Wb, bb, Wg, Wo, qc_w, qc_b, kc_w, kc_b, vc_w, vc_b, ln_g, ln_b):
        import jax, jax.numpy as jnp
        import numpy as np
        B, S, HID = (1, 128, 256)
        H, DQK, DV = (16, 128, 128)
        K = 4
        SCALE = DQK ** (-0.5)

        def _dwconv_causal(x_btc, wk, bk, seq):
            y = jax.lax.conv_general_dilated(x_btc.transpose(0, 2, 1), wk, (1,), [(K - 1, K - 1)], dimension_numbers=('NCH', 'OIH', 'NCH'), feature_group_count=wk.shape[0])
            return (y[:, :, :seq] + bk[None, :, None]).transpose(0, 2, 1)

        def _kda_forward(x, Wq, Wk, Wv, Wa, ba, Wb, bb, Wg, Wo, qc_w, qc_b, kc_w, kc_b, vc_w, vc_b, ln_g, ln_b):
            Bb, Ss, _ = x.shape
            q = x @ Wq.T
            k = x @ Wk.T
            v = x @ Wv.T
            q = jax.nn.silu(_dwconv_causal(q, qc_w, qc_b, Ss))
            k = jax.nn.silu(_dwconv_causal(k, kc_w, kc_b, Ss))
            v = jax.nn.silu(_dwconv_causal(v, vc_w, vc_b, Ss))
            q = q.reshape(Bb, Ss, H, DQK)
            k = k.reshape(Bb, Ss, H, DQK) * SCALE
            v = v.reshape(Bb, Ss, H, DV)
            a = jax.nn.sigmoid(x @ Wa.T + ba).reshape(Bb, Ss, H, DV)
            beta = jax.nn.sigmoid(x @ Wb.T + bb)

            def step(St, inp):
                kt, qt, vt, at, bt = inp
                Sk = jnp.einsum('bhij,bhj->bhi', St, kt)
                err = Sk - vt
                Sn = at[..., None] * St - (bt[..., None] * err)[..., None] * kt[:, :, None, :]
                ot = jnp.einsum('bhij,bhj->bhi', Sn, qt)
                return (Sn, ot)
            tfirst = lambda u: u.transpose(1, 0, 2, 3)
            S0 = jnp.zeros((Bb, H, DV, DQK), x.dtype)
            _, outs = jax.lax.scan(step, S0, (tfirst(k), tfirst(q), tfirst(v), tfirst(a), beta.transpose(1, 0, 2)))
            out = outs.transpose(1, 0, 2, 3)
            mu = out.mean(-1, keepdims=True)
            var = out.var(-1, keepdims=True)
            o = (out - mu) * jax.lax.rsqrt(var + 1e-05) * ln_g + ln_b
            g = jax.nn.sigmoid(x @ Wg.T).reshape(Bb, Ss, H, DV)
            o = (o * g).reshape(Bb, Ss, H * DV)
            return o @ Wo.T
        return _kda_forward(x, Wq, Wk, Wv, Wa, ba, Wb, bb, Wg, Wo, qc_w, qc_b, kc_w, kc_b, vc_w, vc_b, ln_g, ln_b)

    def _L1_ffn_ref(hidden_states, gate_w, wd, bd, wu, bu, ws_d, bs_d, ws_u, bs_u):
        import jax, jax.numpy as jnp
        import numpy as np
        NUM_EXPERTS = 8
        TOP_K = 2
        IN_DIM = 256
        BOT_DIM = 64
        BATCH, SEQ = (4, 256)

        def _gelu(x):
            return jax.nn.gelu(x, approximate=False)
        B, S, D = hidden_states.shape
        x = hidden_states.reshape(-1, D)
        T = x.shape[0]
        logits = x @ gate_w.T
        probs = jax.nn.softmax(logits.astype(jnp.float32), axis=-1)
        rw, sel = jax.lax.top_k(probs, TOP_K)
        rw = rw / rw.sum(axis=-1, keepdims=True)
        rw = rw.astype(x.dtype)
        combine = jnp.zeros((T, NUM_EXPERTS), x.dtype).at[jnp.arange(T)[:, None], sel].add(rw)
        down = jnp.einsum('td,ebd->teb', x, wd) + bd[None]
        h = _gelu(down) * combine[:, :, None]
        expert_out = jnp.einsum('teb,edb->td', h, wu) + combine @ bu
        shared = _gelu(x @ ws_d.T + bs_d) @ ws_u.T + bs_u
        out = (expert_out + shared).reshape(B, S, D)
        return out
    x = L0_attn_hidden_states
    mod = (_silu(L0_c) @ L0_wmod).reshape(L0_c.shape[0], 6, 1, -1)
    sa, ca, ga, sb, cb, gb = (mod[:, 0], mod[:, 1], mod[:, 2], mod[:, 3], mod[:, 4], mod[:, 5])
    ga = (2 * (ga >= 0) - 1) * jnp.maximum(jnp.abs(ga), 0.25)
    gb = (2 * (gb >= 0) - 1) * jnp.maximum(jnp.abs(gb), 0.25)
    h = _layernorm(x, axis=-1) * (1 + ca) + sa
    x = x + ga * _L0_attn_ref(h, L0_attn_position_ids, L0_attn_q_w, L0_attn_k_w, L0_attn_v_w, L0_attn_o_w, L0_attn_W1, L0_attn_b1, L0_attn_ttt_norm_weight, L0_attn_ttt_norm_bias, L0_attn_ttt_lr_weight, L0_attn_ttt_lr_bias, L0_attn_learnable_token_idx, L0_attn_post_norm_weight, L0_attn_post_norm_bias)
    h = _layernorm(x, axis=-1) * (1 + cb) + sb
    x = x + gb * _L0_ffn_ref(h, L0_ffn_gate_weight, L0_ffn_w_gate, L0_ffn_w_up, L0_ffn_w_down, L0_ffn_ws_gate, L0_ffn_ws_up, L0_ffn_ws_down)
    mod = (_silu(L1_c) @ L1_wmod).reshape(L1_c.shape[0], 6, 1, -1)
    sa, ca, ga, sb, cb, gb = (mod[:, 0], mod[:, 1], mod[:, 2], mod[:, 3], mod[:, 4], mod[:, 5])
    ga = (2 * (ga >= 0) - 1) * jnp.maximum(jnp.abs(ga), 0.25)
    gb = (2 * (gb >= 0) - 1) * jnp.maximum(jnp.abs(gb), 0.25)
    h = _layernorm(x, axis=-1) * (1 + ca) + sa
    x = x + ga * _L1_attn_ref(h, L1_attn_Wq, L1_attn_Wk, L1_attn_Wv, L1_attn_Wa, L1_attn_ba, L1_attn_Wb, L1_attn_bb, L1_attn_Wg, L1_attn_Wo, L1_attn_qc_w, L1_attn_qc_b, L1_attn_kc_w, L1_attn_kc_b, L1_attn_vc_w, L1_attn_vc_b, L1_attn_ln_g, L1_attn_ln_b)
    h = _layernorm(x, axis=-1) * (1 + cb) + sb
    x = x + gb * _L1_ffn_ref(h, L1_ffn_gate_w, L1_ffn_wd, L1_ffn_bd, L1_ffn_wu, L1_ffn_bu, L1_ffn_ws_d, L1_ffn_bs_d, L1_ffn_ws_u, L1_ffn_bs_u)
    return x

_drawn_inputs = setup_inputs


def setup_inputs(seed=0):
    import zlib

    import numpy as np

    out = dict(_drawn_inputs(seed))
    spreads = {'L0_attn_b1': (0.0, 0.1),
     'L0_attn_ttt_norm_weight': (1.0, 0.2),
     'L0_attn_ttt_norm_bias': (0.0, 0.1),
     'L0_attn_ttt_lr_bias': (0.0, 0.1),
     'L0_attn_learnable_token_idx': (0.0, 0.1),
     'L0_attn_post_norm_weight': (1.0, 0.2),
     'L0_attn_post_norm_bias': (0.0, 0.1),
     'L1_attn_ba': (0.0, 0.1),
     'L1_attn_bb': (0.0, 0.1),
     'L1_attn_qc_b': (0.0, 0.1),
     'L1_attn_kc_b': (0.0, 0.1),
     'L1_attn_vc_b': (0.0, 0.1),
     'L1_attn_ln_g': (1.0, 0.2),
     'L1_attn_ln_b': (0.0, 0.1),
     'L1_ffn_bd': (0.0, 0.1),
     'L1_ffn_bu': (0.0, 0.1),
     'L1_ffn_bs_d': (0.0, 0.1),
     'L1_ffn_bs_u': (0.0, 0.1)}
    factors = {}
    for name, (base, spread) in spreads.items():
        noise = np.random.default_rng([zlib.crc32(name.encode()), seed]).standard_normal(out[name].shape)
        drawn = base * np.exp(spread * noise) if base else spread * noise
        out[name] = jnp.asarray(drawn.astype(out[name].dtype))
    for name, factor in factors.items():
        out[name] = (out[name] * factor).astype(out[name].dtype)
    return out
```

```python
from contextlib import ExitStack

import numpy as np

import concourse.bass as bass
from concourse import mybir

F32 = mybir.dt.float32
ALU = mybir.AluOpType
ACT = mybir.ActivationFunctionType
AX_X = mybir.AxisListType.X

P = 128
T = 2048
D = 256
KD = D // P
NT = T // P
MB = 16
NMB = T // MB
TH, HD = 32, 8
HG, HR = 8, 4
EPS = 1e-5
TTT_EPS = 1e-6


class Chain:

    def __init__(self, eng, sem, base=0):
        self.eng, self.sem, self.base, self.n = eng, sem, base, 0

    def mark(self, ins):
        self.n += 1
        ins.then_inc(self.sem, 1)
        return self.n

    def wait(self, n):
        self.eng.wait_ge(self.sem, self.base + n)

    def done(self, ins):
        self.wait(self.mark(ins))

    def done_before(self, ins, pad):
        self.done(ins)
        self.eng.tensor_copy(pad[:, 1:2], pad[:, 0:1])


class Alloc:

    def __init__(self, nc, ctx, phase):
        self.nc, self.ctx, self.phase, self.sems = nc, ctx, phase, []
        ctx.callback(self.release)

    def release(self):
        if self.sems:
            self.nc.clear_and_free_semaphores(self.sems)
            self.nc.all_engine_barrier()

    def sb(self, name, shape):
        return self.ctx.enter_context(self.nc.sbuf_tensor(f"{self.phase}_{name}", shape, F32))

    def ps(self, name, shape):
        return self.ctx.enter_context(self.nc.psum_tensor(f"{self.phase}_{name}", shape, F32))

    def sem(self, name):
        self.sems.append(self.nc.alloc_semaphore(name=f"{self.phase}_{name}"))
        return self.sems[-1]


def bcast(ap, axis, n):
    shape = list(ap.shape)
    return ap.unsqueeze(axis).broadcast_to(shape[:axis] + [n] + shape[axis:])


def setup_phase(nc, I, C):
    with ExitStack() as ctx:
        A = Alloc(nc, ctx, "setup")
        wmod = A.sb("wmod", [P, 2, KD, 6 * D])
        cond = A.sb("cond", [P, 2, KD])
        sig = A.sb("sig", [P, 2, KD])
        sc = A.sb("sc", [P, 2, KD])
        scb = A.sb("scb", [P, 2, KD, P])
        sgn = A.sb("sgn", [P, 4, D])
        ones = A.sb("ones", [P, P])
        ps_col = A.ps("ps_col", [P, 512])
        ps_row = [A.ps(f"ps_row{i}", [P, 512]) for i in range(2)]
        loaded = A.sem("loaded")
        sig_ready = A.sem("sig_ready")
        silu_ready = A.sem("silu_ready")
        col_ready = A.sem("col_ready")
        row_ready = A.sem("row_ready")
        dve_step = A.sem("dve_step")
        block = ctx.enter_context(nc.Block())

        @block.sync
        def _(sp):
            for l in range(2):
                sp.dma_start(wmod[:, l], I[f"wmod{l}"].rearrange("(k p) n -> p k n", p=P)).then_inc(loaded, 16)
                sp.dma_start(cond[:, l], I[f"c{l}"]).then_inc(loaded, 16)
            sp.dma_start(C["ident"][:, :], I["c_ident"]).then_inc(loaded, 16)
            sp.wait_ge(loaded, 80)

        @block.scalar
        def _(act):
            act.wait_ge(loaded, 80)
            nc.scalar.activation(sig[:, :, :], cond[:, :, :], ACT.Sigmoid).then_inc(sig_ready, 1)

        @block.vector
        def _(dve):
            ch = Chain(dve, dve_step)
            nc.vector.memset(C["nhalf"][:, :], -0.5)
            nc.vector.memset(C["pad"][:, :], 0.0)
            ch.done(nc.vector.memset(ones[:, :], 1.0))
            dve.wait_ge(sig_ready, 1)
            ch.done(nc.vector.tensor_tensor(sc[:, :, :], cond[:, :, :], sig[:, :, :], ALU.mult))
            for l in range(2):
                for k in range(KD):
                    ins = nc.vector.tensor_scalar(scb[:, l, k, :], ones[:, :], sc[:, l, k:k + 1], None, ALU.mult)
            ins.then_inc(silu_ready, 1)
            dve.wait_ge(col_ready, 1)
            ch.done(nc.vector.tensor_copy(C["mod_col"][:, :, :, :], ps_col[:, 0:16].rearrange(
                "p (l m k) -> p l m k", l=2, m=4)))
            for m in (1, 3):
                last = nc.vector.tensor_scalar(C["mod_col"][:, :, m, :], C["mod_col"][:, :, m, :], 1.0, None, ALU.add)
            for l in range(2):
                dve.wait_ge(row_ready, l + 1)
                g = ps_row[l][:, :].rearrange("p (m n) -> p m n", m=2)
                s = sgn[:, 2 * l:2 * l + 2, :]
                out = C["gate_row"][:, l, :, :]
                ch.done(nc.vector.tensor_scalar(s, g, 0.0, 2.0, ALU.is_ge, ALU.mult))
                ch.done(nc.vector.tensor_scalar(s, s, -1.0, None, ALU.add))
                ch.done(nc.vector.tensor_tensor(out, g, s, ALU.mult))
                ch.done(nc.vector.scalar_tensor_tensor(out=out, in0=out, scalar=0.25, in1=s,
                                                       op0=ALU.max, op1=ALU.mult))

        @block.tensor
        def _(pe):
            pe.wait_ge(loaded, 80)
            pe.wait_ge(silu_ready, 1)
            for l in range(2):
                for m, at in enumerate((0, 1, 3, 4)):
                    for a in range(KD):
                        n = (l * 4 + m) * KD + a
                        for k in range(KD):
                            ins = nc.tensor.matmul(ps_col[:, n:n + 1], wmod[:, l, k, at * D + a * P:at * D + a * P + P],
                                                   sc[:, l, k:k + 1], start=(k == 0), stop=(k == KD - 1))
            ins.then_inc(col_ready, 1)
            for l in range(2):
                for m, at in enumerate((2, 5)):
                    for k in range(KD):
                        ins = nc.tensor.matmul(ps_row[l][:, m * D:(m + 1) * D], scb[:, l, k, :],
                                               wmod[:, l, k, at * D:(at + 1) * D], start=(k == 0), stop=(k == KD - 1))
                ins.then_inc(row_ready, 1)


def ttt_project_phase(nc, I, C, S):
    with ExitStack() as ctx:
        A = Alloc(nc, ctx, "proj")
        x_t = A.sb("x_t", [P, D])
        stats = A.sb("stats", [P, 6])
        mv = A.sb("mv", [P, 2])
        rstd = A.sb("rstd", [P, 1])
        xh = A.sb("xh", [P, D])
        hT = A.sb("hT", [P, KD, P])
        wq = A.sb("wq", [P, KD, D])
        wk = A.sb("wk", [P, KD, D])
        wv = A.sb("wv", [P, KD, D])
        wlr = A.sb("wlr", [P, KD, TH])
        lr_b = A.sb("lr_b", [P, TH])
        gam = A.sb("gam", [P, D])
        bet = A.sb("bet", [P, D])
        c_t = A.sb("c_t", [P, D + TH])
        c_m = A.sb("c_m", [P, TH])
        ps_T = A.ps("ps_T", [P, KD, P])
        ps_f = A.ps("ps_f", [P, 2, KD, P])
        ps_c = A.ps("ps_c", [P, D])
        ps_l = A.ps("ps_l", [P, TH])
        loaded = A.sem("loaded")
        x_ready = A.sem("x_ready")
        mv_ready = A.sem("mv_ready")
        rstd_ready = A.sem("rstd_ready")
        xh_ready = A.sem("xh_ready")
        T_ready = A.sem("T_ready")
        hT_ready = A.sem("hT_ready")
        f_ready = A.sem("f_ready")
        c_ready = A.sem("c_ready")
        f_copied = A.sem("f_copied")
        c_done = A.sem("c_done")
        lr_done = A.sem("lr_done")
        c_stored = A.sem("c_stored")
        c_back = A.sem("c_back")
        dve_step = A.sem("dve_step")
        block = ctx.enter_context(nc.Block())
        DVE_PER = 5

        @block.sync
        def _(sp):
            for w, n in ((wq, "qwT"), (wk, "kwT"), (wv, "vwT"), (wlr, "lrwT")):
                sp.dma_start(w[:, :, :], I[n].rearrange("(k p) n -> p k n", p=P)).then_inc(loaded, 16)
            for r, n in ((lr_b, "lrb"), (gam, "ttt_w"), (bet, "ttt_b")):
                sp.dma_start(r[:, :], I[n].broadcast_to([P, I[n].shape[1]])).then_inc(loaded, 16)
            with sp.Fori(0, NT) as t:
                sp.wait_ge(xh_ready, t)
                sp.dma_start(x_t[:, :], I["x"][bass.ds(t * P, P), :]).then_inc(x_ready, 16)
                sp.wait_ge(c_done, t + 1)
                sp.wait_ge(lr_done, t + 1)
                sp.dma_start(S["c_tok"][bass.ds(t * P, P), :], c_t[:, :]).then_inc(c_stored, 16)
            sp.wait_ge(c_stored, NT * 16)
            for g in range(HG):
                src = S["c_tok"].rearrange("(m t) n -> t m n", t=MB)
                sp.dma_start(S["cA"][g * MB:(g + 1) * MB, :, :], src[:, :, g * 32:(g + 1) * 32]).then_inc(c_back, 16)
                sp.dma_start(S["lA"][g * MB:(g + 1) * MB, :, :],
                             src[:, :, D + g * HR:D + (g + 1) * HR]).then_inc(c_back, 16)
            sp.wait_ge(c_back, 16 * 2 * HG)

        @block.vector
        def _(dve):
            dve.wait_ge(loaded, 16 * 7)
            nc.vector.tensor_tensor(wv[:, :, :], wk[:, :, :], wv[:, :, :], ALU.subtract).then_inc(dve_step, 1)
            with dve.Fori(0, NT) as t:
                ch = Chain(dve, dve_step, 1 + t * DVE_PER)
                dve.wait_ge(x_ready, (t + 1) * 16)
                ch.done_before(nc.vector.bn_stats(stats[:, :], x_t[:, :]), C["pad"])
                ch.done(nc.vector.bn_aggr(mv[:, :], stats[:, :]))
                nc.vector.tensor_scalar(mv[:, 1:2], mv[:, 1:2], EPS, None, ALU.add).then_inc(mv_ready, 1)
                dve.wait_ge(rstd_ready, t + 1)
                nc.vector.tensor_scalar(xh[:, :], x_t[:, :], mv[:, 0:1], rstd[:, 0:1], ALU.subtract,
                                        ALU.mult).then_inc(xh_ready, 1)
                dve.wait_ge(f_ready, t + 1)
                nc.vector.tensor_copy(S["XKT"][:, :, bass.ds(t * P, P)], ps_f[:, 0, :, :])
                nc.vector.tensor_copy(S["XQT"][:, :, bass.ds(t * P, P)], ps_f[:, 1, :, :]).then_inc(f_copied, 1)
                dve.wait_ge(c_ready, t + 1)
                dve.wait_ge(c_stored, t * 16)
                c3 = c_t[:, 0:D]
                ch.done(nc.vector.tensor_tensor(c3, ps_c[:, :], bet[:, :], ALU.add))
                ch.done(nc.vector.tensor_tensor(c3, c3, gam[:, :], ALU.mult))
                c3 = c3.rearrange("p (h e) -> p h e", e=HD)
                ch.done(nc.vector.tensor_reduce(c_m[:, :], c3, AX_X, ALU.add))
                nc.vector.scalar_tensor_tensor(out=c3, in0=bcast(c_m[:, :], 2, HD), scalar=-1.0 / HD, in1=c3,
                                               op0=ALU.mult, op1=ALU.add).then_inc(c_done, 1)
            assert ch.n == DVE_PER, ch.n

        @block.gpsimd
        def _(pool):
            with pool.Fori(0, NT) as t:
                pool.wait_ge(mv_ready, t + 1)
                nc.gpsimd.tensor_tensor(rstd[:, :], mv[:, 1:2], C["nhalf"][:, 0:1], ALU.pow).then_inc(rstd_ready, 1)

        @block.scalar
        def _(act):
            act.wait_ge(loaded, 16 * 7)
            lr_step = A.sem("lr_step")
            with act.Fori(0, NT) as t:
                act.wait_ge(T_ready, t + 1)
                for k in range(KD):
                    ins = nc.scalar.activation(hT[:, k, :], ps_T[:, k, :], ACT.Identity,
                                               bias=C["mod_col"][:, 0, 0, k:k + 1], scale=C["mod_col"][:, 0, 1, k:k + 1])
                ins.then_inc(hT_ready, 1)
                act.wait_ge(c_ready, t + 1)
                act.wait_ge(c_stored, t * 16)
                nc.scalar.activation(c_t[:, D:], ps_l[:, :], ACT.Sigmoid).then_inc(lr_step, 1)
                act.wait_ge(lr_step, t + 1)
                nc.scalar.mul(c_t[:, D:], c_t[:, D:], float(HD) ** 0.5 / HD).then_inc(lr_done, 1)

        @block.tensor
        def _(pe):
            pe.wait_ge(loaded, 16 * 7)
            pe.wait_ge(dve_step, 1)
            with pe.Fori(0, NT) as t:
                pe.wait_ge(xh_ready, t + 1)
                for k in range(KD):
                    ins = nc.tensor.matmul(ps_T[:, k, :], xh[:, k * P:(k + 1) * P], C["ident"][:, :], start=True, stop=True)
                ins.then_inc(T_ready, 1)
                pe.wait_ge(hT_ready, t + 1)
                pe.wait_ge(f_copied, t)
                for n, w in enumerate((wk, wq)):
                    for a in range(KD):
                        for k in range(KD):
                            ins = nc.tensor.matmul(ps_f[:, n, a, :], w[:, k, a * P:(a + 1) * P], hT[:, k, :],
                                                   start=(k == 0), stop=(k == KD - 1))
                ins.then_inc(f_ready, 1)
                pe.wait_ge(c_done, t)
                pe.wait_ge(lr_done, t)
                for k in range(KD):
                    nc.tensor.matmul(ps_c[:, :], hT[:, k, :], wv[:, k, :], start=(k == 0), stop=(k == KD - 1))
                for k in range(KD):
                    nc.tensor.matmul(ps_l[:, :], hT[:, k, :], wlr[:, k, :], start=(k == 0), stop=False)
                nc.tensor.matmul(ps_l[:, :], C["ident"][:, :], lr_b[:, :], start=False, stop=True).then_inc(c_ready, 1)


def ttt_scan_phase(nc, I, C, S):
    with ExitStack() as ctx:
        A = Alloc(nc, ctx, "scan")
        W = A.sb("W", [P, KD + 1, 32])
        w_m = A.sb("w_m", [P, (KD + 1) * HR])
        gmask = A.sb("gmask", [P, HR])
        rmask = A.sb("rmask", [P, KD + 1, HR])
        tok = A.sb("tok", [P, MB])
        idx = A.sb("idx", [P, MB])
        ntok = A.sb("ntok", [P, 1])
        first = A.sb("first", [P, P])
        same = A.sb("same", [P, P])
        gam2 = A.sb("gam2", [P, 32])
        xk1 = [A.sb(f"xk1_{b}", [P, KD, HR, MB]) for b in range(2)]
        xk2 = [A.sb(f"xk2_{b}", [P, P]) for b in range(2)]
        zc = A.sb("zc", [P, 32])
        sq = A.sb("sq", [P, HR, HD + 1])
        vs = A.sb("vs", [P, HR])
        rs = A.sb("rs", [P, HR])
        rl = A.sb("rl", [P, HR])
        xn = A.sb("xn", [P, 32])
        g = A.sb("g", [P, 32])
        sg = A.sb("sg", [P, HR])
        u = A.sb("u", [P, 32])
        v = A.sb("v", [P, 32])
        grad = A.sb("grad", [P, 32])
        psZ = A.ps("psZ", [P, 512])
        psW = A.ps("psW", [P, KD + 1, 512])
        psX = [A.ps(f"psX{b}", [P, 512]) for b in range(2)]
        loaded = A.sem("loaded")
        consts = A.sem("consts")
        pool_step = A.sem("pool_step")
        xk1_ready = A.sem("xk1_ready")
        xk1T_ready = A.sem("xk1T_ready")
        xk2_ready = A.sem("xk2_ready")
        z_ready = A.sem("z_ready")
        sq_ready = A.sem("sq_ready")
        vs_ready = A.sem("vs_ready")
        rs_ready = A.sem("rs_ready")
        rl_ready = A.sem("rl_ready")
        zc_ready = A.sem("zc_ready")
        g_ready = A.sem("g_ready")
        g_kept = A.sem("g_kept")
        dw_ready = A.sem("dw_ready")
        w_ready = A.sem("w_ready")
        dve_step = A.sem("dve_step")
        block = ctx.enter_context(nc.Block())
        TILE_MB = P // MB
        INIT = 6
        PER = 9

        def heads(ap):
            return ap.rearrange("p (r e) -> p r e", e=HD)

        def heads3(ap):
            return ap[:, :, :].rearrange("p a (r e) -> p (a r) e", e=HD)

        @block.sync
        def _(sp):
            for dst, n in ((W[:, 0:KD, :], "W1bd"), (W[:, KD, :], "b1A"), (gmask[:, :], "c_gmask"), (rmask[:, :, :], "c_rmask"),
                           (first[:, :], "c_first"), (same[:, :], "c_same"), (gam2[:, :], "ttt_wA")):
                sp.dma_start(dst, I[n]).then_inc(loaded, 16)
            sp.dma_start(idx[:, :], I["tokidx"].broadcast_to([P, MB])).then_inc(loaded, 16)
            sp.dma_start(tok[:, :], I["c_recip"].broadcast_to([P, MB])).then_inc(loaded, 16)
            sp.wait_ge(loaded, 16 * 9)

        @block.gpsimd
        def _(pool):
            pool.wait_ge(loaded, 16 * 9)
            with pool.Fori(0, NMB // 2) as it:
                for b in range(2):
                    m = it * 2 + b
                    pool.wait_ge(xk1T_ready, m)
                    if b == 0:
                        pool.wait_ge(z_ready, it * 2)
                    else:
                        pool.wait_ge(z_ready, it * 2)
                    for a in range(KD):
                        ins = nc.gpsimd.tensor_tensor(xk1[b][:, a, :, :],
                                                      bcast(S["XKT"][:, a, bass.ds(m * MB, MB)], 1, HR),
                                                      bcast(gmask[:, :], 2, MB), ALU.mult)
                    ins.then_inc(xk1_ready, 1)
                    pool.wait_ge(vs_ready, m + 1)
                    nc.gpsimd.tensor_tensor(rs[:, :], vs[:, :], C["nhalf"][:, 0:HR], ALU.pow).then_inc(rs_ready, 1)
                    pool.wait_ge(rs_ready, m + 1)
                    nc.gpsimd.tensor_tensor(rl[:, :], rs[:, :], S["lA"][:, m, :], ALU.mult).then_inc(rl_ready, 1)

        @block.scalar
        def _(act):
            act.wait_ge(consts, 1)
            with act.Fori(0, NMB // 2) as it:
                for b in range(2):
                    m = it * 2 + b
                    act.wait_ge(xk1T_ready, m + 1)
                    act.wait_ge(dw_ready, it * 2)
                    nc.scalar.activation(xk2[b][:, :], psX[b][:, 0:P], ACT.Copy, scale=ntok[:, 0:1]).then_inc(xk2_ready, 1)
                    act.wait_ge(z_ready, m + 1)
                    act.wait_ge(vs_ready, m)
                    nc.scalar.activation(sq[:, :, 0:HD], heads(psZ[:, 0:32]), ACT.Square).then_inc(sq_ready, 1)
                    act.wait_ge(g_ready, m + 1)
                    nc.scalar.activation(S["GA"][:, m, :], grad[:, :], ACT.Copy).then_inc(g_kept, 1)

        @block.vector
        def _(dve):
            dve.wait_ge(loaded, 16 * 9)
            ch = Chain(dve, dve_step)
            ch.mark(nc.vector.memset(sq[:, :, HD:HD + 1], HD * TTT_EPS))
            ch.done(nc.vector.tensor_reduce(w_m[:, :], heads3(W), AX_X, ALU.add))
            ch.done(nc.vector.scalar_tensor_tensor(out=heads3(W), in0=bcast(w_m[:, :], 2, HD), scalar=-1.0 / HD,
                                                   in1=heads3(W), op0=ALU.mult, op1=ALU.add))
            ch.mark(nc.vector.scalar_tensor_tensor(out=gam2[:, :], in0=gam2[:, :], scalar=float(HD) ** 0.5,
                                                   in1=gam2[:, :], op0=ALU.mult, op1=ALU.mult))
            ch.done(nc.vector.tensor_tensor(tok[:, :], tok[:, :], idx[:, :], ALU.add))
            ch.done(nc.vector.tensor_scalar(tok[:, :], tok[:, :], 0.0, None, ALU.max))
            assert ch.n == INIT, ch.n
            nc.vector.tensor_scalar(ntok[:, :], tok[:, MB - 1:MB], -1.0, None, ALU.mult).then_inc(consts, 1)
            dve.wait_ge(consts, 1)
            nc.vector.tensor_scalar(same[:, :], same[:, :], ntok[:, 0:1], None, ALU.mult).then_inc(consts, 1)
            nc.vector.tensor_copy(S["tok"][:, :], tok[:, :])
            with dve.Fori(0, NT) as t:
                nc.vector.tensor_copy(S["Wt"][:, t, :, :], W[:, :, :])
                with dve.Fori(0, TILE_MB) as s:
                    m = t * TILE_MB + s
                    ch = Chain(dve, dve_step, INIT + m * PER)
                    dve.wait_ge(sq_ready, m + 1)
                    nc.vector.tensor_reduce(vs[:, :], sq[:, :, :], AX_X, ALU.add).then_inc(vs_ready, 1)
                    dve.wait_ge(rs_ready, m + 1)
                    ch.done(nc.vector.tensor_tensor(heads(xn[:, :]), heads(psZ[:, 0:32]), bcast(rs[:, :], 2, HD), ALU.mult))
                    ch.done(nc.vector.tensor_tensor(g[:, :], xn[:, :], gam2[:, :], ALU.mult))
                    ch.done(nc.vector.tensor_tensor(g[:, :], g[:, :], S["cA"][:, m, :], ALU.add))
                    ch.done(nc.vector.tensor_tensor(u[:, :], g[:, :], xn[:, :], ALU.mult))
                    ch.done(nc.vector.tensor_reduce(sg[:, :], heads(u[:, :]), AX_X, ALU.add))
                    ch.done(nc.vector.tensor_tensor(heads(u[:, :]), heads(xn[:, :]), bcast(sg[:, :], 2, HD), ALU.mult))
                    ch.done(nc.vector.tensor_tensor(v[:, :], g[:, :], u[:, :], ALU.subtract))
                    ch.done(nc.vector.tensor_reduce(sg[:, :], heads(v[:, :]), AX_X, ALU.add))
                    ch.done(nc.vector.scalar_tensor_tensor(out=heads(v[:, :]), in0=bcast(sg[:, :], 2, HD),
                                                           scalar=-1.0 / HD, in1=heads(v[:, :]), op0=ALU.mult,
                                                           op1=ALU.add))
                    dve.wait_ge(rl_ready, m + 1)
                    dve.wait_ge(g_kept, m)
                    nc.vector.tensor_tensor(heads(grad[:, :]), heads(v[:, :]), bcast(rl[:, :], 2, HD),
                                            ALU.mult).then_inc(g_ready, 1)
                    assert ch.n == PER, ch.n
                    dve.wait_ge(dw_ready, m + 1)
                    nc.vector.tensor_tensor(W[:, :, :].rearrange("p a (r e) -> p a r e", e=HD),
                                            psW[:, :, 0:32].rearrange("p a (r e) -> p a r e", e=HD),
                                            bcast(rmask[:, :, :], 3, HD), ALU.mult).then_inc(w_ready, 1)
                    dve.wait_ge(w_ready, m + 1)

        @block.tensor
        def _(pe):
            pe.wait_ge(consts, 2)
            with pe.Fori(0, NMB // 2) as it:
                for b in range(2):
                    m = it * 2 + b
                    pe.wait_ge(xk1_ready, m + 1)
                    pe.wait_ge(xk2_ready, it * 2)
                    for a in range(KD):
                        ins = nc.tensor.matmul(psX[b][64 * a:64 * a + 64, 0:P],
                                               xk1[b][:, a, :, :].rearrange("p g t -> p (g t)"), C["ident"][:, :],
                                               start=True, stop=True)
                    ins.then_inc(xk1T_ready, 1)
                    pe.wait_ge(w_ready, m)
                    nc.tensor.matmul(psZ[:, 0:32], first[:, :], W[:, KD, :], start=True, stop=False)
                    for a in range(KD):
                        ins = nc.tensor.matmul(psZ[64 * a:64 * a + 64, 0:32],
                                               xk1[b][:, a, :, :].rearrange("p g t -> p (g t)"), W[:, a, :],
                                               start=False, stop=True)
                    ins.then_inc(z_ready, 1)
                    for a in range(KD + 1):
                        nc.tensor.matmul(psW[:, a, 0:32], C["ident"][:, :], W[:, a, :], start=True, stop=False)
                    pe.wait_ge(xk2_ready, m + 1)
                    pe.wait_ge(g_ready, m + 1)
                    for a in range(KD):
                        nc.tensor.matmul(psW[:, a, 0:32], xk2[b][64 * a:64 * a + 64, :],
                                         grad[64 * a:64 * a + 64, :], start=False, stop=True)
                    nc.tensor.matmul(psW[:, KD, 0:32], same[:, :], grad[:, :], start=False, stop=True).then_inc(dw_ready, 1)


def ttt_output_phase(nc, I, C, S, x_in, x_out):
    with ExitStack() as ctx:
        A = Alloc(nc, ctx, "tout")
        wo = A.sb("wo", [P, KD, D])
        post = A.sb("post", [P, 2, KD])
        gmask = A.sb("gmask", [P, HR])
        rmask = A.sb("rmask", [P, KD + 1, HR])
        brow = A.sb("brow", [P, HG])
        pick = A.sb("pick", [P, P])
        mask = A.sb("mask", [P, P])
        prev = A.sb("prev", [P, P])
        lnw = A.sb("lnw", [P, D])
        lnb = A.sb("lnb", [P, D])
        xk_t = A.sb("xk_t", [P, KD, P])
        xq_t = A.sb("xq_t", [P, KD, P])
        qm = A.sb("qm", [P, KD, HR, P])
        w_bd = A.sb("w_bd", [P, KD, HR, 32])
        b_bd = A.sb("b_bd", [P, HG, 32])
        g_tok = A.sb("g_tok", [P, D])
        x_t = A.sb("x_t", [P, D])
        sm = A.sb("sm", [P, HG, HR, P])
        sq = A.sb("sq", [P, TH, HD + 1])
        vs = A.sb("vs", [P, TH])
        rs = A.sb("rs", [P, TH])
        y = A.sb("y", [P, D])
        stats = A.sb("stats", [P, 6])
        mv = A.sb("mv", [P, 2])
        rstd = A.sb("rstd", [P, 1])
        yT = A.sb("yT", [P, KD, P])
        o_t = A.sb("o_t", [P, D])
        psA = [A.ps(f"psA{b}", [P, HR, P]) for b in range(4)]
        psZ = A.ps("psZ", [P, D])
        psQ = A.ps("psQ", [P, D])
        psT = A.ps("psT", [P, KD, P])
        psO = A.ps("psO", [P, D])
        loaded = A.sem("loaded")
        g_stored = A.sem("g_stored")
        t_loaded = A.sem("t_loaded")
        qk_ready = A.sem("qk_ready")
        qm_ready = A.sem("qm_ready")
        bd_ready = A.sem("bd_ready")
        a_ready = A.sem("a_ready")
        sm_ready = A.sem("sm_ready")
        z_ready = A.sem("z_ready")
        sq_ready = A.sem("sq_ready")
        vs_ready = A.sem("vs_ready")
        rs_ready = A.sem("rs_ready")
        mv_ready = A.sem("mv_ready")
        rstd_ready = A.sem("rstd_ready")
        y_ready = A.sem("y_ready")
        T_ready = A.sem("T_ready")
        yT_ready = A.sem("yT_ready")
        o_ready = A.sem("o_ready")
        x_done = A.sem("x_done")
        stored = A.sem("stored")
        dve_step = A.sem("dve_step")
        block = ctx.enter_context(nc.Block())
        INIT, PER = 5, 7
        NLOAD = 10

        @block.sync
        def _(sp):
            dst = S["g_dram"].rearrange("(m t) n -> t m n", t=MB)
            for g in range(HG):
                sp.dma_start(dst[:, :, g * 32:(g + 1) * 32], S["GA"][g * MB:(g + 1) * MB, :, :]).then_inc(g_stored, 16)
            sp.dma_start(wo[:, :, :], I["owT"].rearrange("(k p) n -> p k n", p=P)).then_inc(loaded, 16)
            for d, n in ((gmask[:, :], "c_gmask"), (rmask[:, :, :], "c_rmask"), (brow[:, :], "c_brow"),
                         (pick[:, :], "c_pick"), (mask[:, :], "c_causal"), (prev[:, :], "c_prev"),
                         (post[:, :, :], "post"), (lnw[:, :], "ttt_w"), (lnb[:, :], "ttt_b")):
                src = I[n].broadcast_to([P, D]) if n.startswith("ttt") else I[n]
                sp.dma_start(d, src).then_inc(loaded, 16)
            sp.wait_ge(g_stored, 16 * HG)
            with sp.Fori(0, NT) as t:
                sp.wait_ge(x_done, t)
                sp.dma_start(g_tok[:, :], S["g_dram"][bass.ds(t * P, P), :]).then_inc(t_loaded, 16)
                sp.dma_start(x_t[:, :], x_in[bass.ds(t * P, P), :]).then_inc(t_loaded, 16)
                sp.wait_ge(x_done, t + 1)
                sp.dma_start(x_out[bass.ds(t * P, P), :], o_t[:, :]).then_inc(stored, 16)
            sp.wait_ge(stored, 16 * NT)

        @block.scalar
        def _(act):
            act.wait_ge(loaded, 16 * NLOAD)
            act.wait_ge(bd_ready, 1)
            with act.Fori(0, NT) as t:
                act.wait_ge(z_ready, t)
                nc.scalar.activation(xk_t[:, :, :], S["XKT"][:, :, bass.ds(t * P, P)], ACT.Copy)
                nc.scalar.activation(xq_t[:, :, :], S["XQT"][:, :, bass.ds(t * P, P)], ACT.Copy).then_inc(qk_ready, 1)
                act.wait_ge(z_ready, t + 1)
                nc.scalar.activation(sq[:, :, 0:HD], psZ[:, :].rearrange("p (h e) -> p h e", e=HD),
                                     ACT.Square).then_inc(sq_ready, 1)
                act.wait_ge(T_ready, t + 1)
                for k in range(KD):
                    ins = nc.scalar.activation(yT[:, k, :], psT[:, k, :], ACT.Identity,
                                               bias=post[:, 1, k:k + 1], scale=post[:, 0, k:k + 1])
                ins.then_inc(yT_ready, 1)

        @block.gpsimd
        def _(pool):
            with pool.Fori(0, NT) as t:
                pool.wait_ge(qk_ready, t + 1)
                pool.wait_ge(z_ready, t)
                for a in range(KD):
                    ins = nc.gpsimd.tensor_tensor(qm[:, a, :, :], bcast(xq_t[:, a, :], 1, HR),
                                                  bcast(rmask[:, 0, :], 2, P), ALU.mult)
                ins.then_inc(qm_ready, 1)
                pool.wait_ge(vs_ready, t + 1)
                nc.gpsimd.tensor_tensor(rs[:, :], vs[:, :], C["nhalf"][:, :], ALU.pow).then_inc(rs_ready, 1)
                pool.wait_ge(mv_ready, t + 1)
                nc.gpsimd.tensor_tensor(rstd[:, :], mv[:, 1:2], C["nhalf"][:, 0:1], ALU.pow).then_inc(rstd_ready, 1)

        @block.vector
        def _(dve):
            dve.wait_ge(loaded, 16 * NLOAD)
            ch = Chain(dve, dve_step)
            ch.mark(nc.vector.memset(sq[:, :, HD:HD + 1], HD * TTT_EPS))
            ch.mark(nc.vector.tensor_scalar(lnw[:, :], lnw[:, :], float(HD) ** 0.5, None, ALU.mult))
            m3 = mask[:, :].rearrange("p (m t) -> p m t", t=MB)
            ch.done(nc.vector.tensor_tensor(m3, m3, bcast(S["tok"][:, :], 1, P // MB), ALU.mult))
            ch.done(nc.vector.scalar_tensor_tensor(out=mask[:, :], in0=prev[:, :], scalar=S["tok"][:, MB - 1:MB],
                                                   in1=mask[:, :], op0=ALU.mult, op1=ALU.add))
            ch.done(nc.vector.tensor_scalar(mask[:, :], mask[:, :], -1.0, None, ALU.mult))
            nc.vector.memset(stats[:, :], 0.0).then_inc(bd_ready, 1)
            assert ch.n == INIT, ch.n
            with dve.Fori(0, NT) as t:
                ch = Chain(dve, dve_step, INIT + t * PER)
                dve.wait_ge(z_ready, t)
                for a in range(KD):
                    nc.vector.tensor_tensor(w_bd[:, a, :, :], bcast(S["Wt"][:, t, a, :], 1, HR),
                                            bcast(gmask[:, :], 2, 32), ALU.mult)
                nc.vector.tensor_tensor(b_bd[:, :, :], bcast(S["Wt"][:, t, KD, :], 1, HG),
                                        bcast(brow[:, :], 2, 32), ALU.mult).then_inc(bd_ready, 1)
                for g in range(HG):
                    dve.wait_ge(a_ready, t * HG + g + 1)
                    nc.vector.scalar_tensor_tensor(out=sm[:, g, :, :], in0=psA[g % 4][:, :, :], scalar=1.0,
                                                   in1=bcast(mask[:, :], 1, HR), op0=ALU.add,
                                                   op1=ALU.mult).then_inc(sm_ready, 1)
                dve.wait_ge(sq_ready, t + 1)
                nc.vector.tensor_reduce(vs[:, :], sq[:, :, :], AX_X, ALU.add).then_inc(vs_ready, 1)
                y3 = y[:, :].rearrange("p (h e) -> p h e", e=HD)
                dve.wait_ge(rs_ready, t + 1)
                ch.done(nc.vector.tensor_tensor(y3, psZ[:, :].rearrange("p (h e) -> p h e", e=HD),
                                                bcast(rs[:, :], 2, HD), ALU.mult))
                ch.done(nc.vector.tensor_tensor(y[:, :], y[:, :], lnw[:, :], ALU.mult))
                ch.done(nc.vector.tensor_tensor(y[:, :], y[:, :], lnb[:, :], ALU.add))
                ch.done(nc.vector.tensor_tensor(y[:, :], psQ[:, :], y[:, :], ALU.add))
                ch.done_before(nc.vector.bn_stats(stats[:, :], y[:, :]), C["pad"])
                ch.done(nc.vector.bn_aggr(mv[:, :], stats[:, :]))
                nc.vector.tensor_scalar(mv[:, 1:2], mv[:, 1:2], TTT_EPS, None, ALU.add).then_inc(mv_ready, 1)
                dve.wait_ge(rstd_ready, t + 1)
                nc.vector.tensor_scalar(y[:, :], y[:, :], mv[:, 0:1], rstd[:, 0:1], ALU.subtract,
                                        ALU.mult).then_inc(y_ready, 1)
                dve.wait_ge(o_ready, t + 1)
                dve.wait_ge(t_loaded, 32 * (t + 1))
                dve.wait_ge(stored, 16 * t)
                ch.done(nc.vector.tensor_tensor(o_t[:, :], psO[:, :], C["gate_row"][:, 0, 0, :], ALU.mult))
                nc.vector.tensor_tensor(o_t[:, :], o_t[:, :], x_t[:, :], ALU.add).then_inc(x_done, 1)
                assert ch.n == PER, ch.n

        @block.tensor
        def _(pe):
            pe.wait_ge(loaded, 16 * NLOAD)
            with pe.Fori(0, NT) as t:
                pe.wait_ge(qk_ready, t + 1)
                pe.wait_ge(bd_ready, t + 2)
                pe.wait_ge(y_ready, t)
                for a in range(KD):
                    nc.tensor.matmul(psQ[:, a * P:(a + 1) * P], xq_t[:, a, :], C["ident"][:, :], start=True, stop=True)
                nc.tensor.matmul(psZ[:, :], pick[:, :], b_bd[:, :, :], start=True, stop=False)
                for a in range(KD):
                    nc.tensor.matmul(psZ[:, a * P:(a + 1) * P], xq_t[:, a, :], w_bd[:, a, :, :], start=False, stop=False)
                pe.wait_ge(qm_ready, t + 1)
                for g in range(HG):
                    a, q = g // HR, g % HR
                    if a:
                        pe.wait_ge(sm_ready, t * HG + g - HR + 1)
                    nc.tensor.matmul(psA[q][:, :, :], xk_t[32 * q:32 * q + 32, a, :], qm[32 * q:32 * q + 32, a, :, :],
                                     start=True, stop=True).then_inc(a_ready, 1)
                pe.wait_ge(t_loaded, 32 * (t + 1))
                for g in range(HG):
                    pe.wait_ge(sm_ready, t * HG + g + 1)
                    for r in range(HR):
                        c = (g * HR + r) * HD
                        ins = nc.tensor.matmul(psZ[:, c:c + HD], sm[:, g, r, :], g_tok[:, c:c + HD], start=False,
                                               stop=(g == HG - 1 and r == HR - 1))
                ins.then_inc(z_ready, 1)
                pe.wait_ge(y_ready, t + 1)
                for k in range(KD):
                    ins = nc.tensor.matmul(psT[:, k, :], y[:, k * P:(k + 1) * P], C["ident"][:, :], start=True, stop=True)
                ins.then_inc(T_ready, 1)
                pe.wait_ge(yT_ready, t + 1)
                for k in range(KD):
                    ins = nc.tensor.matmul(psO[:, :], yT[:, k, :], wo[:, k, :], start=(k == 0), stop=(k == KD - 1))
                ins.then_inc(o_ready, 1)


E1, K1, I1 = 32, 8, 128
E1S = E1 + 2
SCALE1 = 2.5


def moe1_route_phase(nc, I, C, S, x_in):
    with ExitStack() as ctx:
        A = Alloc(nc, ctx, "route")
        gw = A.sb("gw", [P, KD, E1])
        x_t = [A.sb(f"x_t{b}", [P, D]) for b in range(2)]
        stats = A.sb("stats", [P, 6])
        mv = A.sb("mv", [P, 2])
        rstd = A.sb("rstd", [P, 1])
        xh = A.sb("xh", [P, D])
        hT = A.sb("hT", [P, KD, P])
        sc = A.sb("sc", [P, E1])
        top = A.sb("top", [P, K1])
        rest = A.sb("rest", [P, E1])
        tot = A.sb("tot", [P, 1])
        dw = A.sb("dw", [P, E1])
        dwT = A.sb("dwT", [E1, T])
        ones = A.sb("ones", [E1S - E1, T])
        psT = A.ps("psT", [P, KD, P])
        psS = A.ps("psS", [P, E1])
        psD = A.ps("psD", [E1, P])
        loaded = A.sem("loaded")
        x_ready = [A.sem(f"x_ready{b}") for b in range(2)]
        mv_ready = A.sem("mv_ready")
        rstd_ready = A.sem("rstd_ready")
        xh_ready = A.sem("xh_ready")
        T_ready = A.sem("T_ready")
        hT_ready = A.sem("hT_ready")
        s_ready = A.sem("s_ready")
        sc_ready = A.sem("sc_ready")
        dw_ready = A.sem("dw_ready")
        dT_ready = A.sem("dT_ready")
        dT_kept = A.sem("dT_kept")
        stored = A.sem("stored")
        ones_ready = A.sem("ones_ready")
        dve_step2 = A.sem("dve_step2")
        dve_step = A.sem("dve_step")
        block = ctx.enter_context(nc.Block())
        PER = 8

        @block.sync
        def _(sp):
            sp.dma_start(gw[:, :, :], I["gate1T"].rearrange("(k p) n -> p k n", p=P)).then_inc(loaded, 16)
            with sp.Fori(0, NT // 2) as it:
                for b in range(2):
                    sp.wait_ge(xh_ready, it * 2)
                    sp.dma_start(x_t[b][:, :], x_in[bass.ds((it * 2 + b) * P, P), :]).then_inc(x_ready[b], 16)
            sp.wait_ge(dT_kept, NT)
            sp.dma_start(S["dwT"][0:E1, :], dwT[:, :]).then_inc(stored, 16)
            sp.wait_ge(ones_ready, 1)
            sp.dma_start(S["dwT"][E1:E1S, :], ones[:, :]).then_inc(stored, 16)
            sp.wait_ge(stored, 32)

        @block.vector
        def _(dve):
            nc.vector.memset(ones[:, :], 1.0).then_inc(ones_ready, 1)
            with dve.Fori(0, NT // 2) as it:
                ch = Chain(dve, dve_step, it * 2 * PER)
                for b in range(2):
                    t = it * 2 + b
                    dve.wait_ge(x_ready[b], (it + 1) * 16)
                    ch.done_before(nc.vector.bn_stats(stats[:, :], x_t[b][:, :]), C["pad"])
                    ch.done(nc.vector.bn_aggr(mv[:, :], stats[:, :]))
                    nc.vector.tensor_scalar(mv[:, 1:2], mv[:, 1:2], EPS, None, ALU.add).then_inc(mv_ready, 1)
                    dve.wait_ge(rstd_ready, t + 1)
                    dve.wait_ge(T_ready, t)
                    nc.vector.tensor_scalar(xh[:, :], x_t[b][:, :], mv[:, 0:1], rstd[:, 0:1], ALU.subtract,
                                            ALU.mult).then_inc(xh_ready, 1)
                    dve.wait_ge(sc_ready, t + 1)
                    nc.vector.tensor_copy(C["pad"][:, 1:2], C["pad"][:, 0:1])
                    ch.done_before(nc.vector.max(out=top[:, :], in_=sc[:, :]), C["pad"])
                    ch.done(nc.vector.match_replace(out=rest[:, :], in_to_replace=top[:, :], in_values=sc[:, :],
                                                    imm_value=-1.0))
                    ch.mark(nc.vector.tensor_reduce(tot[:, :], top[:, :], AX_X, ALU.add))
                    ch.done(nc.vector.tensor_tensor(rest[:, :], rest[:, :], sc[:, :], ALU.not_equal))
                    ch.done(nc.vector.tensor_scalar(tot[:, :], tot[:, :], 1e-20, None, ALU.add))
                    ch.done(nc.vector.reciprocal(tot[:, :], tot[:, :]))
                    nc.vector.tensor_tensor(rest[:, :], rest[:, :], sc[:, :], ALU.mult).then_inc(dve_step2, 1)
                    dve.wait_ge(dve_step2, t + 1)
                    dve.wait_ge(dT_ready, t)
                    nc.vector.tensor_scalar(dw[:, :], rest[:, :], tot[:, 0:1], SCALE1, ALU.mult, ALU.mult).then_inc(dw_ready, 1)
                assert ch.n == 2 * PER, ch.n

        @block.gpsimd
        def _(pool):
            with pool.Fori(0, NT) as t:
                pool.wait_ge(mv_ready, t + 1)
                nc.gpsimd.tensor_tensor(rstd[:, :], mv[:, 1:2], C["nhalf"][:, 0:1], ALU.pow).then_inc(rstd_ready, 1)

        @block.scalar
        def _(act):
            with act.Fori(0, NT) as t:
                act.wait_ge(T_ready, t + 1)
                act.wait_ge(s_ready, t)
                for k in range(KD):
                    ins = nc.scalar.activation(hT[:, k, :], psT[:, k, :], ACT.Identity,
                                               bias=C["mod_col"][:, 0, 2, k:k + 1], scale=C["mod_col"][:, 0, 3, k:k + 1])
                ins.then_inc(hT_ready, 1)
                act.wait_ge(hT_ready, t + 1)
                nc.scalar.activation(S["hT"][:, :, bass.ds(t * P, P)], hT[:, :, :], ACT.Copy)
                act.wait_ge(s_ready, t + 1)
                act.wait_ge(dw_ready, t)
                nc.scalar.activation(sc[:, :], psS[:, :], ACT.Sigmoid).then_inc(sc_ready, 1)
                act.wait_ge(dT_ready, t + 1)
                nc.scalar.activation(dwT[:, bass.ds(t * P, P)], psD[:, :], ACT.Copy).then_inc(dT_kept, 1)

        @block.tensor
        def _(pe):
            pe.wait_ge(loaded, 16)
            with pe.Fori(0, NT) as t:
                pe.wait_ge(xh_ready, t + 1)
                pe.wait_ge(hT_ready, t)
                for k in range(KD):
                    ins = nc.tensor.matmul(psT[:, k, :], xh[:, k * P:(k + 1) * P], C["ident"][:, :], start=True, stop=True)
                ins.then_inc(T_ready, 1)
                pe.wait_ge(hT_ready, t + 1)
                pe.wait_ge(sc_ready, t)
                for k in range(KD):
                    ins = nc.tensor.matmul(psS[:, :], hT[:, k, :], gw[:, k, :], start=(k == 0), stop=(k == KD - 1))
                ins.then_inc(s_ready, 1)
                pe.wait_ge(dw_ready, t + 1)
                pe.wait_ge(dT_kept, t)
                nc.tensor.matmul(psD[:, :], dw[:, :], C["ident"][:, :], start=True, stop=True).then_inc(dT_ready, 1)


def moe1_expert_phase(nc, I, C, S, x_in, x_out):
    with ExitStack() as ctx:
        A = Alloc(nc, ctx, "experts")
        NS, SUB = 2, 512
        BLK = NS * SUB
        NB = T // BLK
        NTB = BLK // P
        w = [A.sb(f"w{b}", [P, 3, D]) for b in range(2)]
        dwb = [A.sb(f"dwb{b}", [P, NS, SUB]) for b in range(2)]
        sg = [A.sb(f"sg{b}", [P, SUB]) for b in range(2)]
        up = [A.sb(f"up{b}", [P, SUB]) for b in range(2)]
        act_ = [A.sb(f"act{b}", [P, SUB]) for b in range(2)]
        zeros = A.sb("zeros", [P, SUB])
        x_t = A.sb("x_t", [P, NTB, D])
        psG = [A.ps(f"psG{b}", [P, SUB]) for b in range(2)]
        psU = [A.ps(f"psU{b}", [P, SUB]) for b in range(2)]
        psY = A.ps("psY", [P, NTB, D])
        w_ready = [A.sem(f"w_ready{b}") for b in range(2)]
        gu_ready = A.sem("gu_ready")
        sg_ready = A.sem("sg_ready")
        up_ready = A.sem("up_ready")
        act_ready = A.sem("act_ready")
        down_done = A.sem("down_done")
        y_ready = A.sem("y_ready")
        y_read = A.sem("y_read")
        x_ready = A.sem("x_ready")
        gated = A.sem("gated")
        x_done = A.sem("x_done")
        stored = A.sem("stored")
        zero_ready = A.sem("zero_ready")
        block = ctx.enter_context(nc.Block())
        NP = E1S // 2
        STEPS = NP * 2 * NS
        Q = 2 * NS

        @block.sync
        def _(sp):
            with sp.Fori(0, NB) as n:
                with sp.Fori(0, NP) as it:
                    for b in range(2):
                        sp.wait_ge(down_done, n * STEPS + it * Q)
                        sp.dma_start(w[b][:, :, :], I["w1"][bass.ds((it * 2 + b), 1), :, :].rearrange(
                            "e p (c n) -> p (e c) n", c=3)).then_inc(w_ready[b], 16)
                        sp.dma_start(dwb[b][:, :, :].rearrange("p s n -> p (s n)"),
                                     S["dwT"][bass.ds(it * 2 + b, 1), bass.ds(n * BLK, BLK)].broadcast_to(
                                         [P, BLK])).then_inc(w_ready[b], 16)
                sp.wait_ge(stored, n * 16)
                sp.dma_start(x_t[:, :, :], x_in[bass.ds(n * BLK, BLK), :].rearrange("(j p) d -> p j d", p=P)).then_inc(x_ready, 16)
                sp.wait_ge(x_done, n + 1)
                sp.dma_start(x_out[bass.ds(n * BLK, BLK), :].rearrange("(j p) d -> p j d", p=P), x_t[:, :, :]).then_inc(stored, 16)
            sp.wait_ge(stored, NB * 16)

        @block.scalar
        def _(act):
            with act.Fori(0, NB * NP) as it:
                for i in range(Q):
                    s = it * Q + i
                    act.wait_ge(gu_ready, s + 1)
                    if i < 2:
                        act.wait_ge(act_ready, it * Q)
                    else:
                        act.wait_ge(act_ready, s - 1)
                    nc.scalar.activation(sg[i % 2][:, :], psG[i % 2][:, :], ACT.Silu).then_inc(sg_ready, 1)

        @block.vector
        def _(dve):
            nc.vector.memset(zeros[:, :], 0.0).then_inc(zero_ready, 1)
            with dve.Fori(0, NB) as n:
                with dve.Fori(0, NP) as it:
                    for i in range(Q):
                        s = n * STEPS + it * Q + i
                        b, h = i // NS, i % NS
                        if h == 0:
                            dve.wait_ge(w_ready[b], 32 * (n * NP + it + 1))
                        dve.wait_ge(gu_ready, s + 1)
                        nc.vector.tensor_tensor(up[i % 2][:, :], psU[i % 2][:, :], dwb[b][:, h, :], ALU.mult).then_inc(up_ready, 1)
                        dve.wait_ge(sg_ready, s + 1)
                        dve.wait_ge(up_ready, s + 1)
                        if i < 2:
                            dve.wait_ge(down_done, n * STEPS + it * Q)
                        else:
                            dve.wait_ge(down_done, s - 1)
                        nc.vector.tensor_tensor(act_[i % 2][:, :], up[i % 2][:, :], sg[i % 2][:, :], ALU.mult).then_inc(act_ready, 1)
                dve.wait_ge(y_ready, n + 1)
                dve.wait_ge(x_ready, (n + 1) * 16)
                for j in range(NTB):
                    nc.vector.tensor_tensor(psY[:, j, :], psY[:, j, :], C["gate_row"][:, 0, 1, :], ALU.mult).then_inc(gated, 1)
                dve.wait_ge(gated, (n + 1) * NTB)
                nc.vector.tensor_tensor(x_t[:, :, :], psY[:, :, :], x_t[:, :, :], ALU.add).then_inc(x_done, 1)

        @block.tensor
        def _(pe):
            pe.wait_ge(zero_ready, 1)
            with pe.Fori(0, NB) as n:
                pe.wait_ge(x_done, n)
                for j in range(0, NTB, 2):
                    nc.tensor.matmul(psY[:, j:j + 2, :], C["ident"][:, :], zeros[:, :], start=True, stop=False)
                with pe.Fori(0, NP) as it:
                    base = n * STEPS + it * Q

                    def gate_up(i):
                        b, h = i // NS, i % NS
                        if h == 0:
                            pe.wait_ge(w_ready[b], 32 * (n * NP + it + 1))
                        if i < 2:
                            pe.wait_ge(act_ready, base)
                        else:
                            pe.wait_ge(act_ready, base + i - 1)
                        for c, ps in enumerate((psG[i % 2], psU[i % 2])):
                            for k in range(KD):
                                ins = nc.tensor.matmul(ps[:, :], w[b][:, k, c * I1:(c + 1) * I1],
                                                       S["hT"][:, k, bass.ds(n * BLK + h * SUB, SUB)],
                                                       start=(k == 0), stop=(k == KD - 1))
                        ins.then_inc(gu_ready, 1)

                    def down(i):
                        b, h = i // NS, i % NS
                        pe.wait_ge(act_ready, base + i + 1)
                        for j in range(SUB // P):
                            ins = nc.tensor.matmul(psY[:, h * (SUB // P) + j, :], act_[i % 2][:, j * P:(j + 1) * P],
                                                   w[b][:, 2, :], start=False, stop=False)
                        ins.then_inc(down_done, 1)

                    gate_up(0)
                    for i in range(1, Q):
                        gate_up(i)
                        down(i - 1)
                    down(Q - 1)
                for j in range(0, NTB, 2):
                    ins = nc.tensor.matmul(psY[:, j:j + 2, :], C["ident"][:, :], zeros[:, :], start=False, stop=True)
                ins.then_inc(y_ready, 1)


E2, K2, BOT = 8, 2, 64
M2 = E2 * BOT // P


def moe2_phase(nc, I, C, x_in, x_out):
    with ExitStack() as ctx:
        A = Alloc(nc, ctx, "moe2")
        TB = 4
        BLK = TB * P
        NB = T // BLK
        gw = A.sb("gw", [P, KD, E2])
        wd = A.sb("wd", [P, KD, E2 * BOT])
        wu = A.sb("wu", [P, M2, D])
        bd = A.sb("bd", [P, M2])
        wsd = A.sb("wsd", [P, KD, BOT])
        wsu = A.sb("wsu", [BOT, D])
        bsd = A.sb("bsd", [BOT, 1])
        bu = A.sb("bu", [E2 + 1, D])
        sel = A.sb("sel", [E2 + 1, M2, P])
        tri = A.sb("tri", [P, E2 * E2])
        x_t = [A.sb(f"x_t{b}", [P, TB, D]) for b in range(2)]
        stats = A.sb("stats", [P, TB, 6])
        mv = A.sb("mv", [P, TB, 2])
        rstd = A.sb("rstd", [P, TB])
        xh = A.sb("xh", [P, TB, D])
        hT = A.sb("hT", [P, KD, BLK])
        pr = A.sb("pr", [P, TB, E2])
        mx = A.sb("mx", [P, TB])
        gt = A.sb("gt", [P, TB, E2, E2])
        eq = A.sb("eq", [P, TB, E2, E2])
        rank = A.sb("rank", [P, TB, E2])
        cT = A.sb("cT", [E2 + 1, BLK])
        hm = A.sb("hm", [P, M2, BLK])
        hs = A.sb("hs", [BOT, BLK])
        y = A.sb("y", [P, TB, D])
        psT = A.ps("psT", [P, 2, 512])
        psL = A.ps("psL", [P, TB, E2])
        psH = [A.ps(f"psH{b}", [P, BLK]) for b in range(2)]
        psC = A.ps("psC", [P, BLK])
        psY = A.ps("psY", [P, 2, 512])
        loaded = A.sem("loaded")
        x_ready = [A.sem(f"x_ready{b}") for b in range(2)]
        mv_ready = A.sem("mv_ready")
        rstd_ready = A.sem("rstd_ready")
        xh_ready = A.sem("xh_ready")
        T_ready = A.sem("T_ready")
        hT_ready = A.sem("hT_ready")
        l_ready = A.sem("l_ready")
        e_in = A.sem("e_in")
        e_ready = A.sem("e_ready")
        c_ready = A.sem("c_ready")
        cT_ready = A.sem("cT_ready")
        cT_kept = A.sem("cT_kept")
        h_ready = A.sem("h_ready")
        gelu_ready = A.sem("gelu_ready")
        w_ready = A.sem("w_ready")
        hm_ready = A.sem("hm_ready")
        y_ready = A.sem("y_ready")
        y_gated = A.sem("y_gated")
        x_done = A.sem("x_done")
        stored = [A.sem(f"stored{b}") for b in range(2)]
        ones_ready = A.sem("ones_ready")
        dve_step = A.sem("dve_step")
        block = ctx.enter_context(nc.Block())
        PER = 13
        NLOAD = 10

        @block.sync
        def _(sp):
            for d, n in ((gw, "gate2T"), (wd, "wdT"), (wsd, "wsdT")):
                sp.dma_start(d[:, :, :], I[n].rearrange("(k p) n -> p k n", p=P)).then_inc(loaded, 16)
            sp.dma_start(wu[:, :, :], I["wuT"].rearrange("(m p) n -> p m n", p=P)).then_inc(loaded, 16)
            sp.dma_start(sel[:, :, :], I["c_sel"]).then_inc(loaded, 16)
            for d, n in ((bd, "bd"), (wsu, "wsuT"), (bsd, "bsd"), (bu, "bu")):
                sp.dma_start(d[:, :], I[n]).then_inc(loaded, 16)
            sp.dma_start(tri[:, :], I["c_tri"].broadcast_to([P, E2 * E2])).then_inc(loaded, 16)
            with sp.Fori(0, NB // 2) as it:
                for b in range(2):
                    sp.wait_ge(stored[b], it * 16)
                    sp.dma_start(x_t[b][:, :, :], x_in[bass.ds((it * 2 + b) * BLK, BLK), :].rearrange(
                        "(j p) d -> p j d", p=P)).then_inc(x_ready[b], 16)
                for b in range(2):
                    sp.wait_ge(x_done, it * 2 + b + 1)
                    sp.dma_start(x_out[bass.ds((it * 2 + b) * BLK, BLK), :].rearrange("(j p) d -> p j d", p=P),
                                 x_t[b][:, :, :]).then_inc(stored[b], 16)
            for b in range(2):
                sp.wait_ge(stored[b], NB // 2 * 16)

        @block.gpsimd
        def _(pool):
            nc.gpsimd.memset(cT[:, :], 1.0).then_inc(ones_ready, 1)
            with pool.Fori(0, NB) as n:
                pool.wait_ge(mv_ready, n + 1)
                nc.gpsimd.tensor_tensor(rstd[:, :], mv[:, :, 1], C["nhalf"][:, 0:TB], ALU.pow).then_inc(rstd_ready, 1)

        @block.scalar
        def _(act):
            act.wait_ge(loaded, 16 * NLOAD)
            act.wait_ge(ones_ready, 1)
            with act.Fori(0, NB) as n:
                act.wait_ge(h_ready, n * (M2 + 1))
                for k in range(KD):
                    act.wait_ge(T_ready, n * KD + k + 1)
                    ins = nc.scalar.activation(hT[:, k, :], psT[:, k, :], ACT.Identity,
                                               bias=C["mod_col"][:, 1, 2, k:k + 1], scale=C["mod_col"][:, 1, 3, k:k + 1])
                ins.then_inc(hT_ready, 1)
                act.wait_ge(e_in, n + 1)
                nc.scalar.activation(pr[:, :, :], pr[:, :, :], ACT.Exp).then_inc(e_ready, 1)
                for m in range(M2):
                    act.wait_ge(h_ready, n * (M2 + 1) + m + 1)
                    act.wait_ge(y_ready, n * TB)
                    nc.scalar.activation(hm[:, m, :], psH[m % 2][:, :], ACT.Gelu, bias=bd[:, m:m + 1]).then_inc(gelu_ready, 1)
                act.wait_ge(h_ready, n * (M2 + 1) + M2 + 1)
                nc.scalar.activation(hs[:, :], psH[M2 % 2][0:BOT, :], ACT.Gelu, bias=bsd[:, 0:1]).then_inc(gelu_ready, 1)

        @block.vector
        def _(dve):
            dve.wait_ge(loaded, 16 * NLOAD)
            with dve.Fori(0, NB // 2) as it:
                for b in range(2):
                    n = it * 2 + b
                    ch = Chain(dve, dve_step, n * PER)
                    dve.wait_ge(x_ready[b], (it + 1) * 16)
                    for j in range(TB):
                        ins = nc.vector.bn_stats(stats[:, j, :], x_t[b][:, j, :])
                    ch.done_before(ins, C["pad"])
                    for j in range(TB):
                        ins = nc.vector.bn_aggr(mv[:, j, :], stats[:, j, :])
                    ch.done(ins)
                    nc.vector.tensor_scalar(mv[:, :, 1], mv[:, :, 1], EPS, None, ALU.add).then_inc(mv_ready, 1)
                    dve.wait_ge(rstd_ready, n + 1)
                    for j in range(TB):
                        nc.vector.tensor_scalar(xh[:, j, :], x_t[b][:, j, :], mv[:, j, 0:1], rstd[:, j:j + 1], ALU.subtract,
                                                ALU.mult).then_inc(xh_ready, 1)
                    dve.wait_ge(l_ready, n + 1)
                    ch.done(nc.vector.tensor_reduce(mx[:, :], psL[:, :, :], AX_X, ALU.max))
                    nc.vector.tensor_tensor(pr[:, :, :], psL[:, :, :], bcast(mx[:, :], 2, E2), ALU.subtract).then_inc(e_in, 1)
                    dve.wait_ge(e_ready, n + 1)
                    ch.done(nc.vector.tensor_reduce(mx[:, :], pr[:, :, :], AX_X, ALU.add))
                    ch.done(nc.vector.reciprocal(mx[:, :], mx[:, :]))
                    ch.done(nc.vector.tensor_tensor(pr[:, :, :], pr[:, :, :], bcast(mx[:, :], 2, E2), ALU.mult))
                    mine, other = bcast(pr[:, :, :], 3, E2), bcast(pr[:, :, :], 2, E2)
                    nc.vector.tensor_tensor(gt[:, :, :, :], other, mine, ALU.is_gt)
                    ch.done(nc.vector.tensor_tensor(eq[:, :, :, :], other, mine, ALU.is_equal))
                    flat = lambda a: a[:, :, :, :].rearrange("p j a b -> p j (a b)")
                    ch.done(nc.vector.tensor_tensor(flat(eq), flat(eq), bcast(tri[:, :], 1, TB), ALU.mult))
                    ch.done(nc.vector.tensor_tensor(flat(gt), flat(gt), flat(eq), ALU.add))
                    ch.done(nc.vector.tensor_reduce(rank[:, :, :], gt[:, :, :, :], AX_X, ALU.add))
                    ch.done(nc.vector.scalar_tensor_tensor(out=pr[:, :, :], in0=rank[:, :, :], scalar=float(K2),
                                                           in1=pr[:, :, :], op0=ALU.is_lt, op1=ALU.mult))
                    ch.done(nc.vector.tensor_reduce(mx[:, :], pr[:, :, :], AX_X, ALU.add))
                    ch.done(nc.vector.reciprocal(mx[:, :], mx[:, :]))
                    dve.wait_ge(cT_ready, n)
                    nc.vector.tensor_tensor(rank[:, :, :], pr[:, :, :], bcast(mx[:, :], 2, E2), ALU.mult).then_inc(c_ready, 1)
                    dve.wait_ge(cT_ready, n + 1)
                    nc.vector.tensor_copy(cT[0:E2, :], psC[0:E2, :]).then_inc(cT_kept, 1)
                    for m in range(M2):
                        dve.wait_ge(w_ready, n * M2 + m + 1)
                        dve.wait_ge(gelu_ready, n * (M2 + 1) + m + 1)
                        nc.vector.tensor_tensor(hm[:, m, :], psC[:, :], hm[:, m, :], ALU.mult).then_inc(hm_ready, 1)
                    for j in range(TB):
                        dve.wait_ge(y_ready, n * TB + j + 1)
                        nc.vector.tensor_tensor(y[:, j, :], psY[:, j % 2, 0:D], C["gate_row"][:, 1, 1, :],
                                                ALU.mult).then_inc(y_gated, 1)
                    dve.wait_ge(y_gated, n * TB + TB)
                    nc.vector.tensor_tensor(x_t[b][:, :, :], y[:, :, :], x_t[b][:, :, :], ALU.add).then_inc(x_done, 1)
                    assert ch.n == PER, ch.n

        @block.tensor
        def _(pe):
            pe.wait_ge(loaded, 16 * NLOAD)
            with pe.Fori(0, NB) as n:
                pe.wait_ge(hT_ready, n)
                for k in range(KD):
                    for j in range(TB):
                        if k == 0:
                            pe.wait_ge(xh_ready, n * TB + j + 1)
                        ins = nc.tensor.matmul(psT[:, k, j * P:(j + 1) * P], xh[:, j, k * P:(k + 1) * P],
                                               C["ident"][:, :], start=True, stop=True)
                    ins.then_inc(T_ready, 1)
                pe.wait_ge(hT_ready, n + 1)
                pe.wait_ge(e_in, n)
                for j in range(TB):
                    for k in range(KD):
                        ins = nc.tensor.matmul(psL[:, j, :], hT[:, k, j * P:(j + 1) * P], gw[:, k, :],
                                               start=(k == 0), stop=(k == KD - 1))
                ins.then_inc(l_ready, 1)

                def bottleneck(m):
                    if m >= 2:
                        pe.wait_ge(gelu_ready, n * (M2 + 1) + m - 1)
                    else:
                        pe.wait_ge(gelu_ready, n * (M2 + 1))
                    for k in range(KD):
                        if m < M2:
                            ins = nc.tensor.matmul(psH[m % 2][:, :], wd[:, k, m * P:(m + 1) * P], hT[:, k, :],
                                                   start=(k == 0), stop=(k == KD - 1))
                        else:
                            ins = nc.tensor.matmul(psH[m % 2][0:BOT, :], wsd[:, k, :], hT[:, k, :],
                                                   start=(k == 0), stop=(k == KD - 1))
                    ins.then_inc(h_ready, 1)

                def spread(m):
                    if m:
                        pe.wait_ge(hm_ready, n * M2 + m)
                    nc.tensor.matmul(psC[:, :], sel[:, m, :], cT[:, :], start=True, stop=True).then_inc(w_ready, 1)

                bottleneck(0)
                bottleneck(1)
                pe.wait_ge(c_ready, n + 1)
                pe.wait_ge(hm_ready, n * M2)
                for j in range(TB):
                    ins = nc.tensor.matmul(psC[0:E2, j * P:(j + 1) * P], rank[:, j, :], C["ident"][:, :],
                                           start=True, stop=True)
                ins.then_inc(cT_ready, 1)
                pe.wait_ge(cT_kept, n + 1)
                spread(0)
                bottleneck(2)
                spread(1)
                bottleneck(3)
                spread(2)
                bottleneck(4)
                spread(3)
                pe.wait_ge(hm_ready, (n + 1) * M2)
                pe.wait_ge(gelu_ready, (n + 1) * (M2 + 1))
                for j in range(TB):
                    if j >= 2:
                        pe.wait_ge(y_gated, n * TB + j - 1)
                    else:
                        pe.wait_ge(y_gated, n * TB)
                    t = slice(j * P, (j + 1) * P)
                    for m in range(M2):
                        nc.tensor.matmul(psY[:, j % 2, 0:D], hm[:, m, t], wu[:, m, :], start=(m == 0), stop=False)
                    nc.tensor.matmul(psY[:, j % 2, 0:D], hs[:, t], wsu[:, :], start=False, stop=False)
                    nc.tensor.matmul(psY[:, j % 2, 0:D], cT[:, t], bu[:, :], start=False, stop=True).then_inc(y_ready, 1)


NH = 16
TAPS = 4
L, SB = 32, 8
NC, NSB = P // L, L // SB
NV = NC * NSB
KAPPA = 2.0 ** -64
SCALE = float(P) ** -0.5
RECTS = [(0, 2, 1, 7, 0), (2, 2, 3, 5, 14 * NH), (4, 2, 5, 3, 24 * NH), (6, 1, 7, 1, 30 * NH)]
NPAIR = 31 * NH


def kda_phase(nc, I, C, S, x_in, x_out):
    with ExitStack() as ctx:
        A = Alloc(nc, ctx, "kda")
        w_in = A.sb("w_in", [P, KD, NH, 4, P])
        w_g = A.sb("w_g", [P, KD, NH * P])
        w_b = A.sb("w_b", [P, KD, NH])
        w_o = A.sb("w_o", [P, NH, D])
        taps = A.sb("taps", [P, NH, 3, TAPS])
        cbias = A.sb("cbias", [P, NH, 3])
        abias = A.sb("abias", [P, NH])
        bbias = A.sb("bbias", [NH, 1])
        ln = A.sb("ln", [P, 2])
        m01 = A.sb("m01", [P, 2, P])
        hmask = A.sb("hmask", [P, NH])
        cmask = A.sb("cmask", [P, NH, SB])
        centre = A.sb("centre", [P, P])
        ones = A.sb("ones", [P, P])
        x_t = A.sb("x_t", [P, D])
        stats = A.sb("stats", [P, 6])
        mv = A.sb("mv", [P, 2])
        rstd = A.sb("rstd", [P, 1])
        xh = A.sb("xh", [P, D])
        hT = A.sb("hT", [P, KD, P])
        bT = A.sb("bT", [NH, P])
        raw = A.sb("raw", [P, 3, TAPS - 1 + P])
        hist = A.sb("hist", [P, NH, 3, TAPS - 1])
        yc = A.sb("yc", [P, 3, P])
        sv = A.sb("sv", [P, P])
        sa = A.sb("sa", [P, P])
        d01 = A.sb("d01", [P, 2, P])
        rr = A.sb("rr", [P, P])
        bv = A.sb("bv", [P, P])
        QK = A.sb("QK", [P, 2, NH, P])
        VT = A.sb("VT", [P, NH, P])
        DT = A.sb("DT", [P, NH, P])
        RI = A.sb("RI", [P, NH, P])
        F = A.sb("F", [P, NC, NH])
        frow = A.sb("frow", [NC * NH, P])
        fb = A.sb("fb", [P, NH, P])
        St = A.sb("St", [P, NH, P])
        FS = A.sb("FS", [P, NH, P])
        kk = [A.sb(f"kk{b}", [P, NPAIR]) for b in range(2)]
        H = [A.sb(f"H{b}", [P, NPAIR]) for b in range(2)]
        gk = [A.sb(f"gk{b}", [P, NH, L - SB]) for b in range(2)]
        gq = [A.sb(f"gq{b}", [P, NH, L]) for b in range(2)]
        E = A.sb("E", [P, 2, NH, SB])
        ks = A.sb("ks", [P, 2, NH, SB])
        EF = A.sb("EF", [P, NH, L])
        tmp = A.sb("tmp", [P, NH, SB])
        wt = [A.sb(f"wt{b}", [P, P]) for b in range(2)]
        ktok = A.sb("ktok", [P, 4, P])
        ws = A.sb("ws", [P, 4, P])
        sq = A.sb("sq", [P, NH * L])
        var = A.sb("var", [P, NH])
        dg = A.sb("dg", [P, 4, P])
        o_t = xh
        psX = A.ps("psX", [P, NH, L])
        psO = A.ps("psO", [P, NH, L])
        psS = [A.ps(f"psS{b}", [P, 4, P]) for b in range(2)]
        psG = A.ps("psG", [P, 512])
        psT = A.ps("psT", [P, 4, P])
        psA = A.ps("psA", [P, 4, P])
        psB = A.ps("psB", [P, 4, P])
        names = """loaded x_ready mv_ready rstd_ready xh_ready T_ready hT_ready ks_ready kc_ready b_ready bs_ready bT_ready
            in_ready raw_ready tap_ready a_ready conv_done silu_ready ia_ready d_ready beta_ready beta_used
            f_ready fT_ready frow_ready f_stored f_loaded fs_ready
            kk_ready kko_ready h_ready gk_ready gkm_ready gq_ready gqm_ready sk_ready sq_done x_next x_read e_done
            wt_ready wt_kept kt_ready kt_kept ws_ready ws_kept ef_ready su_ready s_part s_ready o_sum o_read
            g_ready gate_ready c_ready csq_ready v_ready ve_ready rs_ready c_kept dg_ready r_ready n_ready ng_ready n_gated y_ready
            x_done stored dve_step""".split()
        Z = {n: A.sem(n) for n in names}
        block = ctx.enter_context(nc.Block())
        NLOAD = 15
        ps_beta = [psB, psT]
        ps_gate = [psA[:, 0, :], psG[:, 0:P], psS[0][:, 0, :], psS[1][:, 0, :]]

        def cbank(c):
            return (psX, psO)[c % 2][:, :, :]

        def at_chunk(ap, c):
            return ap[:, :, c * L:(c + 1) * L]

        def at_sub(ap, v):
            return ap[:, :, v * SB:(v + 1) * SB]

        def rect(ap, r):
            _, n, _, m, off = r
            return ap[:, off:off + NH * n * m].rearrange("p (h t u) -> p h t u", h=NH, t=n)

        @block.sync
        def _(sp):
            for k in range(KD):
                sp.dma_start(w_in[:, k].rearrange("p h c n -> p (h c n)"), I["win"][k * P:(k + 1) * P, :]).then_inc(Z["loaded"], 16)
                sp.dma_start(w_g[:, k, :], I["wgT"][k * P:(k + 1) * P, :]).then_inc(Z["loaded"], 16)
            sp.dma_start(w_o[:, :, :], I["woT"].rearrange("(h p) n -> p h n", p=P)).then_inc(Z["loaded"], 16)
            sp.dma_start(w_b[:, :, :], I["wbT"].rearrange("(k p) n -> p k n", p=P)).then_inc(Z["loaded"], 16)
            for d, n in ((taps[:, :, :, :], "taps"), (cbias[:, :, :], "cbias"), (abias[:, :], "abias"), (bbias[:, :], "bbias"),
                         (ln[:, :], "kln"), (m01[:, :, :], "c_m01"), (hmask[:, :], "c_hmask"), (cmask[:, :, :], "c_cmask"),
                         (centre[:, :], "c_centre")):
                sp.dma_start(d, I[n]).then_inc(Z["loaded"], 16)
            with sp.Fori(0, NT) as t:
                sp.wait_ge(Z["x_done"], t)
                sp.dma_start(x_t[:, :], x_in[bass.ds(t * P, P), :]).then_inc(Z["x_ready"], 16)
                sp.wait_ge(Z["frow_ready"], t + 1)
                sp.dma_start(S["f_rows"][:, :], frow[:, :]).then_inc(Z["f_stored"], 16)
                sp.wait_ge(Z["f_stored"], (t + 1) * 16)
                for c in range(NC):
                    if c:
                        sp.wait_ge(Z["fs_ready"], t * NC + c)
                    sp.dma_start(fb[:, :, :].rearrange("p h i -> p (h i)"),
                                 S["f_rows"][c * NH:(c + 1) * NH, :].rearrange("(a h) i -> a (h i)", a=1).broadcast_to(
                                     [P, NH * P])).then_inc(Z["f_loaded"], 16)
                sp.wait_ge(Z["x_done"], t + 1)
                sp.dma_start(x_out[bass.ds(t * P, P), :], o_t[:, :]).then_inc(Z["stored"], 16)
            sp.wait_ge(Z["stored"], 16 * NT)

        @block.gpsimd
        def _(pool):
            pool.wait_ge(Z["loaded"], 16 * NLOAD)
            with pool.Fori(0, NT) as t:
                pool.wait_ge(Z["mv_ready"], t + 1)
                nc.gpsimd.tensor_tensor(rstd[:, :], mv[:, 1:2], C["nhalf"][:, 0:1], ALU.pow).then_inc(Z["rstd_ready"], 1)
                for h in range(NH):
                    pool.wait_ge(Z["ia_ready"], t * NH + h + 1)
                    nc.gpsimd.tensor_tensor(d01[:, :, :], bcast(sa[:, :], 1, 2), m01[:, :, :], ALU.mult).then_inc(Z["d_ready"], 1)
                pool.wait_ge(Z["silu_ready"], (t + 1) * NH)
                for v in range(NV):
                    pool.wait_ge(Z["kko_ready"], t * NV + max(v - 1, 0))
                    for t0, n, u0, m, off in RECTS:
                        k1 = QK[:, 1, :, v * SB + t0:v * SB + t0 + n]
                        k2 = QK[:, 1, :, v * SB + u0:v * SB + u0 + m]
                        ins = nc.gpsimd.tensor_tensor(rect(kk[v % 2], (t0, n, u0, m, off)), bcast(k1, 3, m), bcast(k2, 2, n), ALU.mult)
                    ins.then_inc(Z["kk_ready"], 1)
                    if v % NSB == 0:
                        c = v // NSB
                        pool.wait_ge(Z["f_loaded"], (t * NC + c + 1) * 16)
                        pool.wait_ge(Z["s_ready"], t * NC + c + 1)
                        nc.gpsimd.tensor_tensor(FS[:, :, :], St[:, :, :], fb[:, :, :], ALU.mult).then_inc(Z["fs_ready"], 1)
                pool.wait_ge(Z["ve_ready"], t + 1)
                nc.gpsimd.tensor_tensor(var[:, :], var[:, :], C["nhalf"][:, 0:NH], ALU.pow).then_inc(Z["rs_ready"], 1)
                for c in range(NC):
                    pool.wait_ge(Z["ng_ready"], t * NC + c + 1)
                    nc.gpsimd.tensor_tensor(at_chunk(VT, c), sq[:, :].rearrange("p (h t) -> p h t", h=NH), at_chunk(DT, c),
                                            ALU.mult).then_inc(Z["n_gated"], 1)

        @block.scalar
        def _(act):
            act.wait_ge(Z["loaded"], 16 * NLOAD)
            with act.Fori(0, NT) as t:
                act.wait_ge(Z["T_ready"], t + 1)
                for k in range(KD):
                    ins = nc.scalar.activation(hT[:, k, :], psB[:, k, :], ACT.Identity,
                                               bias=C["mod_col"][:, 1, 0, k:k + 1], scale=C["mod_col"][:, 1, 1, k:k + 1])
                ins.then_inc(Z["hT_ready"], 1)
                act.wait_ge(Z["b_ready"], t + 1)
                nc.scalar.activation(bT[:, :], psB[0:NH, 2, :], ACT.Sigmoid, bias=bbias[:, 0:1]).then_inc(Z["bs_ready"], 1)
                for h in range(NH):
                    n = t * NH + h
                    act.wait_ge(Z["in_ready"], n + 1)
                    act.wait_ge(Z["conv_done"], n)
                    act.wait_ge(Z["silu_ready"], n)
                    nc.scalar.activation(raw[:, :, TAPS - 1:], psA[:, 0:3, :], ACT.Copy).then_inc(Z["raw_ready"], 1)
                    for j in range(3):
                        ins = nc.scalar.activation(yc[:, j, :], psA[:, j, :], ACT.Identity, bias=cbias[:, h, j:j + 1],
                                                   scale=taps[:, h, j, TAPS - 1:TAPS])
                    ins.then_inc(Z["tap_ready"], 1)
                    act.wait_ge(Z["beta_used"], n)
                    nc.scalar.activation(sa[:, :], psA[:, 3, :], ACT.Sigmoid, bias=abias[:, h:h + 1]).then_inc(Z["a_ready"], 1)
                    act.wait_ge(Z["conv_done"], n + 1)
                    nc.scalar.activation(QK[:, :, h, :], yc[:, 0:2, :], ACT.Silu)
                    nc.scalar.activation(sv[:, :], yc[:, 2, :], ACT.Silu).then_inc(Z["silu_ready"], 1)
                act.wait_ge(Z["fT_ready"], t + 1)
                act.wait_ge(Z["f_stored"], t * 16)
                nc.scalar.activation(frow[:, :], psB[0:NC * NH, 3, :], ACT.Copy).then_inc(Z["frow_ready"], 1)
                nc.scalar.activation(ks[:, 0], QK[:, 1, :, 0:SB], ACT.Copy).then_inc(Z["ks_ready"], 1)
                for v in range(NV):
                    c, s = v // NSB, v % NSB
                    if s == 0:
                        act.wait_ge(Z["ws_ready"], t * NC + c)
                        nc.scalar.activation(EF[:, :, :], QK[:, 1, :, c * L:(c + 1) * L], ACT.Copy).then_inc(Z["kc_ready"], 1)
                        act.wait_ge(Z["kt_ready"], t * NC + c + 1)
                        nc.scalar.activation(ktok[:, :, :], psT[:, :, :], ACT.Copy).then_inc(Z["kt_kept"], 1)
                    act.wait_ge(Z["wt_ready"], t * NV + v + 1)
                    nc.scalar.activation(wt[v % 2][:, :], psT[:, 0, :], ACT.Copy).then_inc(Z["wt_kept"], 1)
                    if v < NV - 1:
                        act.wait_ge(Z["gq_ready"], t * NV + v)
                        nc.scalar.activation(ks[:, (v + 1) % 2], QK[:, 1, :, (v + 1) * SB:(v + 2) * SB],
                                             ACT.Copy).then_inc(Z["ks_ready"], 1)
                    if s == NSB - 1:
                        act.wait_ge(Z["ws_ready"], t * NC + c + 1)
                        nc.scalar.activation(ws[:, :, :], psT[:, :, :], ACT.Copy).then_inc(Z["ws_kept"], 1)
                for h in range(NH):
                    act.wait_ge(Z["g_ready"], t * NH + h + 1)
                    nc.scalar.activation(DT[:, h, :], ps_gate[h % 4], ACT.Sigmoid).then_inc(Z["gate_ready"], 1)
                for c in range(NC):
                    act.wait_ge(Z["c_ready"], t * NC + c + 1)
                    act.wait_ge(Z["v_ready"], t * NC + c)
                    nc.scalar.activation(sq[:, :].rearrange("p (h t) -> p h t", h=NH), cbank(c), ACT.Square).then_inc(Z["csq_ready"], 1)
                act.wait_ge(Z["v_ready"], (t + 1) * NC)
                for c in range(NC):
                    act.wait_ge(Z["n_ready"], t * NC + c + 1)
                    act.wait_ge(Z["n_gated"], t * NC + c)
                    nc.scalar.activation(sq[:, :].rearrange("p (h t) -> p h t", h=NH), at_chunk(VT, c), ACT.Identity, bias=ln[:, 1:2], scale=ln[:, 0:1]).then_inc(Z["ng_ready"], 1)

        @block.vector
        def _(dve):
            dve.wait_ge(Z["loaded"], 16 * NLOAD)
            nc.vector.memset(hist[:, :, :, :], 0.0)
            nc.vector.memset(ones[:, :], 1.0).then_inc(Z["dve_step"], 1)
            nc.vector.memset(St[:, :, :], 0.0).then_inc(Z["s_ready"], 1)
            dve.wait_ge(Z["s_ready"], 1)
            PER = 2 + NH * 12 + NV * (1 + 13) + 1
            with dve.Fori(0, NT) as t:
                ch = Chain(dve, Z["dve_step"], 1 + t * PER)
                dve.wait_ge(Z["x_ready"], (t + 1) * 16)
                ch.done_before(nc.vector.bn_stats(stats[:, :], x_t[:, :]), C["pad"])
                ch.done(nc.vector.bn_aggr(mv[:, :], stats[:, :]))
                nc.vector.tensor_scalar(mv[:, 1:2], mv[:, 1:2], EPS, None, ALU.add).then_inc(Z["mv_ready"], 1)
                dve.wait_ge(Z["rstd_ready"], t + 1)
                dve.wait_ge(Z["stored"], 16 * t)
                nc.vector.tensor_scalar(xh[:, :], x_t[:, :], mv[:, 0:1], rstd[:, 0:1], ALU.subtract,
                                        ALU.mult).then_inc(Z["xh_ready"], 1)
                dve.wait_ge(Z["bs_ready"], t + 1)
                nc.vector.tensor_scalar(bT[:, :], bT[:, :], SCALE * SCALE, None, ALU.mult).then_inc(Z["bT_ready"], 1)
                for h in range(NH):
                    n = t * NH + h
                    dve.wait_ge(Z["raw_ready"], n + 1)
                    ch.done(nc.vector.tensor_copy(raw[:, :, 0:TAPS - 1], hist[:, h, :, :]))
                    nc.vector.tensor_copy(hist[:, h, :, :], raw[:, :, P:])
                    dve.wait_ge(Z["tap_ready"], n + 1)
                    first = ch.n
                    for m in range(TAPS - 1):
                        for j in range(3):
                            if m:
                                ch.wait(first + 3 * (m - 1) + j + 1)
                            ins = nc.vector.scalar_tensor_tensor(out=yc[:, j, :], in0=raw[:, j, m:m + P],
                                                                 scalar=taps[:, h, j, m:m + 1], in1=yc[:, j, :],
                                                                 op0=ALU.mult, op1=ALU.add)
                            if m == TAPS - 2 and j == 2:
                                ins.then_inc(Z["conv_done"], 1)
                            else:
                                ch.mark(ins)
                    dve.wait_ge(Z["a_ready"], n + 1)
                    nc.vector.reciprocal(sa[:, :], sa[:, :]).then_inc(Z["ia_ready"], 1)
                    dve.wait_ge(Z["d_ready"], n + 1)
                    ch.done(nc.vector.tensor_tensor_scan(rr[:, :], d01[:, 0, :], d01[:, 1, :], 0.0, ALU.mult, ALU.add))
                    nc.vector.reciprocal(RI[:, h, :], rr[:, :])
                    dve.wait_ge(Z["beta_ready"], n + 1)
                    nc.vector.tensor_tensor(DT[:, h, :], ps_beta[h % 2][:, 0, :], sa[:, :], ALU.mult)
                    dve.wait_ge(Z["silu_ready"], n + 1)
                    ch.done(nc.vector.tensor_tensor(bv[:, :], ps_beta[h % 2][:, 0, :], sv[:, :], ALU.mult))
                    ch.mark(nc.vector.tensor_tensor(VT[:, h, :], bv[:, :], rr[:, :], ALU.mult))
                    nc.vector.tensor_copy(C["pad"][:, 1:2], C["pad"][:, 0:1]).then_inc(Z["beta_used"], 1)
                ch.wait(ch.n)
                dve.wait_ge(Z["beta_used"], (t + 1) * NH)
                nc.vector.tensor_scalar(F[:, :, :], RI[:, :, L - 1::L].rearrange("p h c -> p c h"), KAPPA, None,
                                        ALU.mult).then_inc(Z["f_ready"], 1)
                dve.wait_ge(Z["f_ready"], t + 1)

                def pairs(v):
                    dve.wait_ge(Z["kko_ready"], t * NV + v + 1)
                    for r in RECTS:
                        t0, n, u0, m, off = r
                        ins = nc.vector.tensor_tensor(rect(H[v % 2], r), rect(psA[:, :, :].rearrange("p a b -> p (a b)"), r),
                                                      bcast(DT[:, :, v * SB + u0:v * SB + u0 + m], 2, n), ALU.mult)
                    ins.then_inc(Z["h_ready"], 1)

                pairs(0)
                for v in range(NV):
                    c, s = v // NSB, v % NSB
                    G = t * NC + c
                    if s == 0:
                        dve.wait_ge(Z["sk_ready"], G + 1)
                    else:
                        dve.wait_ge(Z["x_next"], G * (NSB - 1) + s)
                    Ev = E[:, v % 2]
                    nc.vector.tensor_tensor(tmp[:, :, :], at_sub(psX, s), at_sub(DT, v), ALU.mult).then_inc(Z["x_read"], 1)
                    dve.wait_ge(Z["x_read"], t * NV + v + 1)
                    ch.mark(nc.vector.tensor_tensor(Ev, at_sub(VT, v), tmp[:, :, :], ALU.subtract))
                    if s < NSB - 1:
                        dve.wait_ge(Z["gk_ready"], G * (NSB - 1) + s + 1)
                        nc.vector.tensor_tensor(gk[v % 2][:, :, 0:(NSB - 1 - s) * SB],
                                                psG[:, 0:NH * (NSB - 1 - s) * SB].rearrange("p (h t) -> p h t", h=NH),
                                                bcast(hmask[:, :], 2, (NSB - 1 - s) * SB), ALU.mult).then_inc(Z["gkm_ready"], 1)
                    ch.wait(ch.n)
                    dve.wait_ge(Z["h_ready"], t * NV + v + 1)
                    for k in range(SB - 1):
                        r = RECTS[k // 2]
                        h_k = rect(H[v % 2], r)[:, :, k - r[0], k + 1 - r[2]:]
                        m = SB - 1 - k
                        ch.done(nc.vector.tensor_tensor(tmp[:, :, 0:m], bcast(Ev[:, :, k], 2, m), h_k, ALU.mult))
                        ins = nc.vector.tensor_tensor(Ev[:, :, k + 1:], Ev[:, :, k + 1:], tmp[:, :, 0:m], ALU.subtract)
                        if k < SB - 2:
                            ch.done(ins)
                    ins.then_inc(Z["e_done"], 1)
                    dve.wait_ge(Z["e_done"], t * NV + v + 1)
                    if s == 0:
                        dve.wait_ge(Z["kt_ready"], G + 1)
                    nc.vector.tensor_tensor(EF[:, :, s * SB:(s + 1) * SB], Ev, bcast(F[:, c, :], 2, SB), ALU.mult).then_inc(Z["ef_ready"], 1)
                    n = (NSB - s) * SB
                    dve.wait_ge(Z["gq_ready"], t * NV + v + 1)
                    g3 = psG[:, 0:NH * n].rearrange("p (h t) -> p h t", h=NH)
                    ins = nc.vector.tensor_tensor(gq[v % 2][:, :, 0:SB], g3[:, :, 0:SB], cmask[:, :, :], ALU.mult)
                    if n > SB:
                        ins = nc.vector.tensor_tensor(gq[v % 2][:, :, SB:n], g3[:, :, SB:], bcast(hmask[:, :], 2, n - SB), ALU.mult)
                    ins.then_inc(Z["gqm_ready"], 1)
                    if v < NV - 1:
                        pairs(v + 1)
                    if s == NSB - 1:
                        dve.wait_ge(Z["fs_ready"], G + 1)
                        for r in range(4):
                            dve.wait_ge(Z["su_ready"], G * 4 + r + 1)
                            ins = nc.vector.tensor_tensor(St[:, r::4, :], psS[r % 2][:, :, :], FS[:, r::4, :], ALU.add)
                            if r < 3:
                                ins.then_inc(Z["s_part"], 1)
                        ins.then_inc(Z["s_ready"], 1)
                        dve.wait_ge(Z["o_sum"], G + 1)
                        nc.vector.scalar_tensor_tensor(out=at_chunk(VT, c), in0=psO[:, :, :], scalar=1.0 / SCALE,
                                                       in1=at_chunk(RI, c), op0=ALU.mult, op1=ALU.mult).then_inc(Z["o_read"], 1)
                for c in range(NC):
                    dve.wait_ge(Z["csq_ready"], t * NC + c + 1)
                    nc.vector.tensor_copy(at_chunk(VT, c), cbank(c)).then_inc(Z["c_kept"], 1)
                dve.wait_ge(Z["v_ready"], (t + 1) * NC)
                nc.vector.tensor_scalar(var[:, :], psG[:, 0:NH], 1.0 / P, EPS, ALU.mult, ALU.add).then_inc(Z["ve_ready"], 1)
                dve.wait_ge(Z["rs_ready"], t + 1)
                for c in range(NC):
                    if c:
                        dve.wait_ge(Z["r_ready"], t * NC + c)
                    nc.vector.tensor_tensor(dg[:, :, :], bcast(C["ident"][:, :], 1, 4), bcast(var[:, 4 * c:4 * c + 4], 2, P),
                                            ALU.mult).then_inc(Z["dg_ready"], 1)
                    dve.wait_ge(Z["r_ready"], t * NC + c + 1)
                    nc.vector.tensor_tensor(at_chunk(VT, c), at_chunk(VT, c), cbank(c), ALU.mult).then_inc(Z["n_ready"], 1)
                dve.wait_ge(Z["y_ready"], t + 1)
                ch.done(nc.vector.tensor_tensor(o_t[:, :], psB[:, 0:2, :].rearrange("p a b -> p (a b)"), C["gate_row"][:, 1, 0, :], ALU.mult))
                nc.vector.tensor_tensor(o_t[:, :], o_t[:, :], x_t[:, :], ALU.add).then_inc(Z["x_done"], 1)
                assert ch.n == PER, (ch.n, PER)

        @block.tensor
        def _(pe):
            pe.wait_ge(Z["loaded"], 16 * NLOAD)
            pe.wait_ge(Z["dve_step"], 1)
            with pe.Fori(0, NT) as t:
                pe.wait_ge(Z["x_done"], t)
                pe.wait_ge(Z["xh_ready"], t + 1)
                for k in range(KD):
                    ins = nc.tensor.matmul(psB[:, k, :], xh[:, k * P:(k + 1) * P], C["ident"][:, :], start=True, stop=True)
                ins.then_inc(Z["T_ready"], 1)
                pe.wait_ge(Z["hT_ready"], t + 1)
                for k in range(KD):
                    ins = nc.tensor.matmul(psB[0:NH, 2, :], w_b[:, k, :], hT[:, k, :], start=(k == 0), stop=(k == KD - 1))
                ins.then_inc(Z["b_ready"], 1)
                pe.wait_ge(Z["bT_ready"], t + 1)
                for h in range(NH):
                    n = t * NH + h
                    pe.wait_ge(Z["a_ready"], n)
                    for j in range(4):
                        for k in range(KD):
                            ins = nc.tensor.matmul(psA[:, j, :], w_in[:, k, h, j, :], hT[:, k, :], start=(k == 0), stop=(k == KD - 1))
                    ins.then_inc(Z["in_ready"], 1)
                    pe.wait_ge(Z["beta_used"], t * NH + max(h - 1, 0))
                    nc.tensor.matmul(ps_beta[h % 2][:, 0, :], C["ident"][0:NH, h:h + 1].broadcast_to([NH, P]), bT[:, :],
                                     start=True, stop=True).then_inc(Z["beta_ready"], 1)
                pe.wait_ge(Z["f_ready"], t + 1)
                nc.tensor.matmul(psB[0:NC * NH, 3, :], F[:, :, :], C["ident"][:, :], start=True, stop=True).then_inc(Z["fT_ready"], 1)

                def spread(v):
                    pe.wait_ge(Z["kk_ready"], t * NV + v + 1)
                    pe.wait_ge(Z["h_ready"], t * NV + v)
                    nc.tensor.matmul(psA[:, :, :].rearrange("p a b -> p (a b)")[:, 0:NPAIR], ones[:, :], kk[v % 2][:, :],
                                     start=True, stop=True).then_inc(Z["kko_ready"], 1)

                spread(0)
                for v in range(NV):
                    c, s = v // NSB, v % NSB
                    G = t * NC + c
                    if s == 0:
                        pe.wait_ge(Z["s_ready"], G + 1)
                        for h in range(NH):
                            ins = nc.tensor.matmul(psX[:, h, :], St[:, h, :], QK[:, 1, h, c * L:(c + 1) * L], start=(h == 0),
                                                   stop=True, skip_group_check=True)
                        ins.then_inc(Z["sk_ready"], 1)
                        pe.wait_ge(Z["o_read"], G)
                        for h in range(NH):
                            ins = nc.tensor.matmul(psO[:, h, :], St[:, h, :], QK[:, 0, h, c * L:(c + 1) * L], start=(h == 0),
                                                   stop=True, skip_group_check=True)
                    pe.wait_ge(Z["ks_ready"], t * NV + v + 1)
                    keys = ks[:, v % 2].rearrange("p h t -> p (h t)")
                    if s < NSB - 1:
                        pe.wait_ge(Z["gqm_ready"], t * NV + v)
                        nc.tensor.matmul(psG[:, 0:NH * (NSB - 1 - s) * SB], keys, QK[:, 1, :, (v + 1) * SB:(c + 1) * L],
                                         start=True, stop=True).then_inc(Z["gk_ready"], 1)
                        pe.wait_ge(Z["gkm_ready"], G * (NSB - 1) + s + 1)
                    else:
                        pe.wait_ge(Z["gqm_ready"], t * NV + v)
                    nc.tensor.matmul(psG[:, 0:NH * (NSB - s) * SB], keys, QK[:, 0, :, v * SB:(c + 1) * L],
                                     start=True, stop=True).then_inc(Z["gq_ready"], 1)
                    if s == 0:
                        pe.wait_ge(Z["ws_kept"], G)
                        pe.wait_ge(Z["kc_ready"], G + 1)
                        for q in range(4):
                            ins = nc.tensor.matmul(psT[:, q, :], EF[:, 4 * q:4 * q + 4, :], C["ident"][:, :],
                                                   start=True, stop=True)
                        ins.then_inc(Z["kt_ready"], 1)
                        pe.wait_ge(Z["kt_kept"], G + 1)
                    if v < NV - 1:
                        spread(v + 1)
                    pe.wait_ge(Z["e_done"], t * NV + v + 1)
                    if s:
                        pe.wait_ge(Z["wt_kept"], t * NV + v)
                    nc.tensor.matmul(psT[:, 0, :], E[:, v % 2].rearrange("p h t -> p (h t)"), C["ident"][:, :], start=True,
                                     stop=True).then_inc(Z["wt_ready"], 1)
                    pe.wait_ge(Z["wt_kept"], t * NV + v + 1)
                    if s < NSB - 1:
                        nc.tensor.matmul(psX[:, :, (s + 1) * SB:(s + 2) * SB], wt[v % 2][:, :], gk[v % 2][:, :, 0:SB], start=False,
                                         stop=True, skip_group_check=True).then_inc(Z["x_next"], 1)
                        if s < NSB - 2:
                            pe.wait_ge(Z["x_read"], t * NV + v + 2)
                            nc.tensor.matmul(psX[:, :, (s + 2) * SB:], wt[v % 2][:, :], gk[v % 2][:, :, SB:(NSB - 1 - s) * SB],
                                             start=False, stop=True, skip_group_check=True)
                    else:
                        pe.wait_ge(Z["ef_ready"], t * NV + v + 1)
                        for q in range(4):
                            ins = nc.tensor.matmul(psT[:, q, :], EF[:, 4 * q:4 * q + 4, :], C["ident"][:, :], start=True, stop=True)
                        ins.then_inc(Z["ws_ready"], 1)
                        pe.wait_ge(Z["ws_kept"], G + 1)
                        for r in range(4):
                            if r >= 2:
                                pe.wait_ge(Z["s_part"], G * 3 + r - 1)
                            for q in range(4):
                                ins = nc.tensor.matmul(psS[r % 2][:, q, :], ktok[32 * r:32 * r + 32, q, :],
                                                       ws[32 * r:32 * r + 32, q, :], start=True, stop=True)
                            ins.then_inc(Z["su_ready"], 1)
                    pe.wait_ge(Z["gqm_ready"], t * NV + v + 1)
                    ins = nc.tensor.matmul(psO[:, :, s * SB:], wt[v % 2][:, :], gq[v % 2][:, :, 0:(NSB - s) * SB], start=False,
                                           stop=True, skip_group_check=True)
                    if s == NSB - 1:
                        ins.then_inc(Z["o_sum"], 1)
                pe.wait_ge(Z["o_read"], (t + 1) * NC)
                for h in range(NH):
                    pe.wait_ge(Z["gate_ready"], t * NH + max(h - 3, 0))
                    for k in range(KD):
                        ins = nc.tensor.matmul(ps_gate[h % 4], w_g[:, k, h * P:(h + 1) * P], hT[:, k, :], start=(k == 0), stop=(k == KD - 1))
                    ins.then_inc(Z["g_ready"], 1)
                for c in range(NC):
                    if c >= 2:
                        pe.wait_ge(Z["c_kept"], t * NC + c - 1)
                    nc.tensor.matmul(cbank(c), centre[:, :], at_chunk(VT, c), start=True, stop=True).then_inc(Z["c_ready"], 1)
                    pe.wait_ge(Z["csq_ready"], t * NC + c + 1)
                    for q in range(4):
                        ins = nc.tensor.matmul(psG[:, 4 * c + q:4 * c + q + 1], sq[:, q * P:(q + 1) * P], ones[:, 0:1],
                                               start=True, stop=True)
                    ins.then_inc(Z["v_ready"], 1)
                pe.wait_ge(Z["c_kept"], (t + 1) * NC)
                for c in range(NC):
                    pe.wait_ge(Z["dg_ready"], t * NC + c + 1)
                    nc.tensor.matmul(cbank(c), ones[:, :], dg[:, :, :].rearrange("p a b -> p (a b)"), start=True,
                                     stop=True).then_inc(Z["r_ready"], 1)
                pe.wait_ge(Z["n_gated"], (t + 1) * NC)
                for h in range(NH):
                    ins = nc.tensor.matmul(psB[:, 0:2, :], VT[:, h, :], w_o[:, h, :], start=(h == 0), stop=(h == NH - 1))
                ins.then_inc(Z["y_ready"], 1)


def ttt_layer(nc, I, C, x_in, x_out):
    with ExitStack() as ctx:
        B = Alloc(nc, ctx, "ttt")
        S = {"XKT": B.sb("XKT", [P, KD, T]), "XQT": B.sb("XQT", [P, KD, T]),
             "cA": B.sb("cA", [P, NMB, 32]), "lA": B.sb("lA", [P, NMB, HR]),
             "GA": B.sb("GA", [P, NMB, 32]), "Wt": B.sb("Wt", [P, NT, KD + 1, 32]),
             "tok": B.sb("tok", [P, MB]),
             "g_dram": nc.dram_tensor("g_tok", [T, D], F32, kind="Internal").ap(),
             "c_tok": nc.dram_tensor("c_tok", [T, D + TH], F32, kind="Internal").ap()}
        ttt_project_phase(nc, I, C, S)
        ttt_scan_phase(nc, I, C, S)
        ttt_output_phase(nc, I, C, S, x_in, x_out)


def moe1_layer(nc, I, C, x_in, x_out):
    with ExitStack() as ctx:
        B = Alloc(nc, ctx, "moe1")
        S = {"hT": B.sb("hT", [P, KD, T]), "dwT": nc.dram_tensor("dwT", [E1S, T], F32, kind="Internal").ap()}
        moe1_route_phase(nc, I, C, S, x_in)
        moe1_expert_phase(nc, I, C, S, x_in, x_out)


def build(nc, I, out):
    with ExitStack() as ctx:
        A = Alloc(nc, ctx, "g")
        C = {"ident": A.sb("ident", [P, P]), "nhalf": A.sb("nhalf", [P, TH]), "pad": A.sb("pad", [P, 2]),
             "mod_col": A.sb("mod_col", [P, 2, 4, KD]), "gate_row": A.sb("gate_row", [P, 2, 2, D])}
        X = [nc.dram_tensor(f"x_stage{n}", [T, D], F32, kind="Internal").ap() for n in range(3)]
        setup_phase(nc, I, C)
        ttt_layer(nc, I, C, I["x"], X[0])
        moe1_layer(nc, I, C, X[0], X[1])
        kda_phase(nc, I, C, {"f_rows": nc.dram_tensor("f_rows", [NC * NH, P], F32, kind="Internal").ap()}, X[1], X[2])
        moe2_phase(nc, I, C, X[2], out)


def layout(i):
    f = {k: np.asarray(v) for k, v in i.items()}
    o = {"x": f["L0_attn_hidden_states"].reshape(T, D), "c_ident": np.eye(P, dtype=np.float32)}
    for l in range(2):
        o[f"wmod{l}"] = f[f"L{l}_wmod"]
        o[f"c{l}"] = f[f"L{l}_c"].reshape(KD, P).T
    o["qwT"], o["kwT"], o["vwT"] = (f[f"L0_attn_{n}_w"].T for n in "qkv")
    o["lrwT"] = f["L0_attn_ttt_lr_weight"].reshape(TH, D).T
    o["lrb"] = f["L0_attn_ttt_lr_bias"].reshape(1, TH)
    o["ttt_w"] = f["L0_attn_ttt_norm_weight"].reshape(1, D)
    o["ttt_b"] = f["L0_attn_ttt_norm_bias"].reshape(1, D)
    row = np.arange(P)
    w1 = f["L0_attn_W1"].reshape(KD, HR, HR, HD, HD)
    bd = np.zeros((HR, HR, HD, KD, HR, HD), np.float32)
    for r in range(HR):
        bd[:, r, :, :, r, :] = w1[:, :, r].transpose(1, 2, 0, 3)
    o["W1bd"] = bd.reshape(P, KD, 32)
    o["b1A"] = np.repeat(f["L0_attn_b1"].reshape(HG, 1, 32), MB, 1).reshape(P, 32)
    o["ttt_wA"] = np.repeat(f["L0_attn_ttt_norm_weight"].reshape(HG, 1, 32), MB, 1).reshape(P, 32)
    o["tokidx"] = f["L0_attn_learnable_token_idx"].reshape(1, MB)
    o["c_recip"] = (1.0 / np.arange(1, MB + 1, dtype=np.float32)).reshape(1, MB)
    o["c_gmask"] = (row[:, None] // 32 == np.arange(HR)).astype(np.float32)
    rmask = np.ones((P, KD + 1, HR), np.float32)
    rmask[:, :KD] = (row[:, None] // HD % HR == np.arange(HR))[:, None]
    o["c_rmask"] = rmask
    o["c_first"] = ((row[:, None] // MB == row // MB) & (row[:, None] % MB == 0)).astype(np.float32)
    o["c_same"] = (row[:, None] // MB == row // MB).astype(np.float32)
    o["owT"] = f["L0_attn_o_w"].T
    o["post"] = np.stack([f[f"L0_attn_post_norm_{n}"].reshape(KD, P).T for n in ("weight", "bias")], 1)
    o["c_brow"] = (row[:, None] // MB == np.arange(HG)).astype(np.float32)
    o["c_pick"] = np.repeat((row[:, None] % MB == 0).astype(np.float32), P, 1)
    o["c_causal"] = ((row[:, None] // MB == row // MB) & (row[:, None] <= row)).astype(np.float32)
    o["c_prev"] = (row[:, None] // MB < row // MB).astype(np.float32)
    wide = lambda a: a.reshape(D, 2, I1).transpose(1, 0, 2)
    gate = np.concatenate([f["L0_ffn_w_gate"], wide(f["L0_ffn_ws_gate"])])
    up = np.concatenate([f["L0_ffn_w_up"], wide(f["L0_ffn_ws_up"])])
    down = np.concatenate([f["L0_ffn_w_down"], f["L0_ffn_ws_down"].reshape(2, I1, D)])
    gu = np.concatenate([gate, up], 2).reshape(E1S, KD, P, D).transpose(0, 2, 1, 3).reshape(E1S, P, KD * D)
    o["w1"] = np.concatenate([gu, down], 2)
    o["gate1T"] = f["L0_ffn_gate_weight"].T
    o["gate2T"], o["wdT"] = f["L1_ffn_gate_w"].T, f["L1_ffn_wd"].reshape(E2 * BOT, D).T
    o["wsdT"], o["wsuT"] = f["L1_ffn_ws_d"].T, f["L1_ffn_ws_u"].T
    o["wuT"] = f["L1_ffn_wu"].transpose(0, 2, 1).reshape(E2 * BOT, D)
    o["bd"] = f["L1_ffn_bd"].reshape(M2, P).T
    o["bsd"] = f["L1_ffn_bs_d"].reshape(BOT, 1)
    o["bu"] = np.concatenate([f["L1_ffn_bu"], f["L1_ffn_bs_u"].reshape(1, D)])
    o["c_sel"] = (np.arange(E2 + 1)[:, None] == np.arange(E2 * BOT) // BOT).astype(np.float32).reshape(E2 + 1, M2, P)
    e = np.arange(E2)
    o["c_tri"] = (e[:, None] > e).astype(np.float32).reshape(1, E2 * E2)
    win = np.stack([f[f"L1_attn_W{n}"].reshape(NH, P, D) for n in "qkva"], 1)
    o["win"] = win.transpose(3, 0, 1, 2).reshape(D, NH * 4 * P)
    o["wgT"], o["wbT"], o["woT"] = f["L1_attn_Wg"].T, f["L1_attn_Wb"].T, f["L1_attn_Wo"].T
    o["taps"] = np.stack([f[f"L1_attn_{n}c_w"].reshape(NH, P, TAPS) for n in "qkv"], 2).transpose(1, 0, 2, 3)
    o["cbias"] = np.stack([f[f"L1_attn_{n}c_b"].reshape(NH, P) for n in "qkv"], 2).transpose(1, 0, 2)
    o["abias"], o["bbias"] = f["L1_attn_ba"].reshape(NH, P).T, f["L1_attn_bb"].reshape(NH, 1)
    o["kln"] = np.stack([f["L1_attn_ln_g"], f["L1_attn_ln_b"]], 1)
    begin = np.arange(P) % L == 0
    o["c_m01"] = np.repeat(np.stack([~begin, begin * KAPPA]).astype(np.float32)[None], P, 0)
    o["c_hmask"] = (row[:, None] // SB == np.arange(NH)).astype(np.float32)
    o["c_cmask"] = (o["c_hmask"][:, :, None] * (row[:, None, None] % SB <= np.arange(SB))).astype(np.float32)
    o["c_centre"] = (np.eye(P) - 1.0 / P).astype(np.float32)
    return {k: np.ascontiguousarray(v) for k, v in o.items()}


def kernel(**inputs):
    import concourse.bacc as _bacc
    from concourse.bass_utils import run_bass_kernel_spmd as _run

    nc = _bacc.Bacc("TRN2", target_bir_lowering=False, num_devices=1)
    arrays, aps = {}, {}
    for name, a in layout(inputs).items():
        arrays[f"in_{name}"] = a
        aps[name] = nc.dram_tensor(f"in_{name}", a.shape, mybir.dt.from_np(a.dtype), kind="ExternalInput").ap()
    out = nc.dram_tensor("out", [T, D], F32, kind="ExternalOutput").ap()
    build(nc, aps, out)
    r = _run(nc, [arrays], core_ids=[0])
    return r.results[0]["out"].reshape(1, T, D)
```

```python
from contextlib import ExitStack

import numpy as np

import concourse.bass as bass
from concourse import mybir

F32 = mybir.dt.float32
ALU = mybir.AluOpType
ACT = mybir.ActivationFunctionType
AX_X = mybir.AxisListType.X

P = 128
T = 2048
D = 256
KD = D // P
NT = T // P
MB = 16
NMB = T // MB
TH, HD = 32, 8
HG, HR = 8, 4
EPS = 1e-5
TTT_EPS = 1e-6


class Chain:

    def __init__(self, eng, sem, base=0):
        self.eng, self.sem, self.base, self.n = eng, sem, base, 0

    def mark(self, ins):
        self.n += 1
        ins.then_inc(self.sem, 1)
        return self.n

    def wait(self, n):
        self.eng.wait_ge(self.sem, self.base + n)

    def done(self, ins):
        self.wait(self.mark(ins))

    def done_before(self, ins, pad):
        self.done(ins)
        self.eng.tensor_copy(pad[:, 1:2], pad[:, 0:1])


class Alloc:

    def __init__(self, nc, ctx, phase):
        self.nc, self.ctx, self.phase, self.sems = nc, ctx, phase, []
        ctx.callback(self.release)

    def release(self):
        if self.sems:
            self.nc.clear_and_free_semaphores(self.sems)
            self.nc.all_engine_barrier()

    def sb(self, name, shape):
        return self.ctx.enter_context(self.nc.sbuf_tensor(f"{self.phase}_{name}", shape, F32))

    def ps(self, name, shape):
        return self.ctx.enter_context(self.nc.psum_tensor(f"{self.phase}_{name}", shape, F32))

    def sem(self, name):
        self.sems.append(self.nc.alloc_semaphore(name=f"{self.phase}_{name}"))
        return self.sems[-1]


def bcast(ap, axis, n):
    shape = list(ap.shape)
    return ap.unsqueeze(axis).broadcast_to(shape[:axis] + [n] + shape[axis:])


def setup_phase(nc, I, C):
    with ExitStack() as ctx:
        A = Alloc(nc, ctx, "setup")
        wmod = A.sb("wmod", [P, 2, KD, 6 * D])
        cond = A.sb("cond", [P, 2, KD])
        sig = A.sb("sig", [P, 2, KD])
        sc = A.sb("sc", [P, 2, KD])
        scb = A.sb("scb", [P, 2, KD, P])
        sgn = A.sb("sgn", [P, 4, D])
        ones = A.sb("ones", [P, P])
        ps_col = A.ps("ps_col", [P, 512])
        ps_row = [A.ps(f"ps_row{i}", [P, 512]) for i in range(2)]
        loaded = A.sem("loaded")
        sig_ready = A.sem("sig_ready")
        silu_ready = A.sem("silu_ready")
        col_ready = A.sem("col_ready")
        row_ready = A.sem("row_ready")
        dve_step = A.sem("dve_step")
        block = ctx.enter_context(nc.Block())

        @block.sync
        def _(sp):
            for l in range(2):
                sp.dma_start(wmod[:, l], I[f"wmod{l}"].rearrange("(k p) n -> p k n", p=P)).then_inc(loaded, 16)
                sp.dma_start(cond[:, l], I[f"c{l}"]).then_inc(loaded, 16)
            sp.dma_start(C["ident"][:, :], I["c_ident"]).then_inc(loaded, 16)
            sp.wait_ge(loaded, 80)

        @block.scalar
        def _(act):
            act.wait_ge(loaded, 80)
            nc.scalar.activation(sig[:, :, :], cond[:, :, :], ACT.Sigmoid).then_inc(sig_ready, 1)

        @block.vector
        def _(dve):
            ch = Chain(dve, dve_step)
            nc.vector.memset(C["nhalf"][:, :], -0.5)
            nc.vector.memset(C["pad"][:, :], 0.0)
            ch.done(nc.vector.memset(ones[:, :], 1.0))
            dve.wait_ge(sig_ready, 1)
            ch.done(nc.vector.tensor_tensor(sc[:, :, :], cond[:, :, :], sig[:, :, :], ALU.mult))
            for l in range(2):
                for k in range(KD):
                    ins = nc.vector.tensor_scalar(scb[:, l, k, :], ones[:, :], sc[:, l, k:k + 1], None, ALU.mult)
            ins.then_inc(silu_ready, 1)
            dve.wait_ge(col_ready, 1)
            ch.done(nc.vector.tensor_copy(C["mod_col"][:, :, :, :], ps_col[:, 0:16].rearrange(
                "p (l m k) -> p l m k", l=2, m=4)))
            for m in (1, 3):
                last = nc.vector.tensor_scalar(C["mod_col"][:, :, m, :], C["mod_col"][:, :, m, :], 1.0, None, ALU.add)
            for l in range(2):
                dve.wait_ge(row_ready, l + 1)
                g = ps_row[l][:, :].rearrange("p (m n) -> p m n", m=2)
                s = sgn[:, 2 * l:2 * l + 2, :]
                out = C["gate_row"][:, l, :, :]
                ch.done(nc.vector.tensor_scalar(s, g, 0.0, 2.0, ALU.is_ge, ALU.mult))
                ch.done(nc.vector.tensor_scalar(s, s, -1.0, None, ALU.add))
                ch.done(nc.vector.tensor_tensor(out, g, s, ALU.mult))
                ch.done(nc.vector.scalar_tensor_tensor(out=out, in0=out, scalar=0.25, in1=s,
                                                       op0=ALU.max, op1=ALU.mult))

        @block.tensor
        def _(pe):
            pe.wait_ge(loaded, 80)
            pe.wait_ge(silu_ready, 1)
            for l in range(2):
                for m, at in enumerate((0, 1, 3, 4)):
                    for a in range(KD):
                        n = (l * 4 + m) * KD + a
                        for k in range(KD):
                            ins = nc.tensor.matmul(ps_col[:, n:n + 1], wmod[:, l, k, at * D + a * P:at * D + a * P + P],
                                                   sc[:, l, k:k + 1], start=(k == 0), stop=(k == KD - 1))
            ins.then_inc(col_ready, 1)
            for l in range(2):
                for m, at in enumerate((2, 5)):
                    for k in range(KD):
                        ins = nc.tensor.matmul(ps_row[l][:, m * D:(m + 1) * D], scb[:, l, k, :],
                                               wmod[:, l, k, at * D:(at + 1) * D], start=(k == 0), stop=(k == KD - 1))
                ins.then_inc(row_ready, 1)


def ttt_project_phase(nc, I, C, S):
    with ExitStack() as ctx:
        A = Alloc(nc, ctx, "proj")
        x_t = A.sb("x_t", [P, D])
        stats = A.sb("stats", [P, 6])
        mv = A.sb("mv", [P, 2])
        rstd = A.sb("rstd", [P, 1])
        xh = A.sb("xh", [P, D])
        hT = A.sb("hT", [P, KD, P])
        wq = A.sb("wq", [P, KD, D])
        wk = A.sb("wk", [P, KD, D])
        wv = A.sb("wv", [P, KD, D])
        wlr = A.sb("wlr", [P, KD, TH])
        lr_b = A.sb("lr_b", [P, TH])
        gam = A.sb("gam", [P, D])
        bet = A.sb("bet", [P, D])
        c_t = A.sb("c_t", [P, D + TH])
        c_m = A.sb("c_m", [P, TH])
        ps_T = A.ps("ps_T", [P, KD, P])
        ps_f = A.ps("ps_f", [P, 2, KD, P])
        ps_c = A.ps("ps_c", [P, D])
        ps_l = A.ps("ps_l", [P, TH])
        loaded = A.sem("loaded")
        x_ready = A.sem("x_ready")
        mv_ready = A.sem("mv_ready")
        rstd_ready = A.sem("rstd_ready")
        xh_ready = A.sem("xh_ready")
        T_ready = A.sem("T_ready")
        hT_ready = A.sem("hT_ready")
        f_ready = A.sem("f_ready")
        c_ready = A.sem("c_ready")
        f_copied = A.sem("f_copied")
        c_done = A.sem("c_done")
        lr_done = A.sem("lr_done")
        c_stored = A.sem("c_stored")
        c_back = A.sem("c_back")
        dve_step = A.sem("dve_step")
        block = ctx.enter_context(nc.Block())
        DVE_PER = 5

        @block.sync
        def _(sp):
            for w, n in ((wq, "qwT"), (wk, "kwT"), (wv, "vwT"), (wlr, "lrwT")):
                sp.dma_start(w[:, :, :], I[n].rearrange("(k p) n -> p k n", p=P)).then_inc(loaded, 16)
            for r, n in ((lr_b, "lrb"), (gam, "ttt_w"), (bet, "ttt_b")):
                sp.dma_start(r[:, :], I[n].broadcast_to([P, I[n].shape[1]])).then_inc(loaded, 16)
            with sp.Fori(0, NT) as t:
                sp.wait_ge(xh_ready, t)
                sp.dma_start(x_t[:, :], I["x"][bass.ds(t * P, P), :]).then_inc(x_ready, 16)
                sp.wait_ge(c_done, t + 1)
                sp.wait_ge(lr_done, t + 1)
                sp.dma_start(S["c_tok"][bass.ds(t * P, P), :], c_t[:, :]).then_inc(c_stored, 16)
            sp.wait_ge(c_stored, NT * 16)
            for g in range(HG):
                src = S["c_tok"].rearrange("(m t) n -> t m n", t=MB)
                sp.dma_start(S["cA"][g * MB:(g + 1) * MB, :, :], src[:, :, g * 32:(g + 1) * 32]).then_inc(c_back, 16)
                sp.dma_start(S["lA"][g * MB:(g + 1) * MB, :, :],
                             src[:, :, D + g * HR:D + (g + 1) * HR]).then_inc(c_back, 16)
            sp.wait_ge(c_back, 16 * 2 * HG)

        @block.vector
        def _(dve):
            dve.wait_ge(loaded, 16 * 7)
            nc.vector.tensor_tensor(wv[:, :, :], wk[:, :, :], wv[:, :, :], ALU.subtract).then_inc(dve_step, 1)
            with dve.Fori(0, NT) as t:
                ch = Chain(dve, dve_step, 1 + t * DVE_PER)
                dve.wait_ge(x_ready, (t + 1) * 16)
                ch.done_before(nc.vector.bn_stats(stats[:, :], x_t[:, :]), C["pad"])
                ch.done(nc.vector.bn_aggr(mv[:, :], stats[:, :]))
                nc.vector.tensor_scalar(mv[:, 1:2], mv[:, 1:2], EPS, None, ALU.add).then_inc(mv_ready, 1)
                dve.wait_ge(rstd_ready, t + 1)
                nc.vector.tensor_scalar(xh[:, :], x_t[:, :], mv[:, 0:1], rstd[:, 0:1], ALU.subtract,
                                        ALU.mult).then_inc(xh_ready, 1)
                dve.wait_ge(f_ready, t + 1)
                nc.vector.tensor_copy(S["XKT"][:, :, bass.ds(t * P, P)], ps_f[:, 0, :, :])
                nc.vector.tensor_copy(S["XQT"][:, :, bass.ds(t * P, P)], ps_f[:, 1, :, :]).then_inc(f_copied, 1)
                dve.wait_ge(c_ready, t + 1)
                dve.wait_ge(c_stored, t * 16)
                c3 = c_t[:, 0:D]
                ch.done(nc.vector.tensor_tensor(c3, ps_c[:, :], bet[:, :], ALU.add))
                ch.done(nc.vector.tensor_tensor(c3, c3, gam[:, :], ALU.mult))
                c3 = c3.rearrange("p (h e) -> p h e", e=HD)
                ch.done(nc.vector.tensor_reduce(c_m[:, :], c3, AX_X, ALU.add))
                nc.vector.scalar_tensor_tensor(out=c3, in0=bcast(c_m[:, :], 2, HD), scalar=-1.0 / HD, in1=c3,
                                               op0=ALU.mult, op1=ALU.add).then_inc(c_done, 1)
            assert ch.n == DVE_PER, ch.n

        @block.gpsimd
        def _(pool):
            with pool.Fori(0, NT) as t:
                pool.wait_ge(mv_ready, t + 1)
                nc.gpsimd.tensor_tensor(rstd[:, :], mv[:, 1:2], C["nhalf"][:, 0:1], ALU.pow).then_inc(rstd_ready, 1)

        @block.scalar
        def _(act):
            act.wait_ge(loaded, 16 * 7)
            lr_step = A.sem("lr_step")
            with act.Fori(0, NT) as t:
                act.wait_ge(T_ready, t + 1)
                for k in range(KD):
                    ins = nc.scalar.activation(hT[:, k, :], ps_T[:, k, :], ACT.Identity,
                                               bias=C["mod_col"][:, 0, 0, k:k + 1], scale=C["mod_col"][:, 0, 1, k:k + 1])
                ins.then_inc(hT_ready, 1)
                act.wait_ge(c_ready, t + 1)
                act.wait_ge(c_stored, t * 16)
                nc.scalar.activation(c_t[:, D:], ps_l[:, :], ACT.Sigmoid).then_inc(lr_step, 1)
                act.wait_ge(lr_step, t + 1)
                nc.scalar.mul(c_t[:, D:], c_t[:, D:], float(HD) ** 0.5 / HD).then_inc(lr_done, 1)

        @block.tensor
        def _(pe):
            pe.wait_ge(loaded, 16 * 7)
            pe.wait_ge(dve_step, 1)
            with pe.Fori(0, NT) as t:
                pe.wait_ge(xh_ready, t + 1)
                for k in range(KD):
                    ins = nc.tensor.transpose(ps_T[:, k, :], xh[:, k * P:(k + 1) * P], C["ident"][:, :])
                ins.then_inc(T_ready, 1)
                pe.wait_ge(hT_ready, t + 1)
                pe.wait_ge(f_copied, t)
                for n, w in enumerate((wk, wq)):
                    for a in range(KD):
                        for k in range(KD):
                            ins = nc.tensor.matmul(ps_f[:, n, a, :], w[:, k, a * P:(a + 1) * P], hT[:, k, :],
                                                   start=(k == 0), stop=(k == KD - 1))
                ins.then_inc(f_ready, 1)
                pe.wait_ge(c_done, t)
                pe.wait_ge(lr_done, t)
                for k in range(KD):
                    nc.tensor.matmul(ps_c[:, :], hT[:, k, :], wv[:, k, :], start=(k == 0), stop=(k == KD - 1))
                for k in range(KD):
                    nc.tensor.matmul(ps_l[:, :], hT[:, k, :], wlr[:, k, :], start=(k == 0), stop=False)
                nc.tensor.matmul(ps_l[:, :], C["ident"][:, :], lr_b[:, :], start=False, stop=True).then_inc(c_ready, 1)


def ttt_scan_phase(nc, I, C, S):
    with ExitStack() as ctx:
        A = Alloc(nc, ctx, "scan")
        W = A.sb("W", [P, KD + 1, 32])
        w_m = A.sb("w_m", [P, (KD + 1) * HR])
        gmask = A.sb("gmask", [P, HR])
        rmask = A.sb("rmask", [P, KD + 1, HR])
        tok = A.sb("tok", [P, MB])
        idx = A.sb("idx", [P, MB])
        ntok = A.sb("ntok", [P, 1])
        first = A.sb("first", [P, P])
        same = A.sb("same", [P, P])
        gam2 = A.sb("gam2", [P, 32])
        xk1 = [A.sb(f"xk1_{b}", [P, KD, HR, MB]) for b in range(2)]
        xk2 = [A.sb(f"xk2_{b}", [P, P]) for b in range(2)]
        zc = A.sb("zc", [P, 32])
        sq = A.sb("sq", [P, HR, HD + 1])
        vs = A.sb("vs", [P, HR])
        rs = A.sb("rs", [P, HR])
        rl = A.sb("rl", [P, HR])
        xn = A.sb("xn", [P, 32])
        g = A.sb("g", [P, 32])
        sg = A.sb("sg", [P, HR])
        u = A.sb("u", [P, 32])
        v = A.sb("v", [P, 32])
        grad = A.sb("grad", [P, 32])
        psZ = A.ps("psZ", [P, 512])
        psW = A.ps("psW", [P, KD + 1, 512])
        psX = [A.ps(f"psX{b}", [P, 512]) for b in range(2)]
        loaded = A.sem("loaded")
        consts = A.sem("consts")
        pool_step = A.sem("pool_step")
        xk1_ready = A.sem("xk1_ready")
        xk1T_ready = A.sem("xk1T_ready")
        xk2_ready = A.sem("xk2_ready")
        z_ready = A.sem("z_ready")
        sq_ready = A.sem("sq_ready")
        vs_ready = A.sem("vs_ready")
        rs_ready = A.sem("rs_ready")
        rl_ready = A.sem("rl_ready")
        zc_ready = A.sem("zc_ready")
        g_ready = A.sem("g_ready")
        g_kept = A.sem("g_kept")
        dw_ready = A.sem("dw_ready")
        w_ready = A.sem("w_ready")
        dve_step = A.sem("dve_step")
        block = ctx.enter_context(nc.Block())
        TILE_MB = P // MB
        INIT = 6
        PER = 9

        def heads(ap):
            return ap.rearrange("p (r e) -> p r e", e=HD)

        def heads3(ap):
            return ap[:, :, :].rearrange("p a (r e) -> p (a r) e", e=HD)

        @block.sync
        def _(sp):
            for dst, n in ((W[:, 0:KD, :], "W1bd"), (W[:, KD, :], "b1A"), (gmask[:, :], "c_gmask"), (rmask[:, :, :], "c_rmask"),
                           (first[:, :], "c_first"), (same[:, :], "c_same"), (gam2[:, :], "ttt_wA")):
                sp.dma_start(dst, I[n]).then_inc(loaded, 16)
            sp.dma_start(idx[:, :], I["tokidx"].broadcast_to([P, MB])).then_inc(loaded, 16)
            sp.dma_start(tok[:, :], I["c_recip"].broadcast_to([P, MB])).then_inc(loaded, 16)
            sp.wait_ge(loaded, 16 * 9)

        @block.gpsimd
        def _(pool):
            pool.wait_ge(loaded, 16 * 9)
            with pool.Fori(0, NMB // 2) as it:
                for b in range(2):
                    m = it * 2 + b
                    pool.wait_ge(xk1T_ready, m)
                    if b == 0:
                        pool.wait_ge(z_ready, it * 2)
                    else:
                        pool.wait_ge(z_ready, it * 2)
                    for a in range(KD):
                        ins = nc.gpsimd.tensor_tensor(xk1[b][:, a, :, :],
                                                      bcast(S["XKT"][:, a, bass.ds(m * MB, MB)], 1, HR),
                                                      bcast(gmask[:, :], 2, MB), ALU.mult)
                    ins.then_inc(xk1_ready, 1)
                    pool.wait_ge(vs_ready, m + 1)
                    nc.gpsimd.tensor_tensor(rs[:, :], vs[:, :], C["nhalf"][:, 0:HR], ALU.pow).then_inc(rs_ready, 1)
                    pool.wait_ge(rs_ready, m + 1)
                    nc.gpsimd.tensor_tensor(rl[:, :], rs[:, :], S["lA"][:, m, :], ALU.mult).then_inc(rl_ready, 1)

        @block.scalar
        def _(act):
            act.wait_ge(consts, 1)
            with act.Fori(0, NMB // 2) as it:
                for b in range(2):
                    m = it * 2 + b
                    act.wait_ge(xk1T_ready, m + 1)
                    act.wait_ge(dw_ready, it * 2)
                    nc.scalar.activation(xk2[b][:, :], psX[b][:, 0:P], ACT.Copy, scale=ntok[:, 0:1]).then_inc(xk2_ready, 1)
                    act.wait_ge(z_ready, m + 1)
                    act.wait_ge(vs_ready, m)
                    nc.scalar.activation(sq[:, :, 0:HD], heads(psZ[:, 0:32]), ACT.Square).then_inc(sq_ready, 1)
                    act.wait_ge(g_ready, m + 1)
                    nc.scalar.activation(S["GA"][:, m, :], grad[:, :], ACT.Copy).then_inc(g_kept, 1)

        @block.vector
        def _(dve):
            dve.wait_ge(loaded, 16 * 9)
            ch = Chain(dve, dve_step)
            ch.mark(nc.vector.memset(sq[:, :, HD:HD + 1], HD * TTT_EPS))
            ch.done(nc.vector.tensor_reduce(w_m[:, :], heads3(W), AX_X, ALU.add))
            ch.done(nc.vector.scalar_tensor_tensor(out=heads3(W), in0=bcast(w_m[:, :], 2, HD), scalar=-1.0 / HD,
                                                   in1=heads3(W), op0=ALU.mult, op1=ALU.add))
            ch.mark(nc.vector.scalar_tensor_tensor(out=gam2[:, :], in0=gam2[:, :], scalar=float(HD) ** 0.5,
                                                   in1=gam2[:, :], op0=ALU.mult, op1=ALU.mult))
            ch.done(nc.vector.tensor_tensor(tok[:, :], tok[:, :], idx[:, :], ALU.add))
            ch.done(nc.vector.tensor_scalar(tok[:, :], tok[:, :], 0.0, None, ALU.max))
            assert ch.n == INIT, ch.n
            nc.vector.tensor_scalar(ntok[:, :], tok[:, MB - 1:MB], -1.0, None, ALU.mult).then_inc(consts, 1)
            dve.wait_ge(consts, 1)
            nc.vector.tensor_scalar(same[:, :], same[:, :], ntok[:, 0:1], None, ALU.mult).then_inc(consts, 1)
            nc.vector.tensor_copy(S["tok"][:, :], tok[:, :])
            with dve.Fori(0, NT) as t:
                nc.vector.tensor_copy(S["Wt"][:, t, :, :], W[:, :, :])
                with dve.Fori(0, TILE_MB) as s:
                    m = t * TILE_MB + s
                    ch = Chain(dve, dve_step, INIT + m * PER)
                    dve.wait_ge(sq_ready, m + 1)
                    nc.vector.tensor_reduce(vs[:, :], sq[:, :, :], AX_X, ALU.add).then_inc(vs_ready, 1)
                    dve.wait_ge(rs_ready, m + 1)
                    ch.done(nc.vector.tensor_tensor(heads(xn[:, :]), heads(psZ[:, 0:32]), bcast(rs[:, :], 2, HD), ALU.mult))
                    ch.done(nc.vector.tensor_tensor(g[:, :], xn[:, :], gam2[:, :], ALU.mult))
                    ch.done(nc.vector.tensor_tensor(g[:, :], g[:, :], S["cA"][:, m, :], ALU.add))
                    ch.done(nc.vector.tensor_tensor(u[:, :], g[:, :], xn[:, :], ALU.mult))
                    ch.done(nc.vector.tensor_reduce(sg[:, :], heads(u[:, :]), AX_X, ALU.add))
                    ch.done(nc.vector.tensor_tensor(heads(u[:, :]), heads(xn[:, :]), bcast(sg[:, :], 2, HD), ALU.mult))
                    ch.done(nc.vector.tensor_tensor(v[:, :], g[:, :], u[:, :], ALU.subtract))
                    ch.done(nc.vector.tensor_reduce(sg[:, :], heads(v[:, :]), AX_X, ALU.add))
                    ch.done(nc.vector.scalar_tensor_tensor(out=heads(v[:, :]), in0=bcast(sg[:, :], 2, HD),
                                                           scalar=-1.0 / HD, in1=heads(v[:, :]), op0=ALU.mult,
                                                           op1=ALU.add))
                    dve.wait_ge(rl_ready, m + 1)
                    dve.wait_ge(g_kept, m)
                    nc.vector.tensor_tensor(heads(grad[:, :]), heads(v[:, :]), bcast(rl[:, :], 2, HD),
                                            ALU.mult).then_inc(g_ready, 1)
                    assert ch.n == PER, ch.n
                    dve.wait_ge(dw_ready, m + 1)
                    nc.vector.tensor_tensor(W[:, :, :].rearrange("p a (r e) -> p a r e", e=HD),
                                            psW[:, :, 0:32].rearrange("p a (r e) -> p a r e", e=HD),
                                            bcast(rmask[:, :, :], 3, HD), ALU.mult).then_inc(w_ready, 1)
                    dve.wait_ge(w_ready, m + 1)

        @block.tensor
        def _(pe):
            pe.wait_ge(consts, 2)
            with pe.Fori(0, NMB // 2) as it:
                for b in range(2):
                    m = it * 2 + b
                    pe.wait_ge(xk1_ready, m + 1)
                    pe.wait_ge(xk2_ready, it * 2)
                    for a in range(KD):
                        ins = nc.tensor.matmul(psX[b][64 * a:64 * a + 64, 0:P],
                                               xk1[b][:, a, :, :].rearrange("p g t -> p (g t)"), C["ident"][:, :],
                                               start=True, stop=True)
                    ins.then_inc(xk1T_ready, 1)
                    pe.wait_ge(w_ready, m)
                    nc.tensor.matmul(psZ[:, 0:32], first[:, :], W[:, KD, :], start=True, stop=False)
                    for a in range(KD):
                        ins = nc.tensor.matmul(psZ[64 * a:64 * a + 64, 0:32],
                                               xk1[b][:, a, :, :].rearrange("p g t -> p (g t)"), W[:, a, :],
                                               start=False, stop=True)
                    ins.then_inc(z_ready, 1)
                    for a in range(KD + 1):
                        nc.tensor.matmul(psW[:, a, 0:32], C["ident"][:, :], W[:, a, :], start=True, stop=False)
                    pe.wait_ge(xk2_ready, m + 1)
                    pe.wait_ge(g_ready, m + 1)
                    for a in range(KD):
                        nc.tensor.matmul(psW[:, a, 0:32], xk2[b][64 * a:64 * a + 64, :],
                                         grad[64 * a:64 * a + 64, :], start=False, stop=True)
                    nc.tensor.matmul(psW[:, KD, 0:32], same[:, :], grad[:, :], start=False, stop=True).then_inc(dw_ready, 1)


def ttt_output_phase(nc, I, C, S, x_in, x_out):
    with ExitStack() as ctx:
        A = Alloc(nc, ctx, "tout")
        wo = A.sb("wo", [P, KD, D])
        post = A.sb("post", [P, 2, KD])
        gmask = A.sb("gmask", [P, HR])
        rmask = A.sb("rmask", [P, KD + 1, HR])
        brow = A.sb("brow", [P, HG])
        pick = A.sb("pick", [P, P])
        mask = A.sb("mask", [P, P])
        prev = A.sb("prev", [P, P])
        lnw = A.sb("lnw", [P, D])
        lnb = A.sb("lnb", [P, D])
        xk_t = A.sb("xk_t", [P, KD, P])
        xq_t = A.sb("xq_t", [P, KD, P])
        qm = A.sb("qm", [P, KD, HR, P])
        w_bd = A.sb("w_bd", [P, KD, HR, 32])
        b_bd = A.sb("b_bd", [P, HG, 32])
        g_tok = A.sb("g_tok", [P, D])
        x_t = A.sb("x_t", [P, D])
        sm = A.sb("sm", [P, HG, HR, P])
        sq = A.sb("sq", [P, TH, HD + 1])
        vs = A.sb("vs", [P, TH])
        rs = A.sb("rs", [P, TH])
        y = A.sb("y", [P, D])
        stats = A.sb("stats", [P, 6])
        mv = A.sb("mv", [P, 2])
        rstd = A.sb("rstd", [P, 1])
        yT = A.sb("yT", [P, KD, P])
        o_t = A.sb("o_t", [P, D])
        psA = [A.ps(f"psA{b}", [P, HR, P]) for b in range(4)]
        psZQ = [A.ps(f"psZQ{b}", [P, 2, D]) for b in range(2)]
        psTO = A.ps("psTO", [P, 2, D])
        loaded = A.sem("loaded")
        g_stored = A.sem("g_stored")
        t_loaded = A.sem("t_loaded")
        x_loaded = A.sem("x_loaded")
        qk_ready = A.sem("qk_ready")
        qm_ready = A.sem("qm_ready")
        bd_ready = A.sem("bd_ready")
        a_ready = A.sem("a_ready")
        sm_ready = A.sem("sm_ready")
        z_ready = A.sem("z_ready")
        sq_ready = A.sem("sq_ready")
        vs_ready = A.sem("vs_ready")
        rs_ready = A.sem("rs_ready")
        mv_ready = A.sem("mv_ready")
        rstd_ready = A.sem("rstd_ready")
        y_ready = A.sem("y_ready")
        T_ready = A.sem("T_ready")
        yT_ready = A.sem("yT_ready")
        o_ready = A.sem("o_ready")
        x_done = A.sem("x_done")
        stored = A.sem("stored")
        dve_step = A.sem("dve_step")
        block = ctx.enter_context(nc.Block())
        INIT, PER = 5, 7
        NLOAD = 10

        def all_tiles(eng, body):
            body(0, 0, True, False)
            with eng.Fori(0, (NT - 2) // 2) as m:
                body(m * 2 + 1, 1, True, True)
                body(m * 2 + 2, 0, True, True)
            body(NT - 1, 1, True, True)
            body(NT, 0, False, True)

        def after(eng, sem, count):
            if not (isinstance(count, int) and count <= 0):
                eng.wait_ge(sem, count)

        @block.sync
        def _(sp):
            dst = S["g_dram"].rearrange("(m t) n -> t m n", t=MB)
            for g in range(HG):
                sp.dma_start(dst[:, :, g * 32:(g + 1) * 32], S["GA"][g * MB:(g + 1) * MB, :, :]).then_inc(g_stored, 16)
            sp.dma_start(wo[:, :, :], I["owT"].rearrange("(k p) n -> p k n", p=P)).then_inc(loaded, 16)
            for d, n in ((gmask[:, :], "c_gmask"), (rmask[:, :, :], "c_rmask"), (brow[:, :], "c_brow"),
                         (pick[:, :], "c_pick"), (mask[:, :], "c_causal"), (prev[:, :], "c_prev"),
                         (post[:, :, :], "post"), (lnw[:, :], "ttt_w"), (lnb[:, :], "ttt_b")):
                src = I[n].broadcast_to([P, D]) if n.startswith("ttt") else I[n]
                sp.dma_start(d, src).then_inc(loaded, 16)
            sp.wait_ge(g_stored, 16 * HG)

            def body(t, par, head, tail):
                if head:
                    after(sp, z_ready, t)
                    sp.dma_start(g_tok[:, :], S["g_dram"][bass.ds(t * P, P), :]).then_inc(t_loaded, 16)
                if tail:
                    after(sp, x_done, t - 1)
                    sp.dma_start(x_t[:, :], x_in[bass.ds((t - 1) * P, P), :]).then_inc(x_loaded, 16)
                    after(sp, x_done, t)
                    sp.dma_start(x_out[bass.ds((t - 1) * P, P), :], o_t[:, :]).then_inc(stored, 16)

            all_tiles(sp, body)
            sp.wait_ge(stored, 16 * NT)

        @block.scalar
        def _(act):
            act.wait_ge(loaded, 16 * NLOAD)
            act.wait_ge(bd_ready, 1)

            def body(t, par, head, tail):
                after(act, z_ready, t)
                if head:
                    nc.scalar.activation(xk_t[:, :, :], S["XKT"][:, :, bass.ds(t * P, P)], ACT.Copy)
                    nc.scalar.activation(xq_t[:, :, :], S["XQT"][:, :, bass.ds(t * P, P)], ACT.Copy).then_inc(qk_ready, 1)
                if tail:
                    nc.scalar.activation(sq[:, :, 0:HD], psZQ[1 - par][:, 0, :].rearrange("p (h e) -> p h e", e=HD),
                                         ACT.Square).then_inc(sq_ready, 1)
                    after(act, T_ready, t)
                    for k in range(KD):
                        ins = nc.scalar.activation(yT[:, k, :], psTO[:, 0, k * P:(k + 1) * P], ACT.Identity,
                                                   bias=post[:, 1, k:k + 1], scale=post[:, 0, k:k + 1])
                    ins.then_inc(yT_ready, 1)

            all_tiles(act, body)

        @block.gpsimd
        def _(pool):
            def body(t, par, head, tail):
                if head:
                    after(pool, qk_ready, t + 1)
                    for a in range(KD):
                        ins = nc.gpsimd.tensor_tensor(qm[:, a, :, :], bcast(xq_t[:, a, :], 1, HR),
                                                      bcast(rmask[:, 0, :], 2, P), ALU.mult)
                    ins.then_inc(qm_ready, 1)
                if tail:
                    after(pool, vs_ready, t)
                    nc.gpsimd.tensor_tensor(rs[:, :], vs[:, :], C["nhalf"][:, :], ALU.pow).then_inc(rs_ready, 1)
                    after(pool, mv_ready, t)
                    nc.gpsimd.tensor_tensor(rstd[:, :], mv[:, 1:2], C["nhalf"][:, 0:1], ALU.pow).then_inc(rstd_ready, 1)

            all_tiles(pool, body)

        @block.vector
        def _(dve):
            dve.wait_ge(loaded, 16 * NLOAD)
            ch = Chain(dve, dve_step)
            ch.mark(nc.vector.memset(sq[:, :, HD:HD + 1], HD * TTT_EPS))
            ch.mark(nc.vector.tensor_scalar(lnw[:, :], lnw[:, :], float(HD) ** 0.5, None, ALU.mult))
            m3 = mask[:, :].rearrange("p (m t) -> p m t", t=MB)
            ch.done(nc.vector.tensor_tensor(m3, m3, bcast(S["tok"][:, :], 1, P // MB), ALU.mult))
            ch.done(nc.vector.scalar_tensor_tensor(out=mask[:, :], in0=prev[:, :], scalar=S["tok"][:, MB - 1:MB],
                                                   in1=mask[:, :], op0=ALU.mult, op1=ALU.add))
            ch.done(nc.vector.tensor_scalar(mask[:, :], mask[:, :], -1.0, None, ALU.mult))
            nc.vector.memset(stats[:, :], 0.0).then_inc(bd_ready, 1)
            assert ch.n == INIT, ch.n

            def masked(t, groups):
                for g in groups:
                    after(dve, a_ready, t * HG + g + 1)
                    nc.vector.scalar_tensor_tensor(out=sm[:, g, :, :], in0=psA[g % 4][:, :, :], scalar=1.0,
                                                   in1=bcast(mask[:, :], 1, HR), op0=ALU.add,
                                                   op1=ALU.mult).then_inc(sm_ready, 1)

            def body(t, par, head, tail):
                ch = Chain(dve, dve_step, INIT + (t - 1) * PER)
                psZ, psQ = psZQ[1 - par][:, 0, :], psZQ[1 - par][:, 1, :]
                if head:
                    after(dve, z_ready, t)
                    for a in range(KD):
                        nc.vector.tensor_tensor(w_bd[:, a, :, :], bcast(S["Wt"][:, t, a, :], 1, HR),
                                                bcast(gmask[:, :], 2, 32), ALU.mult)
                    nc.vector.tensor_tensor(b_bd[:, :, :], bcast(S["Wt"][:, t, KD, :], 1, HG),
                                            bcast(brow[:, :], 2, 32), ALU.mult).then_inc(bd_ready, 1)
                if tail:
                    after(dve, sq_ready, t)
                    nc.vector.tensor_reduce(vs[:, :], sq[:, :, :], AX_X, ALU.add).then_inc(vs_ready, 1)
                if head:
                    masked(t, range(HR))
                if tail:
                    y3 = y[:, :].rearrange("p (h e) -> p h e", e=HD)
                    after(dve, rs_ready, t)
                    ch.done(nc.vector.tensor_tensor(y3, psZ.rearrange("p (h e) -> p h e", e=HD), bcast(rs[:, :], 2, HD), ALU.mult))
                    ch.done(nc.vector.tensor_tensor(y[:, :], y[:, :], lnw[:, :], ALU.mult))
                    ch.done(nc.vector.tensor_tensor(y[:, :], y[:, :], lnb[:, :], ALU.add))
                    ch.done(nc.vector.tensor_tensor(y[:, :], psQ, y[:, :], ALU.add))
                    ch.done_before(nc.vector.bn_stats(stats[:, :], y[:, :]), C["pad"])
                    ch.done(nc.vector.bn_aggr(mv[:, :], stats[:, :]))
                    nc.vector.tensor_scalar(mv[:, 1:2], mv[:, 1:2], TTT_EPS, None, ALU.add).then_inc(mv_ready, 1)
                if head:
                    masked(t, range(HR, HG))
                if tail:
                    after(dve, rstd_ready, t)
                    nc.vector.tensor_scalar(y[:, :], y[:, :], mv[:, 0:1], rstd[:, 0:1], ALU.subtract,
                                            ALU.mult).then_inc(y_ready, 1)
                    after(dve, o_ready, t)
                    after(dve, x_loaded, 16 * t)
                    after(dve, stored, 16 * (t - 1))
                    ch.done(nc.vector.tensor_tensor(o_t[:, :], psTO[:, 1, :], C["gate_row"][:, 0, 0, :], ALU.mult))
                    nc.vector.tensor_tensor(o_t[:, :], o_t[:, :], x_t[:, :], ALU.add).then_inc(x_done, 1)
                    assert ch.n == PER, ch.n

            all_tiles(dve, body)

        @block.tensor
        def _(pe):
            pe.wait_ge(loaded, 16 * NLOAD)

            def own_gradients(t, psZ, groups):
                for g in groups:
                    after(pe, sm_ready, t * HG + g + 1)
                    for r in range(HR):
                        c = (g * HR + r) * HD
                        ins = nc.tensor.matmul(psZ[:, c:c + HD], sm[:, g, r, :], g_tok[:, c:c + HD], start=False,
                                               stop=(g == HG - 1 and r == HR - 1))
                return ins

            def body(t, par, head, tail):
                psZ, psQ = psZQ[par][:, 0, :], psZQ[par][:, 1, :]
                if head:
                    after(pe, qk_ready, t + 1)
                    after(pe, bd_ready, t + 2)
                    after(pe, y_ready, t - 1)
                    for a in range(KD):
                        nc.tensor.transpose(psQ[:, a * P:(a + 1) * P], xq_t[:, a, :], C["ident"][:, :])
                    nc.tensor.matmul(psZ[:, :], pick[:, :], b_bd[:, :, :], start=True, stop=False)
                    for a in range(KD):
                        nc.tensor.matmul(psZ[:, a * P:(a + 1) * P], xq_t[:, a, :], w_bd[:, a, :, :], start=False, stop=False)
                    after(pe, qm_ready, t + 1)
                    for g in range(HG):
                        a, q = g // HR, g % HR
                        after(pe, sm_ready, t * HG + g - HR + 1)
                        nc.tensor.matmul(psA[q][:, :, :], xk_t[32 * q:32 * q + 32, a, :], qm[32 * q:32 * q + 32, a, :, :],
                                         start=True, stop=True).then_inc(a_ready, 1)
                    after(pe, t_loaded, 16 * (t + 1))
                    own_gradients(t, psZ, range(HG - 2))
                if tail:
                    after(pe, y_ready, t)
                    after(pe, x_done, t - 1)
                    for k in range(KD):
                        ins = nc.tensor.transpose(psTO[:, 0, k * P:(k + 1) * P], y[:, k * P:(k + 1) * P], C["ident"][:, :])
                    ins.then_inc(T_ready, 1)
                if head:
                    own_gradients(t, psZ, range(HG - 2, HG - 1))
                if tail:
                    after(pe, yT_ready, t)
                    for k in range(KD):
                        ins = nc.tensor.matmul(psTO[:, 1, :], yT[:, k, :], wo[:, k, :], start=(k == 0), stop=(k == KD - 1))
                    ins.then_inc(o_ready, 1)
                if head:
                    own_gradients(t, psZ, range(HG - 1, HG)).then_inc(z_ready, 1)

            all_tiles(pe, body)


E1, K1, I1 = 32, 8, 128
E1S = E1 + 2
SCALE1 = 2.5


def moe1_route_phase(nc, I, C, S, x_in):
    with ExitStack() as ctx:
        A = Alloc(nc, ctx, "route")
        gw = A.sb("gw", [P, KD, E1])
        x_t = [A.sb(f"x_t{b}", [P, D]) for b in range(2)]
        stats = A.sb("stats", [P, 6])
        mv = A.sb("mv", [P, 2])
        rstd = A.sb("rstd", [P, 1])
        xh = A.sb("xh", [P, D])
        hT = A.sb("hT", [P, KD, P])
        sc = A.sb("sc", [P, E1])
        top = A.sb("top", [P, K1])
        rest = A.sb("rest", [P, E1])
        tot = A.sb("tot", [P, 1])
        dw = A.sb("dw", [P, E1])
        dwT = A.sb("dwT", [E1, T])
        ones = A.sb("ones", [E1S - E1, T])
        psT = A.ps("psT", [P, KD, P])
        psS = A.ps("psS", [P, E1])
        psD = A.ps("psD", [E1, P])
        loaded = A.sem("loaded")
        x_ready = [A.sem(f"x_ready{b}") for b in range(2)]
        mv_ready = A.sem("mv_ready")
        rstd_ready = A.sem("rstd_ready")
        xh_ready = A.sem("xh_ready")
        T_ready = A.sem("T_ready")
        hT_ready = A.sem("hT_ready")
        s_ready = A.sem("s_ready")
        sc_ready = A.sem("sc_ready")
        dw_ready = A.sem("dw_ready")
        dT_ready = A.sem("dT_ready")
        dT_kept = A.sem("dT_kept")
        stored = A.sem("stored")
        ones_ready = A.sem("ones_ready")
        dve_step2 = A.sem("dve_step2")
        dve_step = A.sem("dve_step")
        block = ctx.enter_context(nc.Block())
        PER = 8

        @block.sync
        def _(sp):
            sp.dma_start(gw[:, :, :], I["gate1T"].rearrange("(k p) n -> p k n", p=P)).then_inc(loaded, 16)
            with sp.Fori(0, NT // 2) as it:
                for b in range(2):
                    sp.wait_ge(xh_ready, it * 2)
                    sp.dma_start(x_t[b][:, :], x_in[bass.ds((it * 2 + b) * P, P), :]).then_inc(x_ready[b], 16)
            sp.wait_ge(dT_kept, NT)
            sp.dma_start(S["dwT"][0:E1, :], dwT[:, :]).then_inc(stored, 16)
            sp.wait_ge(ones_ready, 1)
            sp.dma_start(S["dwT"][E1:E1S, :], ones[:, :]).then_inc(stored, 16)
            sp.wait_ge(stored, 32)

        @block.vector
        def _(dve):
            nc.vector.memset(ones[:, :], 1.0).then_inc(ones_ready, 1)
            with dve.Fori(0, NT // 2) as it:
                ch = Chain(dve, dve_step, it * 2 * PER)
                for b in range(2):
                    t = it * 2 + b
                    dve.wait_ge(x_ready[b], (it + 1) * 16)
                    ch.done_before(nc.vector.bn_stats(stats[:, :], x_t[b][:, :]), C["pad"])
                    ch.done(nc.vector.bn_aggr(mv[:, :], stats[:, :]))
                    nc.vector.tensor_scalar(mv[:, 1:2], mv[:, 1:2], EPS, None, ALU.add).then_inc(mv_ready, 1)
                    dve.wait_ge(rstd_ready, t + 1)
                    dve.wait_ge(T_ready, t)
                    nc.vector.tensor_scalar(xh[:, :], x_t[b][:, :], mv[:, 0:1], rstd[:, 0:1], ALU.subtract,
                                            ALU.mult).then_inc(xh_ready, 1)
                    dve.wait_ge(sc_ready, t + 1)
                    nc.vector.tensor_copy(C["pad"][:, 1:2], C["pad"][:, 0:1])
                    ch.done_before(nc.vector.max(out=top[:, :], in_=sc[:, :]), C["pad"])
                    ch.done(nc.vector.match_replace(out=rest[:, :], in_to_replace=top[:, :], in_values=sc[:, :],
                                                    imm_value=-1.0))
                    ch.mark(nc.vector.tensor_reduce(tot[:, :], top[:, :], AX_X, ALU.add))
                    ch.done(nc.vector.tensor_tensor(rest[:, :], rest[:, :], sc[:, :], ALU.not_equal))
                    ch.done(nc.vector.tensor_scalar(tot[:, :], tot[:, :], 1e-20, None, ALU.add))
                    ch.done(nc.vector.reciprocal(tot[:, :], tot[:, :]))
                    nc.vector.tensor_tensor(rest[:, :], rest[:, :], sc[:, :], ALU.mult).then_inc(dve_step2, 1)
                    dve.wait_ge(dve_step2, t + 1)
                    dve.wait_ge(dT_ready, t)
                    nc.vector.tensor_scalar(dw[:, :], rest[:, :], tot[:, 0:1], SCALE1, ALU.mult, ALU.mult).then_inc(dw_ready, 1)
                assert ch.n == 2 * PER, ch.n

        @block.gpsimd
        def _(pool):
            with pool.Fori(0, NT) as t:
                pool.wait_ge(mv_ready, t + 1)
                nc.gpsimd.tensor_tensor(rstd[:, :], mv[:, 1:2], C["nhalf"][:, 0:1], ALU.pow).then_inc(rstd_ready, 1)

        @block.scalar
        def _(act):
            with act.Fori(0, NT) as t:
                act.wait_ge(T_ready, t + 1)
                act.wait_ge(s_ready, t)
                for k in range(KD):
                    ins = nc.scalar.activation(hT[:, k, :], psT[:, k, :], ACT.Identity,
                                               bias=C["mod_col"][:, 0, 2, k:k + 1], scale=C["mod_col"][:, 0, 3, k:k + 1])
                ins.then_inc(hT_ready, 1)
                act.wait_ge(hT_ready, t + 1)
                nc.scalar.activation(S["hT"][:, :, bass.ds(t * P, P)], hT[:, :, :], ACT.Copy)
                act.wait_ge(s_ready, t + 1)
                act.wait_ge(dw_ready, t)
                nc.scalar.activation(sc[:, :], psS[:, :], ACT.Sigmoid).then_inc(sc_ready, 1)
                act.wait_ge(dT_ready, t + 1)
                nc.scalar.activation(dwT[:, bass.ds(t * P, P)], psD[:, :], ACT.Copy).then_inc(dT_kept, 1)

        @block.tensor
        def _(pe):
            pe.wait_ge(loaded, 16)
            with pe.Fori(0, NT) as t:
                pe.wait_ge(xh_ready, t + 1)
                pe.wait_ge(hT_ready, t)
                for k in range(KD):
                    ins = nc.tensor.transpose(psT[:, k, :], xh[:, k * P:(k + 1) * P], C["ident"][:, :])
                ins.then_inc(T_ready, 1)
                pe.wait_ge(hT_ready, t + 1)
                pe.wait_ge(sc_ready, t)
                for k in range(KD):
                    ins = nc.tensor.matmul(psS[:, :], hT[:, k, :], gw[:, k, :], start=(k == 0), stop=(k == KD - 1))
                ins.then_inc(s_ready, 1)
                pe.wait_ge(dw_ready, t + 1)
                pe.wait_ge(dT_kept, t)
                nc.tensor.transpose(psD[:, :], dw[:, :], C["ident"][:, :]).then_inc(dT_ready, 1)


def moe1_expert_phase(nc, I, C, S, x_in, x_out):
    with ExitStack() as ctx:
        A = Alloc(nc, ctx, "experts")
        NS, SUB = 2, 512
        BLK = NS * SUB
        NB = T // BLK
        NTB = BLK // P
        w = [A.sb(f"w{b}", [P, 3, D]) for b in range(2)]
        dwb = [A.sb(f"dwb{b}", [P, NS, SUB]) for b in range(2)]
        sg = [A.sb(f"sg{b}", [P, SUB]) for b in range(2)]
        up = [A.sb(f"up{b}", [P, SUB]) for b in range(2)]
        act_ = [A.sb(f"act{b}", [P, SUB]) for b in range(2)]
        zeros = A.sb("zeros", [P, SUB])
        x_t = A.sb("x_t", [P, NTB, D])
        psG = [A.ps(f"psG{b}", [P, SUB]) for b in range(2)]
        psU = [A.ps(f"psU{b}", [P, SUB]) for b in range(2)]
        psY = A.ps("psY", [P, NTB, D])
        w_ready = [A.sem(f"w_ready{b}") for b in range(2)]
        gu_ready = A.sem("gu_ready")
        sg_ready = A.sem("sg_ready")
        up_ready = A.sem("up_ready")
        act_ready = A.sem("act_ready")
        down_done = A.sem("down_done")
        y_ready = A.sem("y_ready")
        y_read = A.sem("y_read")
        x_ready = A.sem("x_ready")
        gated = A.sem("gated")
        x_done = A.sem("x_done")
        stored = A.sem("stored")
        zero_ready = A.sem("zero_ready")
        block = ctx.enter_context(nc.Block())
        NP = E1S // 2
        STEPS = NP * 2 * NS
        Q = 2 * NS

        @block.sync
        def _(sp):
            with sp.Fori(0, NB) as n:
                with sp.Fori(0, NP) as it:
                    for b in range(2):
                        sp.wait_ge(down_done, n * STEPS + it * Q)
                        sp.dma_start(w[b][:, :, :], I["w1"][bass.ds((it * 2 + b), 1), :, :].rearrange(
                            "e p (c n) -> p (e c) n", c=3)).then_inc(w_ready[b], 16)
                        sp.dma_start(dwb[b][:, :, :].rearrange("p s n -> p (s n)"),
                                     S["dwT"][bass.ds(it * 2 + b, 1), bass.ds(n * BLK, BLK)].broadcast_to(
                                         [P, BLK])).then_inc(w_ready[b], 16)
                sp.wait_ge(stored, n * 16)
                sp.dma_start(x_t[:, :, :], x_in[bass.ds(n * BLK, BLK), :].rearrange("(j p) d -> p j d", p=P)).then_inc(x_ready, 16)
                sp.wait_ge(x_done, n + 1)
                sp.dma_start(x_out[bass.ds(n * BLK, BLK), :].rearrange("(j p) d -> p j d", p=P), x_t[:, :, :]).then_inc(stored, 16)
            sp.wait_ge(stored, NB * 16)

        @block.scalar
        def _(act):
            with act.Fori(0, NB * NP) as it:
                for i in range(Q):
                    s = it * Q + i
                    act.wait_ge(gu_ready, s + 1)
                    if i < 2:
                        act.wait_ge(act_ready, it * Q)
                    else:
                        act.wait_ge(act_ready, s - 1)
                    nc.scalar.activation(sg[i % 2][:, :], psG[i % 2][:, :], ACT.Silu).then_inc(sg_ready, 1)

        @block.vector
        def _(dve):
            nc.vector.memset(zeros[:, :], 0.0).then_inc(zero_ready, 1)
            with dve.Fori(0, NB) as n:
                with dve.Fori(0, NP) as it:
                    for i in range(Q):
                        s = n * STEPS + it * Q + i
                        b, h = i // NS, i % NS
                        if h == 0:
                            dve.wait_ge(w_ready[b], 32 * (n * NP + it + 1))
                        dve.wait_ge(gu_ready, s + 1)
                        nc.vector.tensor_tensor(up[i % 2][:, :], psU[i % 2][:, :], dwb[b][:, h, :], ALU.mult).then_inc(up_ready, 1)
                        dve.wait_ge(sg_ready, s + 1)
                        dve.wait_ge(up_ready, s + 1)
                        if i < 2:
                            dve.wait_ge(down_done, n * STEPS + it * Q)
                        else:
                            dve.wait_ge(down_done, s - 1)
                        nc.vector.tensor_tensor(act_[i % 2][:, :], up[i % 2][:, :], sg[i % 2][:, :], ALU.mult).then_inc(act_ready, 1)
                dve.wait_ge(y_ready, n + 1)
                dve.wait_ge(x_ready, (n + 1) * 16)
                for j in range(NTB):
                    nc.vector.tensor_tensor(psY[:, j, :], psY[:, j, :], C["gate_row"][:, 0, 1, :], ALU.mult).then_inc(gated, 1)
                dve.wait_ge(gated, (n + 1) * NTB)
                nc.vector.tensor_tensor(x_t[:, :, :], psY[:, :, :], x_t[:, :, :], ALU.add).then_inc(x_done, 1)

        @block.tensor
        def _(pe):
            pe.wait_ge(zero_ready, 1)
            with pe.Fori(0, NB) as n:
                pe.wait_ge(x_done, n)
                for j in range(0, NTB, 2):
                    nc.tensor.matmul(psY[:, j:j + 2, :], C["ident"][:, :], zeros[:, :], start=True, stop=False)
                with pe.Fori(0, NP) as it:
                    base = n * STEPS + it * Q

                    def gate_up(i):
                        b, h = i // NS, i % NS
                        if h == 0:
                            pe.wait_ge(w_ready[b], 32 * (n * NP + it + 1))
                        if i < 2:
                            pe.wait_ge(act_ready, base)
                        else:
                            pe.wait_ge(act_ready, base + i - 1)
                        for c, ps in enumerate((psG[i % 2], psU[i % 2])):
                            for k in range(KD):
                                ins = nc.tensor.matmul(ps[:, :], w[b][:, k, c * I1:(c + 1) * I1],
                                                       S["hT"][:, k, bass.ds(n * BLK + h * SUB, SUB)],
                                                       start=(k == 0), stop=(k == KD - 1))
                        ins.then_inc(gu_ready, 1)

                    def down(i):
                        b, h = i // NS, i % NS
                        pe.wait_ge(act_ready, base + i + 1)
                        for j in range(SUB // P):
                            ins = nc.tensor.matmul(psY[:, h * (SUB // P) + j, :], act_[i % 2][:, j * P:(j + 1) * P],
                                                   w[b][:, 2, :], start=False, stop=False)
                        ins.then_inc(down_done, 1)

                    gate_up(0)
                    for i in range(1, Q):
                        gate_up(i)
                        down(i - 1)
                    down(Q - 1)
                for j in range(0, NTB, 2):
                    ins = nc.tensor.matmul(psY[:, j:j + 2, :], C["ident"][:, :], zeros[:, :], start=False, stop=True)
                ins.then_inc(y_ready, 1)


E2, K2, BOT = 8, 2, 64
M2 = E2 * BOT // P


def moe2_phase(nc, I, C, x_in, x_out):
    with ExitStack() as ctx:
        A = Alloc(nc, ctx, "moe2")
        TB = 4
        BLK = TB * P
        NB = T // BLK
        gw = A.sb("gw", [P, KD, E2])
        wd = A.sb("wd", [P, KD, E2 * BOT])
        wu = A.sb("wu", [P, M2, D])
        bd = A.sb("bd", [P, M2])
        wsd = A.sb("wsd", [P, KD, BOT])
        wsu = A.sb("wsu", [BOT, D])
        bsd = A.sb("bsd", [BOT, 1])
        bu = A.sb("bu", [E2 + 1, D])
        sel = A.sb("sel", [E2 + 1, M2, P])
        tri = A.sb("tri", [P, E2 * E2])
        x_t = [A.sb(f"x_t{b}", [P, TB, D]) for b in range(2)]
        stats = A.sb("stats", [P, TB, 6])
        mv = A.sb("mv", [P, TB, 2])
        rstd = A.sb("rstd", [P, TB])
        xh = A.sb("xh", [P, TB, D])
        hT = A.sb("hT", [P, KD, BLK])
        pr = A.sb("pr", [P, TB, E2])
        mx = A.sb("mx", [P, TB])
        gt = A.sb("gt", [P, TB, E2, E2])
        eq = A.sb("eq", [P, TB, E2, E2])
        rank = A.sb("rank", [P, TB, E2])
        cT = A.sb("cT", [E2 + 1, BLK])
        hm = A.sb("hm", [P, M2, BLK])
        hs = A.sb("hs", [BOT, BLK])
        y = A.sb("y", [P, TB, D])
        psT = A.ps("psT", [P, 2, 512])
        psL = A.ps("psL", [P, TB, E2])
        psH = [A.ps(f"psH{b}", [P, BLK]) for b in range(2)]
        psC = A.ps("psC", [P, BLK])
        psY = A.ps("psY", [P, 2, 512])
        loaded = A.sem("loaded")
        x_ready = [A.sem(f"x_ready{b}") for b in range(2)]
        mv_ready = A.sem("mv_ready")
        rstd_ready = A.sem("rstd_ready")
        xh_ready = A.sem("xh_ready")
        T_ready = A.sem("T_ready")
        hT_ready = A.sem("hT_ready")
        l_ready = A.sem("l_ready")
        e_in = A.sem("e_in")
        e_ready = A.sem("e_ready")
        c_ready = A.sem("c_ready")
        cT_ready = A.sem("cT_ready")
        cT_kept = A.sem("cT_kept")
        h_ready = A.sem("h_ready")
        gelu_ready = A.sem("gelu_ready")
        w_ready = A.sem("w_ready")
        hm_ready = A.sem("hm_ready")
        y_ready = A.sem("y_ready")
        y_gated = A.sem("y_gated")
        x_done = A.sem("x_done")
        stored = [A.sem(f"stored{b}") for b in range(2)]
        ones_ready = A.sem("ones_ready")
        dve_step = A.sem("dve_step")
        block = ctx.enter_context(nc.Block())
        PER = 13
        NLOAD = 10

        @block.sync
        def _(sp):
            for d, n in ((gw, "gate2T"), (wd, "wdT"), (wsd, "wsdT")):
                sp.dma_start(d[:, :, :], I[n].rearrange("(k p) n -> p k n", p=P)).then_inc(loaded, 16)
            sp.dma_start(wu[:, :, :], I["wuT"].rearrange("(m p) n -> p m n", p=P)).then_inc(loaded, 16)
            sp.dma_start(sel[:, :, :], I["c_sel"]).then_inc(loaded, 16)
            for d, n in ((bd, "bd"), (wsu, "wsuT"), (bsd, "bsd"), (bu, "bu")):
                sp.dma_start(d[:, :], I[n]).then_inc(loaded, 16)
            sp.dma_start(tri[:, :], I["c_tri"].broadcast_to([P, E2 * E2])).then_inc(loaded, 16)
            with sp.Fori(0, NB // 2) as it:
                for b in range(2):
                    sp.wait_ge(stored[b], it * 16)
                    sp.dma_start(x_t[b][:, :, :], x_in[bass.ds((it * 2 + b) * BLK, BLK), :].rearrange(
                        "(j p) d -> p j d", p=P)).then_inc(x_ready[b], 16)
                for b in range(2):
                    sp.wait_ge(x_done, it * 2 + b + 1)
                    sp.dma_start(x_out[bass.ds((it * 2 + b) * BLK, BLK), :].rearrange("(j p) d -> p j d", p=P),
                                 x_t[b][:, :, :]).then_inc(stored[b], 16)
            for b in range(2):
                sp.wait_ge(stored[b], NB // 2 * 16)

        @block.gpsimd
        def _(pool):
            nc.gpsimd.memset(cT[:, :], 1.0).then_inc(ones_ready, 1)
            with pool.Fori(0, NB) as n:
                pool.wait_ge(mv_ready, n + 1)
                nc.gpsimd.tensor_tensor(rstd[:, :], mv[:, :, 1], C["nhalf"][:, 0:TB], ALU.pow).then_inc(rstd_ready, 1)

        @block.scalar
        def _(act):
            act.wait_ge(loaded, 16 * NLOAD)
            act.wait_ge(ones_ready, 1)
            with act.Fori(0, NB) as n:
                act.wait_ge(h_ready, n * (M2 + 1))
                for k in range(KD):
                    act.wait_ge(T_ready, n * KD + k + 1)
                    ins = nc.scalar.activation(hT[:, k, :], psT[:, k, :], ACT.Identity,
                                               bias=C["mod_col"][:, 1, 2, k:k + 1], scale=C["mod_col"][:, 1, 3, k:k + 1])
                ins.then_inc(hT_ready, 1)
                act.wait_ge(e_in, n + 1)
                nc.scalar.activation(pr[:, :, :], pr[:, :, :], ACT.Exp).then_inc(e_ready, 1)
                for m in range(M2):
                    act.wait_ge(h_ready, n * (M2 + 1) + m + 1)
                    act.wait_ge(y_ready, n * TB)
                    nc.scalar.activation(hm[:, m, :], psH[m % 2][:, :], ACT.Gelu, bias=bd[:, m:m + 1]).then_inc(gelu_ready, 1)
                act.wait_ge(h_ready, n * (M2 + 1) + M2 + 1)
                nc.scalar.activation(hs[:, :], psH[M2 % 2][0:BOT, :], ACT.Gelu, bias=bsd[:, 0:1]).then_inc(gelu_ready, 1)

        @block.vector
        def _(dve):
            dve.wait_ge(loaded, 16 * NLOAD)
            with dve.Fori(0, NB // 2) as it:
                for b in range(2):
                    n = it * 2 + b
                    ch = Chain(dve, dve_step, n * PER)
                    dve.wait_ge(x_ready[b], (it + 1) * 16)
                    for j in range(TB):
                        ins = nc.vector.bn_stats(stats[:, j, :], x_t[b][:, j, :])
                    ch.done_before(ins, C["pad"])
                    for j in range(TB):
                        ins = nc.vector.bn_aggr(mv[:, j, :], stats[:, j, :])
                    ch.done(ins)
                    nc.vector.tensor_scalar(mv[:, :, 1], mv[:, :, 1], EPS, None, ALU.add).then_inc(mv_ready, 1)
                    dve.wait_ge(rstd_ready, n + 1)
                    for j in range(TB):
                        nc.vector.tensor_scalar(xh[:, j, :], x_t[b][:, j, :], mv[:, j, 0:1], rstd[:, j:j + 1], ALU.subtract,
                                                ALU.mult).then_inc(xh_ready, 1)
                    dve.wait_ge(l_ready, n + 1)
                    ch.done(nc.vector.tensor_reduce(mx[:, :], psL[:, :, :], AX_X, ALU.max))
                    nc.vector.tensor_tensor(pr[:, :, :], psL[:, :, :], bcast(mx[:, :], 2, E2), ALU.subtract).then_inc(e_in, 1)
                    dve.wait_ge(e_ready, n + 1)
                    ch.done(nc.vector.tensor_reduce(mx[:, :], pr[:, :, :], AX_X, ALU.add))
                    ch.done(nc.vector.reciprocal(mx[:, :], mx[:, :]))
                    ch.done(nc.vector.tensor_tensor(pr[:, :, :], pr[:, :, :], bcast(mx[:, :], 2, E2), ALU.mult))
                    mine, other = bcast(pr[:, :, :], 3, E2), bcast(pr[:, :, :], 2, E2)
                    nc.vector.tensor_tensor(gt[:, :, :, :], other, mine, ALU.is_gt)
                    ch.done(nc.vector.tensor_tensor(eq[:, :, :, :], other, mine, ALU.is_equal))
                    flat = lambda a: a[:, :, :, :].rearrange("p j a b -> p j (a b)")
                    ch.done(nc.vector.tensor_tensor(flat(eq), flat(eq), bcast(tri[:, :], 1, TB), ALU.mult))
                    ch.done(nc.vector.tensor_tensor(flat(gt), flat(gt), flat(eq), ALU.add))
                    ch.done(nc.vector.tensor_reduce(rank[:, :, :], gt[:, :, :, :], AX_X, ALU.add))
                    ch.done(nc.vector.scalar_tensor_tensor(out=pr[:, :, :], in0=rank[:, :, :], scalar=float(K2),
                                                           in1=pr[:, :, :], op0=ALU.is_lt, op1=ALU.mult))
                    ch.done(nc.vector.tensor_reduce(mx[:, :], pr[:, :, :], AX_X, ALU.add))
                    ch.done(nc.vector.reciprocal(mx[:, :], mx[:, :]))
                    dve.wait_ge(cT_ready, n)
                    nc.vector.tensor_tensor(rank[:, :, :], pr[:, :, :], bcast(mx[:, :], 2, E2), ALU.mult).then_inc(c_ready, 1)
                    dve.wait_ge(cT_ready, n + 1)
                    nc.vector.tensor_copy(cT[0:E2, :], psC[0:E2, :]).then_inc(cT_kept, 1)
                    for m in range(M2):
                        dve.wait_ge(w_ready, n * M2 + m + 1)
                        dve.wait_ge(gelu_ready, n * (M2 + 1) + m + 1)
                        nc.vector.tensor_tensor(hm[:, m, :], psC[:, :], hm[:, m, :], ALU.mult).then_inc(hm_ready, 1)
                    for j in range(TB):
                        dve.wait_ge(y_ready, n * TB + j + 1)
                        nc.vector.tensor_tensor(y[:, j, :], psY[:, j % 2, 0:D], C["gate_row"][:, 1, 1, :],
                                                ALU.mult).then_inc(y_gated, 1)
                    dve.wait_ge(y_gated, n * TB + TB)
                    nc.vector.tensor_tensor(x_t[b][:, :, :], y[:, :, :], x_t[b][:, :, :], ALU.add).then_inc(x_done, 1)
                    assert ch.n == PER, ch.n

        @block.tensor
        def _(pe):
            pe.wait_ge(loaded, 16 * NLOAD)
            with pe.Fori(0, NB) as n:
                pe.wait_ge(hT_ready, n)
                for k in range(KD):
                    for j in range(TB):
                        if k == 0:
                            pe.wait_ge(xh_ready, n * TB + j + 1)
                        ins = nc.tensor.matmul(psT[:, k, j * P:(j + 1) * P], xh[:, j, k * P:(k + 1) * P],
                                               C["ident"][:, :], start=True, stop=True)
                    ins.then_inc(T_ready, 1)
                pe.wait_ge(hT_ready, n + 1)
                pe.wait_ge(e_in, n)
                for j in range(TB):
                    for k in range(KD):
                        ins = nc.tensor.matmul(psL[:, j, :], hT[:, k, j * P:(j + 1) * P], gw[:, k, :],
                                               start=(k == 0), stop=(k == KD - 1))
                ins.then_inc(l_ready, 1)

                def bottleneck(m):
                    if m >= 2:
                        pe.wait_ge(gelu_ready, n * (M2 + 1) + m - 1)
                    else:
                        pe.wait_ge(gelu_ready, n * (M2 + 1))
                    for k in range(KD):
                        if m < M2:
                            ins = nc.tensor.matmul(psH[m % 2][:, :], wd[:, k, m * P:(m + 1) * P], hT[:, k, :],
                                                   start=(k == 0), stop=(k == KD - 1))
                        else:
                            ins = nc.tensor.matmul(psH[m % 2][0:BOT, :], wsd[:, k, :], hT[:, k, :],
                                                   start=(k == 0), stop=(k == KD - 1))
                    ins.then_inc(h_ready, 1)

                def spread(m):
                    if m:
                        pe.wait_ge(hm_ready, n * M2 + m)
                    nc.tensor.matmul(psC[:, :], sel[:, m, :], cT[:, :], start=True, stop=True).then_inc(w_ready, 1)

                bottleneck(0)
                bottleneck(1)
                pe.wait_ge(c_ready, n + 1)
                pe.wait_ge(hm_ready, n * M2)
                for j in range(TB):
                    ins = nc.tensor.matmul(psC[0:E2, j * P:(j + 1) * P], rank[:, j, :], C["ident"][:, :],
                                           start=True, stop=True)
                ins.then_inc(cT_ready, 1)
                pe.wait_ge(cT_kept, n + 1)
                spread(0)
                bottleneck(2)
                spread(1)
                bottleneck(3)
                spread(2)
                bottleneck(4)
                spread(3)
                pe.wait_ge(hm_ready, (n + 1) * M2)
                pe.wait_ge(gelu_ready, (n + 1) * (M2 + 1))
                for j in range(TB):
                    if j >= 2:
                        pe.wait_ge(y_gated, n * TB + j - 1)
                    else:
                        pe.wait_ge(y_gated, n * TB)
                    t = slice(j * P, (j + 1) * P)
                    for m in range(M2):
                        nc.tensor.matmul(psY[:, j % 2, 0:D], hm[:, m, t], wu[:, m, :], start=(m == 0), stop=False)
                    nc.tensor.matmul(psY[:, j % 2, 0:D], hs[:, t], wsu[:, :], start=False, stop=False)
                    nc.tensor.matmul(psY[:, j % 2, 0:D], cT[:, t], bu[:, :], start=False, stop=True).then_inc(y_ready, 1)


NH = 16
TAPS = 4
TK, L, SB = 64, 32, 8
NTK = T // TK
NC, NSB = TK // L, L // SB
NV = NC * NSB
KAPPA = 2.0 ** -64
SCALE = float(P) ** -0.5
RECTS = [(0, 2, 1, 7, 0), (2, 2, 3, 5, 14 * NH), (4, 2, 5, 3, 24 * NH), (6, 1, 7, 1, 30 * NH)]
NPAIR = 31 * NH
WARM = 6


def kda_phase(nc, I, C, S, x_in, x_out):
    with ExitStack() as ctx:
        A = Alloc(nc, ctx, "kda")
        w_in = A.sb("w_in", [P, KD, NH, 4, P])
        w_g = A.sb("w_g", [P, KD, NH * P])
        w_b = A.sb("w_b", [P, KD, NH])
        w_o = A.sb("w_o", [P, NH, D])
        taps = A.sb("taps", [P, NH, 3, TAPS])
        cbias = A.sb("cbias", [P, NH, 3])
        abias = A.sb("abias", [P, NH])
        bbias = A.sb("bbias", [NH, 1])
        ln = A.sb("ln", [P, 2])
        m01 = A.sb("m01", [P, 2, TK])
        hmask = A.sb("hmask", [P, NH])
        cmask = A.sb("cmask", [P, NH, SB])
        centre = A.sb("centre", [P, P])
        ones = A.sb("ones", [P, P])
        eps = A.sb("eps", [P, 1])
        x_t = A.sb("x_t", [TK, D])
        stats = A.sb("stats", [TK, 6])
        mv = A.sb("mv", [TK, 2])
        rstd = A.sb("rstd", [TK, 1])
        xh = A.sb("xh", [TK, D])
        hT = [A.sb(f"hT{b}", [P, KD + 1, TK]) for b in range(2)]
        bT = A.sb("bT", [NH, TK])
        bb = A.sb("bb", [P, NH, TK])
        raw = A.sb("raw", [P, 2, 3, TAPS - 1 + TK])
        hist = A.sb("hist", [P, NH, 3, TAPS - 1])
        tp = [A.sb(f"tp{m}", [P, 6, TK]) for m in range(TAPS - 2)]
        yc = A.sb("yc", [P, 2, 3, TK])
        sg = A.sb("sg", [P, 2, 3, TK])
        tp.append(sg[:, :, :, :].rearrange("p h j t -> p (h j) t"))
        sv = A.sb("sv", [P, 2, TK])
        sa = [A.sb(f"sa{b}", [P, 2, TK]) for b in range(2)]
        d01 = A.sb("d01", [P, 2, 2, TK])
        rr = A.sb("rr", [P, 2, TK])
        bv = A.sb("bv", [P, 2, TK])
        QK = [A.sb(f"QK{b}", [P, 2, NH, TK]) for b in range(2)]
        VT = [A.sb(f"VT{b}", [P, NH, TK]) for b in range(2)]
        DT = [A.sb(f"DT{b}", [P, NH, TK]) for b in range(2)]
        RI = [A.sb(f"RI{b}", [P, NH, TK]) for b in range(2)]
        O = A.sb("O", [P, NH, TK])
        O_first = A.sb("O_first", [P, NH, L])
        GT = A.sb("GT", [P, NH, TK])
        F = A.sb("F", [P, NC, NH])
        frow = A.sb("frow", [NC * NH, P])
        fb = A.sb("fb", [P, NH // 2, P])
        St = A.sb("St", [P, NH, P])
        kk = A.sb("kk", [P, NPAIR])
        H = [A.sb(f"H{b}", [P, NPAIR]) for b in range(2)]
        gk = A.sb("gk", [P, NH, L - SB])
        gq = A.sb("gq", [P, NH, L])
        E = A.sb("E", [P, NH, SB])
        ks = A.sb("ks", [P, 2, NH, SB])
        EF = A.sb("EF", [P, NH, L])
        tmp = A.sb("tmp", [P, NH, SB])
        wt = A.sb("wt", [P, P])
        ktok = A.sb("ktok", [P, 4, P])
        ws = A.sb("ws", [P, 4, P])
        sq = A.sb("sq", [P, NH, L])
        var = A.sb("var", [P, NC * 4])
        yT = A.sb("yT", [P, KD, TK])
        xr = A.sb("xr", [TK, D])
        o_t = xh
        psOX = A.ps("psOX", [P, NH, 2, L])
        psO, psX = psOX[:, :, 0, :], psOX[:, :, 1, :]
        psS = A.ps("psS", [P, 4, P])
        psG = A.ps("psG", [P, 512])
        psT = A.ps("psT", [P, 4, P])
        psK = A.ps("psK", [P, 4, P])
        psP = A.ps("psP", [P, 2, 4, TK])
        psM = A.ps("psM", [P, 512])
        names = """loaded x_ready ln_step mv_ready rstd_ready xh_ready T_ready hT_ready b_ready bs_ready bT_ready b_stored bb_ready
            in_ready raw_ready tap_ready a_ready tapm_ready conv_step conv_done sg_ready silu_ready ia_ready d_ready
            scan_ready ri_ready bv_ready v_done f_ready fT_ready frow_ready f_stored f_loaded fs_ready oc_kept
            kk_ready spread_ready kko_kept h_ready ks_ready kc_ready kt_ready kt_kept gk_ready gkm_ready gq_ready gqm_ready
            sk_ready x_next x_read b_step e_done ef_ready wt_ready wt_kept ws_ready ws_kept su_ready s_part s_ready
            o_sum o_read g_ready gate_ready c_ready csq_ready c_kept v_part v_ready ve_ready rs_ready r_ready
            n_ready ng_ready n_gated y_ready yT_kept yo_ready og_ready xr_ready x_done stored set_up""".split()
        Z = {n: A.sem(n) for n in names}
        block = ctx.enter_context(nc.Block())
        NLOAD = 15
        PAIRS = NH // 2
        assert PAIRS == NV
        CHAIN = 1 + 2 * (SB - 1) - 1

        def after(eng, sem, count):
            if not (isinstance(count, int) and count <= 0):
                eng.wait_ge(Z[sem], count)

        def all_parts(eng, part):
            part(-1, 1, False, False, True, True)
            part(0, 0, True, False, True, True)
            with eng.Fori(0, (NTK - 4) // 2) as m:
                part(m * 2 + 1, 1, True, True, True, True)
                part(m * 2 + 2, 0, True, True, True, True)
            part(NTK - 3, 1, True, True, True, True)
            part(NTK - 2, 0, True, True, True, False)
            part(NTK - 1, 1, True, True, False, False)
            part(NTK, 0, False, True, False, False)

        def at_sub(ap, v):
            return ap[:, :, v * SB:(v + 1) * SB]

        def at_chunk(ap, c):
            return ap[:, :, c * L:(c + 1) * L]

        def at_pair(ap, q):
            return ap[:, 2 * q:2 * q + 2, :]

        def rect(ap, r):
            _, n, _, m, off = r
            return ap[:, off:off + NH * n * m].rearrange("p (h t u) -> p h t u", h=NH, t=n)

        mM = psM[:, :].rearrange("p (h t) -> p h t", h=NH)

        @block.sync
        def _(sp):
            for k in range(KD):
                sp.dma_start(w_in[:, k].rearrange("p h c n -> p (h c n)"), I["win"][k * P:(k + 1) * P, :]).then_inc(Z["loaded"], 16)
                sp.dma_start(w_g[:, k, :], I["wgT"][k * P:(k + 1) * P, :]).then_inc(Z["loaded"], 16)
            sp.dma_start(w_o[:, :, :], I["woT"].rearrange("(h p) n -> p h n", p=P)).then_inc(Z["loaded"], 16)
            sp.dma_start(w_b[:, :, :], I["wbT"].rearrange("(k p) n -> p k n", p=P)).then_inc(Z["loaded"], 16)
            for d, n in ((taps[:, :, :, :], "taps"), (cbias[:, :, :], "cbias"), (abias[:, :], "abias"), (bbias[:, :], "bbias"),
                         (ln[:, :], "kln"), (m01[:, :, :], "c_m01"), (hmask[:, :], "c_hmask"), (cmask[:, :, :], "c_cmask"),
                         (centre[:, :], "c_centre")):
                sp.dma_start(d, I[n]).then_inc(Z["loaded"], 16)

            def load_x(k):
                after(sp, "xh_ready", k)
                sp.dma_start(x_t[:, :], x_in[bass.ds(k * TK, TK), :]).then_inc(Z["x_ready"], 16)

            def load_b(k):
                after(sp, "bT_ready", k + 1)
                sp.dma_start(S["b_rows"][:, :], bT[:, :]).then_inc(Z["b_stored"], 16)
                after(sp, "b_stored", k * 16 + 16)
                sp.dma_start(bb[:, :, :].rearrange("p h t -> p (h t)"),
                             S["b_rows"][:, :].rearrange("(a h) t -> a (h t)", a=1).broadcast_to([P, NH * TK])).then_inc(Z["bb_ready"], 16)

            def load_f(n, c):
                for i in range(2):
                    if c or i:
                        after(sp, "fs_ready", n * (NC * 2) + 2 * c + i)
                    h = c * NH + i * NH // 2
                    sp.dma_start(fb[:, :, :].rearrange("p h i -> p (h i)"),
                                 S["f_rows"][h:h + NH // 2, :].rearrange("(a h) i -> a (h i)", a=1).broadcast_to(
                                     [P, NH // 2 * P])).then_inc(Z["f_loaded"], 16)

            def part(n, par, solve, finish, project, norm):
                if norm:
                    load_x(n + 2)
                if solve:
                    after(sp, "frow_ready", n + 1)
                    sp.dma_start(S["f_rows"][:, :], frow[:, :]).then_inc(Z["f_stored"], 16)
                    after(sp, "f_stored", n * 16 + 16)
                    load_f(n, 0)
                if finish:
                    after(sp, "x_done", n - 1)
                    sp.dma_start(xr[:, :], x_in[bass.ds((n - 1) * TK, TK), :]).then_inc(Z["xr_ready"], 16)
                if solve:
                    load_f(n, 1)
                if finish:
                    after(sp, "x_done", n)
                    sp.dma_start(x_out[bass.ds((n - 1) * TK, TK), :], o_t[:, :]).then_inc(Z["stored"], 16)
                if norm:
                    load_b(n + 2)

            load_x(0)
            load_b(0)
            all_parts(sp, part)
            sp.wait_ge(Z["stored"], 16 * NTK)

        @block.gpsimd
        def _(pool):
            pool.wait_ge(Z["loaded"], 16 * NLOAD)
            add = nc.gpsimd.tensor_tensor

            def root(k):
                after(pool, "mv_ready", k + 1)
                add(rstd[:, :], mv[:, 1:2], C["nhalf"][0:TK, 0:1], ALU.pow).then_inc(Z["rstd_ready"], 1)

            def tap_products(k, q):
                after(pool, "raw_ready", k * PAIRS + q + 1)
                after(pool, "conv_done", k * PAIRS + q)
                after(pool, "silu_ready", k * PAIRS + q)
                for m in range(TAPS - 1):
                    ins = add(tp[m][:, :, :], raw[:, :, :, m:m + TK].rearrange("p h j t -> p (h j) t"),
                              bcast(taps[:, 2 * q:2 * q + 2, :, m].rearrange("p h j -> p (h j)"), 2, TK), ALU.mult)
                ins.then_inc(Z["tapm_ready"], 1)

            def silu(k, par, q):
                after(pool, "sg_ready", k * PAIRS + q + 1)
                add(QK[par][:, :, 2 * q:2 * q + 2, :].rearrange("p j h t -> p h j t"), yc[:, :, 0:2, :], sg[:, :, 0:2, :], ALU.mult)
                add(sv[:, :, :], yc[:, :, 2, :], sg[:, :, 2, :], ALU.mult).then_inc(Z["silu_ready"], 1)
                after(pool, "ia_ready", k * PAIRS + q + 1)
                after(pool, "scan_ready", k * PAIRS + q)
                add(d01[:, :, :, :], bcast(sa[q % 2][:, :, :], 1, 2), bcast(m01[:, :, :], 2, 2), ALU.mult).then_inc(Z["d_ready"], 1)

            def decayed(k, par, q):
                if q == 0:
                    after(pool, "bb_ready", k * 16 + 16)
                add(at_pair(DT[par], q), at_pair(bb, q), sa[q % 2][:, :, :], ALU.mult)
                after(pool, "silu_ready", k * PAIRS + q + 1)
                add(bv[:, :, :], at_pair(bb, q), sv[:, :, :], ALU.mult).then_inc(Z["bv_ready"], 1)
                after(pool, "ri_ready", k * PAIRS + q + 1)
                after(pool, "bv_ready", k * PAIRS + q + 1)
                add(at_pair(VT[par], q), bv[:, :, :], rr[:, :, :], ALU.mult).then_inc(Z["v_done"], 1)

            def key_products(k, par, v):
                after(pool, "silu_ready", k * PAIRS + PAIRS)
                after(pool, "spread_ready", k * NV + v)
                for t0, n, u0, m, off in RECTS:
                    k1 = QK[par][:, 1, :, v * SB + t0:v * SB + t0 + n]
                    k2 = QK[par][:, 1, :, v * SB + u0:v * SB + u0 + m]
                    ins = add(rect(kk, (t0, n, u0, m, off)), bcast(k1, 3, m), bcast(k2, 2, n), ALU.mult)
                ins.then_inc(Z["kk_ready"], 1)

            def couplings(k, par, v):
                after(pool, "kko_kept", k * NV + v + 1)
                after(pool, "v_done", k * PAIRS + PAIRS)
                for r in RECTS:
                    t0, n, u0, m, off = r
                    ins = add(rect(H[v % 2], r), rect(H[v % 2], r), bcast(DT[par][:, :, v * SB + u0:v * SB + u0 + m], 2, n), ALU.mult)
                ins.then_inc(Z["h_ready"], 1)

            def gated(k, c):
                after(pool, "ng_ready", k * NC + c + 1)
                add(at_chunk(O, c), sq[:, :, :], at_chunk(GT, c), ALU.mult).then_inc(Z["n_gated"], 1)

            def part(n, par, solve, finish, project, norm):
                for v in range(NV):
                    if norm and v == 5:
                        root(n + 2)
                    if project:
                        silu(n + 1, 1 - par, v)
                        if v < PAIRS - 1:
                            tap_products(n + 1, v + 1)
                        elif norm:
                            tap_products(n + 2, 0)
                    if finish and v == 3:
                        gated(n - 1, 0)
                    if solve and v < NV - 1:
                        couplings(n, par, v + 1)
                        if v < NV - 2:
                            key_products(n, par, v + 2)
                    if project:
                        if v == NV - 1:
                            key_products(n + 1, 1 - par, 0)
                        decayed(n + 1, 1 - par, v)
                        if v == NV - 1:
                            key_products(n + 1, 1 - par, 1)
                            couplings(n + 1, 1 - par, 0)
                    if finish:
                        k = n - 1
                        if v == 1:
                            after(pool, "ve_ready", k + 1)
                            add(var[:, :], var[:, :], C["nhalf"][:, 0:NC * 4], ALU.pow).then_inc(Z["rs_ready"], 1)
                        if v == 3:
                            gated(k, 1)

            root(0)
            tap_products(0, 0)
            all_parts(pool, part)

        @block.scalar
        def _(act):
            act.wait_ge(Z["loaded"], 16 * NLOAD)
            act.wait_ge(Z["set_up"], 1)
            f = nc.scalar.activation

            def hidden(k, par):
                after(act, "T_ready", k + 1)
                for j in range(KD):
                    ins = f(hT[par][:, j, :], psM[:, j * TK:(j + 1) * TK], ACT.Identity,
                            bias=C["mod_col"][:, 1, 0, j:j + 1], scale=C["mod_col"][:, 1, 1, j:j + 1])
                ins.then_inc(Z["hT_ready"], 1)

            def beta(k):
                after(act, "b_ready", k + 1)
                after(act, "b_stored", k * 16)
                f(bT[:, :], psM[0:NH, 0:TK], ACT.Sigmoid, bias=bbias[:, 0:1]).then_inc(Z["bs_ready"], 1)

            def pair_in(k, q):
                n = k * PAIRS + q
                after(act, "in_ready", n + 1)
                after(act, "tapm_ready", n)
                f(raw[:, :, :, 0:TAPS - 1], hist[:, 2 * q:2 * q + 2, :, :], ACT.Copy)
                f(raw[:, :, :, TAPS - 1:], psP[:, :, 0:3, :], ACT.Copy).then_inc(Z["raw_ready"], 1)
                after(act, "silu_ready", n)
                for h in range(2):
                    for j in range(3):
                        ins = f(yc[:, h, j, :], psP[:, h, j, :], ACT.Identity, bias=cbias[:, 2 * q + h, j:j + 1],
                                scale=taps[:, 2 * q + h, j, TAPS - 1:TAPS])
                ins.then_inc(Z["tap_ready"], 1)
                after(act, "raw_ready", n + 1)
                f(hist[:, 2 * q:2 * q + 2, :, :], psP[:, :, 0:3, TK - (TAPS - 1):], ACT.Copy)
                after(act, "v_done", n - 1)
                for h in range(2):
                    ins = f(sa[q % 2][:, h, :], psP[:, h, 3, :], ACT.Sigmoid, bias=abias[:, 2 * q + h:2 * q + h + 1])
                ins.then_inc(Z["a_ready"], 1)

            def pair_gate(k, q):
                after(act, "conv_done", k * PAIRS + q + 1)
                f(sg[:, :, :, :], yc[:, :, :, :], ACT.Sigmoid).then_inc(Z["sg_ready"], 1)

            def keep_spread(k, v):
                after(act, "spread_ready", k * NV + v + 1)
                after(act, "e_done", k * NV + v - 1)
                f(H[v % 2][:, :], psK[:, :, :].rearrange("p a b -> p (a b)")[:, 0:NPAIR], ACT.Copy).then_inc(Z["kko_kept"], 1)

            def keys(k, par, v):
                if v == 0:
                    after(act, "silu_ready", k * PAIRS + PAIRS)
                after(act, "gq_ready", k * NV + v - 1)
                f(ks[:, v % 2], at_sub(QK[par][:, 1], v), ACT.Copy).then_inc(Z["ks_ready"], 1)

            def sigmoids(n, g):
                after(act, "g_ready", n * 2 + g + 1)
                if g == 0:
                    after(act, "n_gated", n * NC)
                f(GT[:, 8 * g:8 * g + 8, :], psM[:, :].rearrange("p (h t) -> p h t", h=8), ACT.Sigmoid).then_inc(Z["gate_ready"], 1)

            def scaled(k, c):
                after(act, "n_ready", k * NC + c + 1)
                if c:
                    after(act, "n_gated", k * NC + c)
                f(sq[:, :, :], at_chunk(O, c), ACT.Identity, bias=ln[:, 1:2], scale=ln[:, 0:1]).then_inc(Z["ng_ready"], 1)

            def part(n, par, solve, finish, project, norm):
                k = n - 1
                for v in range(NV):
                    c, s = v // NSB, v % NSB
                    if finish and v == 3:
                        scaled(k, 0)
                    if project:
                        pair_gate(n + 1, v)
                    if solve and s == 0:
                        after(act, "ws_ready", n * NC + c)
                        f(EF[:, :, :], at_chunk(QK[par][:, 1], c), ACT.Copy).then_inc(Z["kc_ready"], 1)
                        after(act, "kt_ready", n * NC + c + 1)
                        f(ktok[:, :, :], psT[:, :, :], ACT.Copy).then_inc(Z["kt_kept"], 1)
                    if solve and v == 0:
                        after(act, "fT_ready", n + 1)
                        after(act, "f_stored", n * 16)
                        f(frow[:, :], psM[0:NC * NH, 0:P], ACT.Copy).then_inc(Z["frow_ready"], 1)
                    if project and v < PAIRS - 1:
                        pair_in(n + 1, v + 1)
                    elif norm and v == PAIRS - 1:
                        pair_in(n + 2, 0)
                    if finish and v == 1:
                        after(act, "c_ready", k * NC + v + 1)
                        if v:
                            after(act, "v_part", k + 1)
                        f(sq[:, :, :], mM, ACT.Square).then_inc(Z["csq_ready"], 1)
                        f(at_chunk(O, v), mM, ACT.Copy).then_inc(Z["c_kept"], 1)
                    if solve and v == 5:
                        sigmoids(n, 0)
                    if finish and v == 4:
                        after(act, "y_ready", k + 1)
                        f(yT[:, :, :].rearrange("p k t -> p (k t)"), psM[:, 0:KD * TK], ACT.Copy).then_inc(Z["yT_kept"], 1)
                    if solve and v < NV - 1:
                        keep_spread(n, v + 1)
                    if finish and v == 0:
                        after(act, "c_ready", k * NC + v + 1)
                        if v:
                            after(act, "v_part", k + 1)
                        f(sq[:, :, :], mM, ACT.Square).then_inc(Z["csq_ready"], 1)
                        f(at_chunk(O, v), mM, ACT.Copy).then_inc(Z["c_kept"], 1)
                    if solve and v < NV - 1:
                        keys(n, par, v + 1)
                    if solve and v == 5:
                        sigmoids(n, 1)
                    if solve and v == 6:
                        after(act, "y_ready", n)
                        after(act, "o_read", n * NC + 1)
                        f(at_chunk(O, 0), O_first[:, :, :], ACT.Copy).then_inc(Z["oc_kept"], 1)
                    if finish and v == 1:
                        after(act, "v_ready", k + 1)
                        f(var[:, :], psT[:, 3, 0:NC * 4], ACT.Identity, bias=eps[:, 0:1], scale=1.0 / P).then_inc(Z["ve_ready"], 1)
                    if norm and v == 6:
                        hidden(n + 2, par)
                    if norm and v == 7:
                        beta(n + 2)
                    if solve:
                        after(act, "wt_ready", n * NV + v + 1)
                        f(wt[:, :], psT[:, 0, :], ACT.Copy).then_inc(Z["wt_kept"], 1)
                        if s == NSB - 1:
                            after(act, "ws_ready", n * NC + c + 1)
                            f(ws[:, :, :], psT[:, :, :], ACT.Copy).then_inc(Z["ws_kept"], 1)
                    if finish and v == 3:
                        scaled(k, 1)
                    if project and v == NV - 1:
                        keep_spread(n + 1, 0)
                        keys(n + 1, 1 - par, 0)

            hidden(0, 0)
            beta(0)
            pair_in(0, 0)
            all_parts(act, part)

        @block.vector
        def _(dve):
            dve.wait_ge(Z["loaded"], 16 * NLOAD)
            nc.vector.memset(hist[:, :, :, :], 0.0)
            nc.vector.memset(eps[:, :], EPS)
            for b in range(2):
                nc.vector.memset(hT[b][:, KD, :], 0.0)
            nc.vector.memset(ones[:, :], 1.0)
            nc.vector.memset(St[:, :, :], 0.0).then_inc(Z["set_up"], 1)
            tt = nc.vector.tensor_tensor

            def statistics(k):
                ch = Chain(dve, Z["ln_step"], k * 2)
                after(dve, "x_ready", k * 16 + 16)
                ch.done_before(nc.vector.bn_stats(stats[:, :], x_t[:, :]), C["pad"])
                ch.done(nc.vector.bn_aggr(mv[:, :], stats[:, :]))
                nc.vector.tensor_scalar(mv[:, 1:2], mv[:, 1:2], EPS, None, ALU.add).then_inc(Z["mv_ready"], 1)

            def normed(k):
                after(dve, "rstd_ready", k + 1)
                after(dve, "T_ready", k)
                after(dve, "stored", (k - 2) * 16)
                nc.vector.tensor_scalar(xh[:, :], x_t[:, :], mv[:, 0:1], rstd[:, 0:1], ALU.subtract, ALU.mult).then_inc(Z["xh_ready"], 1)

            def beta(k):
                after(dve, "bs_ready", k + 1)
                after(dve, "v_done", k * PAIRS)
                nc.vector.tensor_scalar(bT[:, :], bT[:, :], SCALE * SCALE, None, ALU.mult).then_inc(Z["bT_ready"], 1)

            def convolve(k, q):
                n = k * PAIRS + q
                after(dve, "a_ready", n + 1)
                nc.vector.reciprocal(sa[q % 2][:, :, :], sa[q % 2][:, :, :]).then_inc(Z["ia_ready"], 1)
                after(dve, "tap_ready", n + 1)
                after(dve, "tapm_ready", n + 1)
                y = yc[:, :, :, :].rearrange("p h j t -> p (h j) t")
                for m in range(TAPS - 1):
                    ins = tt(y, y, tp[m][:, :, :], ALU.add)
                    if m < TAPS - 2:
                        ins.then_inc(Z["conv_step"], 1)
                        after(dve, "conv_step", n * (TAPS - 2) + m + 1)
                ins.then_inc(Z["conv_done"], 1)

            def decays(k, par, q):
                n = k * PAIRS + q
                after(dve, "d_ready", n + 1)
                after(dve, "v_done", n)
                nc.vector.tensor_tensor_scan(rr[:, :, :].rearrange("p h t -> p (h t)"), d01[:, 0, :, :].rearrange("p h t -> p (h t)"),
                                             d01[:, 1, :, :].rearrange("p h t -> p (h t)"), 0.0, ALU.mult, ALU.add).then_inc(Z["scan_ready"], 1)
                after(dve, "scan_ready", n + 1)
                nc.vector.reciprocal(at_pair(RI[par], q), rr[:, :, :]).then_inc(Z["ri_ready"], 1)

            def factors(k, par):
                after(dve, "ri_ready", k * PAIRS + PAIRS)
                after(dve, "fT_ready", k)
                nc.vector.tensor_scalar(F[:, :, :], RI[par][:, :, L - 1::L].rearrange("p h c -> p c h"), KAPPA, None,
                                        ALU.mult).then_inc(Z["f_ready"], 1)

            def normalise(k, c):
                after(dve, "r_ready", k * NC + c + 1)
                tt(at_chunk(O, c), at_chunk(O, c), mM, ALU.mult).then_inc(Z["n_ready"], 1)

            def outputs(n, par, c):
                after(dve, "o_sum", n * NC + c + 1)
                after(dve, *(("y_ready", n) if c else ("oc_kept", n)))
                nc.vector.scalar_tensor_tensor(out=at_chunk(O, c) if c else O_first[:, :, :], in0=psO, scalar=1.0 / SCALE,
                                               in1=at_chunk(RI[par], c), op0=ALU.mult, op1=ALU.mult).then_inc(Z["o_read"], 1)

            def part(n, par, solve, finish, project, norm):
                for v in range(NV):
                    c, s = v // NSB, v % NSB
                    Vn, G = n * NV + v, n * NC + c
                    if solve:
                        if s == 0:
                            after(dve, "sk_ready", G + 1)
                        else:
                            after(dve, "x_next", G * (NSB - 1) + s)
                        after(dve, "wt_ready", Vn)
                        if v == 0:
                            after(dve, "v_done", n * PAIRS + PAIRS)
                            after(dve, "f_ready", n + 1)
                        Ev = E[:, :, :]
                        ch = Chain(dve, Z["b_step"], Vn * CHAIN)
                        tt(tmp[:, :, :], at_sub(psX, s), at_sub(DT[par], v), ALU.mult).then_inc(Z["x_read"], 1)
                        after(dve, "x_read", Vn + 1)
                        here = ch.mark(tt(Ev, at_sub(VT[par], v), tmp[:, :, :], ALU.subtract))
                        if s < NSB - 1:
                            after(dve, "gk_ready", G * (NSB - 1) + s + 1)
                            tt(gk[:, :, 0:(NSB - 1 - s) * SB],
                               psG[:, 0:NH * (NSB - 1 - s) * SB].rearrange("p (h t) -> p h t", h=NH),
                               bcast(hmask[:, :], 2, (NSB - 1 - s) * SB), ALU.mult).then_inc(Z["gkm_ready"], 1)
                    if solve:
                        ch.wait(here)
                        after(dve, "h_ready", Vn + 1)
                        for k in range(SB - 1):
                            r = RECTS[k // 2]
                            h_k = rect(H[v % 2], r)[:, :, k - r[0], k + 1 - r[2]:]
                            m = SB - 1 - k
                            ch.done(tt(tmp[:, :, 0:m], bcast(Ev[:, :, k], 2, m), h_k, ALU.mult))
                            ins = tt(Ev[:, :, k + 1:], Ev[:, :, k + 1:], tmp[:, :, 0:m], ALU.subtract)
                            if k < SB - 2:
                                ch.done(ins)
                        ins.then_inc(Z["e_done"], 1)
                        assert ch.n == CHAIN, (ch.n, CHAIN)
                        after(dve, "e_done", Vn + 1)
                        if s == 0:
                            after(dve, "kt_ready", G + 1)
                        tt(EF[:, :, s * SB:(s + 1) * SB], Ev, bcast(F[:, c, :], 2, SB), ALU.mult).then_inc(Z["ef_ready"], 1)
                        w = (NSB - s) * SB
                        after(dve, "gq_ready", Vn + 1)
                        g3 = psG[:, 0:NH * w].rearrange("p (h t) -> p h t", h=NH)
                        ins = tt(gq[:, :, 0:SB], g3[:, :, 0:SB], cmask[:, :, :], ALU.mult)
                        if w > SB:
                            ins = tt(gq[:, :, SB:w], g3[:, :, SB:], bcast(hmask[:, :], 2, w - SB), ALU.mult)
                        ins.then_inc(Z["gqm_ready"], 1)
                    if finish and v == 3:
                        normalise(n - 1, 1)
                    if project:
                        decays(n + 1, 1 - par, v)
                        if v < PAIRS - 1:
                            convolve(n + 1, v + 1)
                    if norm and v == PAIRS - 1:
                        convolve(n + 2, 0)
                    if solve and s in (1, 2):
                        after(dve, "f_loaded", n * (NC * 32) + (2 * c + s) * 16)
                        half = St[:, (s - 1) * NH // 2:s * NH // 2, :]
                        tt(half, half, fb[:, :, :], ALU.mult).then_inc(Z["fs_ready"], 1)
                    if solve and s == NSB - 1:
                        outputs(n, par, c)
                        after(dve, "fs_ready", G * 2 + 2)
                        for r in range(4):
                            after(dve, "su_ready", G * 4 + r + 1)
                            ins = tt(St[:, r::4, :], (psS, psK)[r % 2][:, :, :], St[:, r::4, :], ALU.add)
                            ins.then_inc(Z["s_part" if r < 3 else "s_ready"], 1)
                    if finish and v == 2:
                        normalise(n - 1, 0)
                    if finish and v == 4:
                        after(dve, "yo_ready", n)
                        if solve and project:
                            after(dve, "T_ready", n + 2)
                        after(dve, "stored", (n - 1) * 16)
                        tt(o_t[:, :], psM[0:TK, 0:D], C["gate_row"][0:TK, 1, 0, :], ALU.mult).then_inc(Z["og_ready"], 1)
                        after(dve, "og_ready", n)
                        after(dve, "xr_ready", n * 16)
                        tt(o_t[:, :], o_t[:, :], xr[:, :], ALU.add).then_inc(Z["x_done"], 1)
                    if norm:
                        if v == 4:
                            statistics(n + 2)
                        if v == 5:
                            normed(n + 2)
                    if project and v == NV - 1:
                        factors(n + 1, 1 - par)
                        if norm:
                            beta(n + 2)

            statistics(0)
            normed(0)
            beta(0)
            convolve(0, 0)
            all_parts(dve, part)

        @block.tensor
        def _(pe):
            pe.wait_ge(Z["loaded"], 16 * NLOAD)
            pe.wait_ge(Z["set_up"], 1)
            mm = nc.tensor.matmul

            def hidden(k, par):
                after(pe, "xh_ready", k + 1)
                for j in range(KD):
                    ins = mm(psM[:, j * TK:(j + 1) * TK], xh[:, j * P:(j + 1) * P], C["ident"][0:TK, 0:TK], start=True, stop=True)
                ins.then_inc(Z["T_ready"], 1)

            def beta(k, par):
                after(pe, "hT_ready", k + 1)
                for j in range(KD):
                    ins = mm(psM[0:NH, 0:TK], w_b[:, j, :], hT[par][:, j, :], start=(j == 0), stop=(j == KD - 1))
                ins.then_inc(Z["b_ready"], 1)

            def pair_in(k, par, q):
                after(pe, "a_ready", k * PAIRS + q)
                after(pe, "hT_ready", k + 1)
                for h in range(2):
                    for c in range(4):
                        for j in range(KD):
                            at = (h * 4 + c) * TK
                            wide = 1 if (h, c) == (1, 3) else 2
                            ins = mm(psP[:, :, :, :].rearrange("p h c t -> p (h c t)")[:, at:at + wide * TK], w_in[:, j, 2 * q + h, c, :],
                                     hT[par][:, j:j + wide, :], start=(j == 0), stop=(j == KD - 1))
                ins.then_inc(Z["in_ready"], 1)

            def spread(k, v):
                after(pe, "kk_ready", k * NV + v + 1)
                after(pe, "kko_kept", k * NV + v)
                after(pe, "s_ready", k * NC + (v - 1) // NSB if v else k * NC)
                mm(psK[:, :, :].rearrange("p a b -> p (a b)")[:, 0:NPAIR], ones[:, :], kk[:, :], start=True,
                   stop=True).then_inc(Z["spread_ready"], 1)

            def centred(k, c):
                mm(mM, centre[:, :], at_chunk(O, c), start=True, stop=True).then_inc(Z["c_ready"], 1)

            def variance(k, c):
                after(pe, "csq_ready", k * NC + c + 1)
                sq2 = sq[:, :, :].rearrange("p h t -> p (h t)")
                for q in range(4):
                    ins = mm(psT[:, 3, 4 * c + q:4 * c + q + 1], sq2[:, q * P:(q + 1) * P], ones[:, 0:1], start=True, stop=True)
                ins.then_inc(Z["v_part" if c == 0 else "v_ready"], 1)

            def roots(k, c):
                after(pe, "rs_ready", k + 1)
                for q in range(4):
                    ins = nc.tensor.transpose(psM[:, q * P:(q + 1) * P], var[:, 4 * c + q:4 * c + q + 1].broadcast_to([P, P]), C["ident"][:, :])
                ins.then_inc(Z["r_ready"], 1)

            def keep_warm(count):
                for _ in range(count):
                    mm(psT[:, 1, :], ones[:, :], centre[:, :], start=True, stop=True)

            def own_outputs(s):
                for i in range(2):
                    half = slice(i * NH // 2, (i + 1) * NH // 2)
                    ins = mm(psO[:, half, s * SB:], wt[:, :], gq[:, half, 0:(NSB - s) * SB], start=False, stop=True,
                             skip_group_check=True)
                return ins

            def gates(n, par, g):
                for i in range(8):
                    h = 8 * g + i
                    for j in range(KD):
                        wide = 1 if i == 7 else 2
                        ins = mm(psM[:, i * TK:(i + wide) * TK], w_g[:, j, h * P:(h + 1) * P], hT[par][:, j:j + wide, :],
                                 start=(j == 0), stop=(j == KD - 1))
                ins.then_inc(Z["g_ready"], 1)

            def part(n, par, solve, finish, project, norm):
                k = n - 1
                for v in range(NV):
                    c, s = v // NSB, v % NSB
                    Vn, G = n * NV + v, n * NC + c
                    if project and s == 0:
                        pair_in(n + 1, 1 - par, v + 1)
                    if solve:
                        if s == 0:
                            if v == 0:
                                after(pe, "silu_ready", n * PAIRS + PAIRS)
                            after(pe, "s_ready", G)
                            after(pe, "o_read", G)
                            for h in range(NH):
                                ins = mm(psOX[:, h, :, :], St[:, h, :], QK[par][:, :, h, c * L:(c + 1) * L], start=(h % (NH // 2) == 0),
                                         stop=True, skip_group_check=True)
                            ins.then_inc(Z["sk_ready"], 1)
                            after(pe, "kc_ready", G + 1)
                            for q in range(4):
                                ins = nc.tensor.transpose(psT[:, q, :], EF[:, 4 * q:4 * q + 4, :], C["ident"][:, :])
                            ins.then_inc(Z["kt_ready"], 1)
                        after(pe, "ks_ready", Vn + 1)
                        after(pe, "gqm_ready", Vn)
                        kb = ks[:, v % 2].rearrange("p h t -> p (h t)")
                        if s < NSB - 1:
                            mm(psG[:, 0:NH * (NSB - 1 - s) * SB], kb, QK[par][:, 1, :, (v + 1) * SB:(c + 1) * L],
                               start=True, stop=True).then_inc(Z["gk_ready"], 1)
                    if finish and v == 4:
                        after(pe, "n_gated", n * NC)
                        for j in range(KD):
                            for h in range(NH):
                                wide = 2 if h < NH - 1 else 1
                                ins = mm(psM[:, j * TK:(j + wide) * TK], w_o[:, h, j * P:(j + 1) * P], O[:, h:h + wide, :], start=(h == 0), stop=(h == NH - 1))
                        ins.then_inc(Z["y_ready"], 1)
                    if project and s and v < PAIRS - 1:
                        pair_in(n + 1, 1 - par, v + 1)
                    elif norm and v == PAIRS - 1:
                        pair_in(n + 2, par, 0)
                    if solve:
                        if s < NSB - 1:
                            after(pe, "gkm_ready", G * (NSB - 1) + s + 1)
                        if s:
                            after(pe, "x_read", Vn + 1)
                            own_outputs(s - 1)
                        mm(psG[:, 0:NH * (NSB - s) * SB], kb, QK[par][:, 0, :, v * SB:(c + 1) * L], start=True,
                           stop=True).then_inc(Z["gq_ready"], 1)
                        if v == 0:
                            after(pe, "f_ready", n + 1)
                            if norm or n == NTK - 2:
                                after(pe, "bs_ready", n + 2)
                            nc.tensor.transpose(psM[0:NC * NH, 0:P], F[:, :, :], C["ident"][:, :]).then_inc(Z["fT_ready"], 1)
                    if finish and v == 1:
                        if solve:
                            after(pe, "wt_kept", Vn)
                        variance(k, 0)
                        after(pe, "c_kept", k * NC + 1)
                        after(pe, "o_read", n * NC)
                        centred(k, 1)
                    if solve and v == 5:
                        after(pe, "og_ready", n)
                        gates(n, par, 0)
                    if norm and v == 6:
                        after(pe, "gate_ready", n * 2 + 2)
                        hidden(n + 2, par)
                    if solve and v < NV - 1:
                        spread(n, v + 1)
                    if finish and v == 0:
                        after(pe, "oc_kept", n)
                        if solve:
                            after(pe, "frow_ready", n + 1)
                        centred(k, 0)
                    if finish and v == 4:
                        after(pe, "yT_kept", n)
                        for j in range(KD):
                            ins = mm(psM[0:TK, j * P:(j + 1) * P], yT[:, j, :], C["ident"][:, :], start=True, stop=True)
                        ins.then_inc(Z["yo_ready"], 1)
                    if finish and v == 2:
                        after(pe, "c_kept", n * NC)
                        roots(k, 0)
                    if finish and v == 3:
                        after(pe, "n_ready", k * NC + 1)
                        roots(k, 1)
                    if finish and v == 1:
                        variance(k, 1)
                        after(pe, "ve_ready", n)
                    if solve and v == 5:
                        after(pe, "gate_ready", n * 2 + 1)
                        gates(n, par, 1)
                    if norm and v == 7:
                        beta(n + 2, par)
                    if solve:
                        if s == 0:
                            after(pe, "kt_kept", G + 1)
                        keep_warm(WARM)
                        after(pe, "e_done", Vn + 1)
                        nc.tensor.transpose(psT[:, 0, :], E[:, :, :].rearrange("p h t -> p (h t)"), C["ident"][:, :]).then_inc(Z["wt_ready"], 1)
                        after(pe, "wt_kept", Vn + 1)
                        if s < NSB - 1:
                            for i in range(2):
                                half = slice(i * NH // 2, (i + 1) * NH // 2)
                                ins = mm(psX[:, half, (s + 1) * SB:], wt[:, :], gk[:, half, 0:(NSB - 1 - s) * SB], start=False,
                                         stop=True, skip_group_check=True)
                            ins.then_inc(Z["x_next"], 1)
                        else:
                            after(pe, "gqm_ready", Vn + 1)
                            own_outputs(s).then_inc(Z["o_sum"], 1)
                            after(pe, "ef_ready", Vn + 1)
                            for q in range(4):
                                ins = nc.tensor.transpose(psT[:, q, :], EF[:, 4 * q:4 * q + 4, :], C["ident"][:, :])
                            ins.then_inc(Z["ws_ready"], 1)
                            after(pe, "ws_kept", G + 1)
                            for r in range(4):
                                if r == 1 and v < NV - 1:
                                    after(pe, "kko_kept", Vn + 2)
                                if r >= 2:
                                    after(pe, "s_part", G * 3 + r - 1)
                                for q in range(4):
                                    ins = mm((psS, psK)[r % 2][:, q, :], ktok[32 * r:32 * r + 32, q, :],
                                             ws[32 * r:32 * r + 32, q, :], start=True, stop=True)
                                ins.then_inc(Z["su_ready"], 1)
                    if project and v == NV - 1:
                        spread(n + 1, 0)

            hidden(0, 0)
            beta(0, 0)
            pair_in(0, 0, 0)
            all_parts(pe, part)


def ttt_layer(nc, I, C, x_in, x_out):
    with ExitStack() as ctx:
        B = Alloc(nc, ctx, "ttt")
        S = {"XKT": B.sb("XKT", [P, KD, T]), "XQT": B.sb("XQT", [P, KD, T]),
             "cA": B.sb("cA", [P, NMB, 32]), "lA": B.sb("lA", [P, NMB, HR]),
             "GA": B.sb("GA", [P, NMB, 32]), "Wt": B.sb("Wt", [P, NT, KD + 1, 32]),
             "tok": B.sb("tok", [P, MB]),
             "g_dram": nc.dram_tensor("g_tok", [T, D], F32, kind="Internal").ap(),
             "c_tok": nc.dram_tensor("c_tok", [T, D + TH], F32, kind="Internal").ap()}
        ttt_project_phase(nc, I, C, S)
        ttt_scan_phase(nc, I, C, S)
        ttt_output_phase(nc, I, C, S, x_in, x_out)


def moe1_layer(nc, I, C, x_in, x_out):
    with ExitStack() as ctx:
        B = Alloc(nc, ctx, "moe1")
        S = {"hT": B.sb("hT", [P, KD, T]), "dwT": nc.dram_tensor("dwT", [E1S, T], F32, kind="Internal").ap()}
        moe1_route_phase(nc, I, C, S, x_in)
        moe1_expert_phase(nc, I, C, S, x_in, x_out)


def build(nc, I, out):
    with ExitStack() as ctx:
        A = Alloc(nc, ctx, "g")
        C = {"ident": A.sb("ident", [P, P]), "nhalf": A.sb("nhalf", [P, TH]), "pad": A.sb("pad", [P, 2]),
             "mod_col": A.sb("mod_col", [P, 2, 4, KD]), "gate_row": A.sb("gate_row", [P, 2, 2, D])}
        X = [nc.dram_tensor(f"x_stage{n}", [T, D], F32, kind="Internal").ap() for n in range(3)]
        setup_phase(nc, I, C)
        ttt_layer(nc, I, C, I["x"], X[0])
        moe1_layer(nc, I, C, X[0], X[1])
        kda_phase(nc, I, C, {"f_rows": nc.dram_tensor("f_rows", [NC * NH, P], F32, kind="Internal").ap(),
                              "b_rows": nc.dram_tensor("b_rows", [NH, TK], F32, kind="Internal").ap()}, X[1], X[2])
        moe2_phase(nc, I, C, X[2], out)


def layout(i):
    f = {k: np.asarray(v) for k, v in i.items()}
    o = {"x": f["L0_attn_hidden_states"].reshape(T, D), "c_ident": np.eye(P, dtype=np.float32)}
    for l in range(2):
        o[f"wmod{l}"] = f[f"L{l}_wmod"]
        o[f"c{l}"] = f[f"L{l}_c"].reshape(KD, P).T
    o["qwT"], o["kwT"], o["vwT"] = (f[f"L0_attn_{n}_w"].T for n in "qkv")
    o["lrwT"] = f["L0_attn_ttt_lr_weight"].reshape(TH, D).T
    o["lrb"] = f["L0_attn_ttt_lr_bias"].reshape(1, TH)
    o["ttt_w"] = f["L0_attn_ttt_norm_weight"].reshape(1, D)
    o["ttt_b"] = f["L0_attn_ttt_norm_bias"].reshape(1, D)
    row = np.arange(P)
    w1 = f["L0_attn_W1"].reshape(KD, HR, HR, HD, HD)
    bd = np.zeros((HR, HR, HD, KD, HR, HD), np.float32)
    for r in range(HR):
        bd[:, r, :, :, r, :] = w1[:, :, r].transpose(1, 2, 0, 3)
    o["W1bd"] = bd.reshape(P, KD, 32)
    o["b1A"] = np.repeat(f["L0_attn_b1"].reshape(HG, 1, 32), MB, 1).reshape(P, 32)
    o["ttt_wA"] = np.repeat(f["L0_attn_ttt_norm_weight"].reshape(HG, 1, 32), MB, 1).reshape(P, 32)
    o["tokidx"] = f["L0_attn_learnable_token_idx"].reshape(1, MB)
    o["c_recip"] = (1.0 / np.arange(1, MB + 1, dtype=np.float32)).reshape(1, MB)
    o["c_gmask"] = (row[:, None] // 32 == np.arange(HR)).astype(np.float32)
    rmask = np.ones((P, KD + 1, HR), np.float32)
    rmask[:, :KD] = (row[:, None] // HD % HR == np.arange(HR))[:, None]
    o["c_rmask"] = rmask
    o["c_first"] = ((row[:, None] // MB == row // MB) & (row[:, None] % MB == 0)).astype(np.float32)
    o["c_same"] = (row[:, None] // MB == row // MB).astype(np.float32)
    o["owT"] = f["L0_attn_o_w"].T
    o["post"] = np.stack([f[f"L0_attn_post_norm_{n}"].reshape(KD, P).T for n in ("weight", "bias")], 1)
    o["c_brow"] = (row[:, None] // MB == np.arange(HG)).astype(np.float32)
    o["c_pick"] = np.repeat((row[:, None] % MB == 0).astype(np.float32), P, 1)
    o["c_causal"] = ((row[:, None] // MB == row // MB) & (row[:, None] <= row)).astype(np.float32)
    o["c_prev"] = (row[:, None] // MB < row // MB).astype(np.float32)
    wide = lambda a: a.reshape(D, 2, I1).transpose(1, 0, 2)
    gate = np.concatenate([f["L0_ffn_w_gate"], wide(f["L0_ffn_ws_gate"])])
    up = np.concatenate([f["L0_ffn_w_up"], wide(f["L0_ffn_ws_up"])])
    down = np.concatenate([f["L0_ffn_w_down"], f["L0_ffn_ws_down"].reshape(2, I1, D)])
    gu = np.concatenate([gate, up], 2).reshape(E1S, KD, P, D).transpose(0, 2, 1, 3).reshape(E1S, P, KD * D)
    o["w1"] = np.concatenate([gu, down], 2)
    o["gate1T"] = f["L0_ffn_gate_weight"].T
    o["gate2T"], o["wdT"] = f["L1_ffn_gate_w"].T, f["L1_ffn_wd"].reshape(E2 * BOT, D).T
    o["wsdT"], o["wsuT"] = f["L1_ffn_ws_d"].T, f["L1_ffn_ws_u"].T
    o["wuT"] = f["L1_ffn_wu"].transpose(0, 2, 1).reshape(E2 * BOT, D)
    o["bd"] = f["L1_ffn_bd"].reshape(M2, P).T
    o["bsd"] = f["L1_ffn_bs_d"].reshape(BOT, 1)
    o["bu"] = np.concatenate([f["L1_ffn_bu"], f["L1_ffn_bs_u"].reshape(1, D)])
    o["c_sel"] = (np.arange(E2 + 1)[:, None] == np.arange(E2 * BOT) // BOT).astype(np.float32).reshape(E2 + 1, M2, P)
    e = np.arange(E2)
    o["c_tri"] = (e[:, None] > e).astype(np.float32).reshape(1, E2 * E2)
    win = np.stack([f[f"L1_attn_W{n}"].reshape(NH, P, D) for n in "qkva"], 1)
    o["win"] = win.transpose(3, 0, 1, 2).reshape(D, NH * 4 * P)
    o["wgT"], o["wbT"], o["woT"] = f["L1_attn_Wg"].T, f["L1_attn_Wb"].T, f["L1_attn_Wo"].T
    o["taps"] = np.stack([f[f"L1_attn_{n}c_w"].reshape(NH, P, TAPS) for n in "qkv"], 2).transpose(1, 0, 2, 3)
    o["cbias"] = np.stack([f[f"L1_attn_{n}c_b"].reshape(NH, P) for n in "qkv"], 2).transpose(1, 0, 2)
    o["abias"], o["bbias"] = f["L1_attn_ba"].reshape(NH, P).T, f["L1_attn_bb"].reshape(NH, 1)
    o["kln"] = np.stack([f["L1_attn_ln_g"], f["L1_attn_ln_b"]], 1)
    begin = np.arange(TK) % L == 0
    o["c_m01"] = np.repeat(np.stack([~begin, begin * KAPPA]).astype(np.float32)[None], P, 0)
    o["c_hmask"] = (row[:, None] // SB == np.arange(NH)).astype(np.float32)
    o["c_cmask"] = (o["c_hmask"][:, :, None] * (row[:, None, None] % SB <= np.arange(SB))).astype(np.float32)
    o["c_centre"] = (np.eye(P) - 1.0 / P).astype(np.float32)
    return {k: np.ascontiguousarray(v) for k, v in o.items()}


def kernel(**inputs):
    import concourse.bacc as _bacc
    from concourse.bass_utils import run_bass_kernel_spmd as _run

    nc = _bacc.Bacc("TRN2", target_bir_lowering=False, num_devices=1)
    arrays, aps = {}, {}
    for name, a in layout(inputs).items():
        arrays[f"in_{name}"] = a
        aps[name] = nc.dram_tensor(f"in_{name}", a.shape, mybir.dt.from_np(a.dtype), kind="ExternalInput").ap()
    out = nc.dram_tensor("out", [T, D], F32, kind="ExternalOutput").ap()
    build(nc, aps, out)
    r = _run(nc, [arrays], core_ids=[0])
    return r.results[0]["out"].reshape(1, T, D)
```
